# Optimizing a Trainium2 kernel written in Bass

```python
import numpy as np
import jax
import jax.numpy as jnp

def _softmax(x, axis=-1):
    return jax.nn.softmax(x, axis=axis)

def _gelu(x):
    return jax.nn.gelu(x, approximate=True)

def _silu(x):
    return jax.nn.silu(x)

def _sigmoid(x):
    return jax.nn.sigmoid(x)

def _layernorm(x, axis=-1, eps=1e-05):
    m = jnp.mean(x, axis=axis, keepdims=True)
    v = jnp.var(x, axis=axis, keepdims=True)
    return (x - m) / jnp.sqrt(v + eps)

def _scatter_add(tgt, idx, src, axis=0):
    return tgt.at[idx].add(src)

def _segment_sum(src, seg, n):
    return jax.ops.segment_sum(src, seg, n)
kernel_name = 'mk_decoder_postln_d4_seqx_r8_0d83ea'

def setup_inputs(seed: int=0):
    np.random.seed(seed)
    _w = jnp.asarray

    def _rec_inputs():
        import jax
        import jax.numpy as jnp
        _rk = jax.random.key(seed)
        x = 7.22e-05 + 1 * jax.random.normal(jax.random.fold_in(_rk, 1), (32, 64, 256), jnp.float32)
        _lenS = 64 - jax.random.randint(jax.random.fold_in(_rk, 7), (32,), 0, max(1, 64 // 4) + 1, jnp.int32)
        _lenS2 = 64 - jax.random.randint(jax.random.fold_in(_rk, 8), (32,), 0, max(1, 64 // 4) + 1, jnp.int32)
        _ctx_512P = jax.random.normal(jax.random.fold_in(_rk, 11), (32, 16, 64), jnp.float32)
        _ctx_512c = jax.random.dirichlet(jax.random.fold_in(_rk, 511), 0.3 * jnp.ones((16,), jnp.float32), (32, 64))
        _ctx_512t = jnp.einsum('bsk,bkd->bsd', _ctx_512c, _ctx_512P)
        _ctx_512t = _ctx_512t * jax.lax.rsqrt(jnp.mean(jnp.square(_ctx_512t)) + 1e-12) * 0.953939
        ctx_512 = -0.000514642 + 1.00011 * (_ctx_512t + 0.3 * jax.random.normal(jax.random.fold_in(_rk, 611), (32, 64, 64), jnp.float32))
        return (x, ctx_512)
    x, ctx_512 = _rec_inputs()

    def _L0_attn_setup():
        import jax, jax.numpy as jnp
        import numpy as np
        B, S, HID, QK, H = (2, 256, 256, 256, 16)
        DK, DV = (QK // H, HID // H)
        EPS = 1e-05
        key = jax.random.key(seed)
        ks = jax.random.split(key, 8)
        sd = 1.0 / np.sqrt(HID)
        inp = {'x': jax.random.normal(ks[0], (B, S, HID), jnp.float32), 'wq': jax.random.normal(ks[1], (HID, QK), jnp.float32) * sd, 'bq': jnp.zeros((QK,), jnp.float32), 'wk': jax.random.normal(ks[2], (HID, QK), jnp.float32) * sd, 'bk': jnp.zeros((QK,), jnp.float32), 'wv': jax.random.normal(ks[3], (HID, HID), jnp.float32) * sd, 'bv': jnp.zeros((HID,), jnp.float32), 'wg': jax.random.normal(ks[4], (HID, HID), jnp.float32) * sd, 'bg': jnp.zeros((HID,), jnp.float32), 'wo': jax.random.normal(ks[5], (HID, HID), jnp.float32) * sd, 'bo': jnp.zeros((HID,), jnp.float32), 'gn_w': jnp.ones((HID,), jnp.float32), 'gn_b': jnp.zeros((HID,), jnp.float32), 'gamma': 1.0 - jnp.exp(jnp.linspace(-np.log(32.0), -np.log(512.0), H)).astype(jnp.float32)}
        return inp
    _L0_attn_all = _L0_attn_setup()
    _L0_attn_in = {k: v for k, v in _L0_attn_all.items() if k in ('wq', 'bq', 'wk', 'bk', 'wv', 'bv', 'wg', 'bg', 'wo', 'bo', 'gn_w', 'gn_b', 'gamma')}
    del _L0_attn_all

    def _L0_xattn_setup():
        import jax, jax.numpy as jnp
        import numpy as np
        N_HEADS = 16
        N_KV_HEADS = 4
        ROPE_THETA = 10000.0
        EPS = 1e-05

        def _rms_norm(x, w):
            var = jnp.mean(x * x, axis=-1, keepdims=True)
            return x * jax.lax.rsqrt(var + EPS) * w

        def _rope_sin_cos(T, head_dim, dtype):
            inv_freq = 1.0 / ROPE_THETA ** (jnp.arange(0, head_dim, 2, dtype=jnp.float32) / head_dim)
            t = jnp.arange(T, dtype=jnp.float32)
            freqs = jnp.outer(t, inv_freq)
            emb = jnp.concatenate([freqs, freqs], -1)
            return (jnp.sin(emb).astype(dtype)[None, None], jnp.cos(emb).astype(dtype)[None, None])

        def _rotate_half(x):
            h = x.shape[-1] // 2
            x1, x2 = (x[..., :h], x[..., h:])
            return jnp.concatenate([-x2, x1], axis=-1)
        key = jax.random.key(seed)
        ks = jax.random.split(key, 6)
        B, T, C = (2, 256, 256)
        Ckv = C // N_HEADS * N_KV_HEADS
        return {'q': jax.random.normal(ks[0], (B, T, C), jnp.float32), 'k': jax.random.normal(ks[1], (B, T, Ckv), jnp.float32), 'v': jax.random.normal(ks[2], (B, T, Ckv), jnp.float32), 'q_norm_w': jnp.ones((C,), jnp.float32), 'k_norm_w': jnp.ones((Ckv,), jnp.float32), 'w_out': jax.random.normal(ks[3], (C, C), jnp.float32) * C ** (-0.5)}
    _L0_xattn_all = _L0_xattn_setup()
    _L0_xattn_in = {k: v for k, v in _L0_xattn_all.items() if k in ('q_norm_w', 'k_norm_w', 'w_out')}
    del _L0_xattn_all

    def _L0_ffn_setup():
        import jax, jax.numpy as jnp
        import numpy as np
        B, S, D = (1, 128, 256)
        E, K, F = (64, 8, 96)
        C = 32

        def _moe(x, router_w, w1, v1, w2):
            T = x.shape[0]
            logits = x @ router_w.T
            probs = jax.nn.softmax(logits, axis=-1)
            wts, idx = jax.lax.top_k(probs, K)
            wts = wts / jnp.sum(wts, axis=-1, keepdims=True)
            R = T * K
            e_flat = idx.reshape(-1)
            tok = jnp.arange(R) // K
            order = jnp.argsort(e_flat)
            e_s, tok_s = (e_flat[order], tok[order])
            w_s = wts.reshape(-1)[order]
            counts = jnp.bincount(e_flat, length=E)
            starts = jnp.cumsum(counts) - counts
            pos = jnp.arange(R) - starts[e_s]
            valid = pos < C
            pos_c = jnp.minimum(pos, C - 1)
            xg = jnp.zeros((E, C, D), x.dtype).at[e_s, pos_c].add(jnp.where(valid[:, None], x[tok_s], 0.0))
            h = jax.nn.silu(jnp.einsum('ecd,efd->ecf', xg, w1)) * jnp.einsum('ecd,efd->ecf', xg, v1)
            y = jnp.einsum('ecf,efd->ecd', h, w2)
            yr = y[e_s, pos_c] * jnp.where(valid, w_s, 0.0)[:, None]
            return jnp.zeros((T, D), x.dtype).at[tok_s].add(yr)
        key = jax.random.key(seed)
        k0, k1, k2, k3, k4 = jax.random.split(key, 5)
        return {'hidden_states': jax.random.normal(k0, (B, S, D), jnp.float32), 'router_w': jax.random.normal(k1, (E, D), jnp.float32) * 0.02, 'w1': jax.random.normal(k2, (E, F, D), jnp.float32) * 0.02, 'v1': jax.random.normal(k3, (E, F, D), jnp.float32) * 0.02, 'w2': jax.random.normal(k4, (E, F, D), jnp.float32) * 0.02}
    _L0_ffn_all = _L0_ffn_setup()
    _L0_ffn_in = {k: v for k, v in _L0_ffn_all.items() if k in ('router_w', 'w1', 'v1', 'w2')}
    del _L0_ffn_all

    def _L1_attn_setup():
        import jax, jax.numpy as jnp
        import numpy as np
        HIDDEN = 256
        N_HEADS = 16
        HEAD_DIM = HIDDEN // N_HEADS

        def rotate_half(x):
            x1, x2 = jnp.split(x, 2, axis=-1)
            return jnp.concatenate([-x2, x1], axis=-1)
        key = jax.random.key(seed)
        k0, k1, k2, k3, k4 = jax.random.split(key, 5)
        B, S = (1, 256)
        scale = 1.0 / np.sqrt(HIDDEN)
        return {'hidden_states': jax.random.normal(k0, (B, S, HIDDEN), dtype=jnp.float32), 'Wq': jax.random.normal(k1, (HIDDEN, HIDDEN), dtype=jnp.float32) * scale, 'Wk': jax.random.normal(k2, (HIDDEN, HIDDEN), dtype=jnp.float32) * scale, 'Wv': jax.random.normal(k3, (HIDDEN, HIDDEN), dtype=jnp.float32) * scale, 'Wo': jax.random.normal(k4, (HIDDEN, HIDDEN), dtype=jnp.float32) * scale, 'gate': jnp.zeros((1, N_HEADS, 1, 1), dtype=jnp.float32)}
    _L1_attn_all = _L1_attn_setup()
    _L1_attn_in = {k: v for k, v in _L1_attn_all.items() if k in ('Wq', 'Wk', 'Wv', 'Wo', 'gate')}
    del _L1_attn_all

    def _L1_xattn_setup():
        import jax, jax.numpy as jnp
        import numpy as np
        B, S, H, NH, L = (2, 256, 256, 16, 64)
        HD = H // NH
        key = jax.random.key(seed)
        k1, k2, k3, k4, k5 = jax.random.split(key, 5)
        scale = 0.02
        return {'q': jax.random.normal(k1, (B, S, H), dtype=jnp.float32), 'latent_kv': jax.random.normal(k2, (B, S, L), dtype=jnp.float32), 'Wq': jax.random.normal(k3, (H, H), dtype=jnp.float32) * scale, 'Wkv_expand': jax.random.normal(k4, (2 * H, L), dtype=jnp.float32) * scale, 'Wout': jax.random.normal(k5, (H, H), dtype=jnp.float32) * scale}
    _L1_xattn_all = _L1_xattn_setup()
    _L1_xattn_in = {k: v for k, v in _L1_xattn_all.items() if k in ('Wq', 'Wkv_expand', 'Wout')}
    del _L1_xattn_all

    def _L1_ffn_setup():
        import jax, jax.numpy as jnp
        import numpy as np
        EPS = 1e-08

        def ternary_quantize(w):
            threshold = 0.7 * jnp.mean(jnp.abs(w), axis=-1, keepdims=True)
            q = jnp.where(w > threshold, 1.0, jnp.where(w < -threshold, -1.0, 0.0)).astype(w.dtype)
            return w + jax.lax.stop_gradient(q - w)
        key = jax.random.key(seed)
        k1, k2, k3 = jax.random.split(key, 3)
        B, S, D_in, D_out = (4, 256, 256, 256)
        x = jax.random.normal(k1, (B, S, D_in), dtype=jnp.float32)
        bound = np.sqrt(6.0 / D_in)
        weight = jax.random.uniform(k2, (D_out, D_in), dtype=jnp.float32, minval=-bound, maxval=bound)
        bias = jax.random.normal(k3, (D_out,), dtype=jnp.float32) * 0.01
        return {'x': x, 'weight': weight, 'bias': bias}
    _L1_ffn_all = _L1_ffn_setup()
    _L1_ffn_in = {k: v for k, v in _L1_ffn_all.items() if k in ('weight', 'bias')}
    del _L1_ffn_all

    def _L2_attn_setup():
        import jax, jax.numpy as jnp
        import numpy as np
        from jax import lax
        H, P, N, G, K, CHUNK = (64, 64, 128, 1, 4, 32)
        D_MODEL = 256
        D_INNER = H * P
        CONV_DIM = D_INNER + 2 * G * N
        EPS = 1e-05

        def _mamba2_forward(hidden_states, in_proj_w, conv_w, conv_b, dt_bias, A_log, D_param, norm_w, out_proj_w):
            b, l, _ = hidden_states.shape
            c = l // CHUNK
            proj = hidden_states @ in_proj_w
            gate = proj[..., :D_INNER]
            hbc = proj[..., D_INNER:D_INNER + CONV_DIM]
            dt = proj[..., D_INNER + CONV_DIM:]
            xt = hbc.transpose(0, 2, 1)
            y = lax.conv_general_dilated(xt, conv_w[:, None, :], window_strides=(1,), padding=[(K - 1, 0)], feature_group_count=CONV_DIM, dimension_numbers=('NCH', 'OIH', 'NCH'))
            hbc = jax.nn.silu(y + conv_b[None, :, None]).transpose(0, 2, 1)
            per_g = D_INNER // G
            hg = hbc.reshape(b, l, G, per_g + 2 * N)
            x = hg[..., :per_g].reshape(b, l, H, P)
            Bm = hg[..., per_g:per_g + N]
            Cm = hg[..., per_g + N:]
            hpg = H // G
            Bh = jnp.repeat(Bm, hpg, axis=2)
            Ch = jnp.repeat(Cm, hpg, axis=2)
            dt = jax.nn.softplus(dt + dt_bias)
            A = -jnp.exp(A_log)
            x_c = x.reshape(b, c, CHUNK, H, P)
            B_c = Bh.reshape(b, c, CHUNK, H, N)
            C_c = Ch.reshape(b, c, CHUNK, H, N)
            dt_c = dt.reshape(b, c, CHUNK, H)
            dA = dt_c * A[None, None, None, :]
            cum = jnp.cumsum(dA, axis=2)
            diff = cum[:, :, :, None, :] - cum[:, :, None, :, :]
            i = jnp.arange(CHUNK)
            mask = i[:, None] >= i[None, :]
            decay = jnp.exp(jnp.where(mask[None, None, :, :, None], diff, -jnp.inf))
            scores = jnp.einsum('bcihn,bcjhn->bcijh', C_c, B_c) * decay * dt_c[:, :, None, :, :]
            Y_diag = jnp.einsum('bcijh,bcjhp->bcihp', scores, x_c)
            decay_states = jnp.exp(cum[:, :, -1:, :] - cum)
            states = jnp.einsum('bclh,bclhn,bclhp->bchpn', decay_states * dt_c, B_c, x_c)
            chunk_decay = jnp.exp(cum[:, :, -1, :])

            def step(prev, inp):
                st, cd = inp
                new = cd[:, :, None, None] * prev + st
                return (new, prev)
            init = jnp.zeros((b, H, P, N), hidden_states.dtype)
            _, prev_states = lax.scan(step, init, (jnp.moveaxis(states, 1, 0), jnp.moveaxis(chunk_decay, 1, 0)))
            prev_states = jnp.moveaxis(prev_states, 0, 1)
            state_decay_out = jnp.exp(cum)
            Y_off = jnp.einsum('bclhn,bchpn,bclh->bclhp', C_c, prev_states, state_decay_out)
            yh = (Y_diag + Y_off).reshape(b, l, H, P) + D_param[None, None, :, None] * x
            yr = yh.reshape(b, l, D_INNER)
            hidden = yr * jax.nn.silu(gate)
            var = jnp.mean(hidden * hidden, axis=-1, keepdims=True)
            hidden = hidden * lax.rsqrt(var + EPS) * norm_w
            return hidden @ out_proj_w
        key = jax.random.key(seed)
        ks = jax.random.split(key, 6)
        s = lambda k, shape, scale: jax.random.normal(k, shape, jnp.float32) * scale
        return {'hidden_states': s(ks[0], (2, 256, D_MODEL), 1.0), 'in_proj_w': s(ks[1], (D_MODEL, D_INNER + CONV_DIM + H), D_MODEL ** (-0.5)), 'conv_w': s(ks[2], (CONV_DIM, K), K ** (-0.5)), 'conv_b': jnp.zeros((CONV_DIM,), jnp.float32), 'dt_bias': jnp.ones((H,), jnp.float32), 'A_log': jnp.log(jnp.arange(1, H + 1, dtype=jnp.float32)), 'D_param': jnp.ones((H,), jnp.float32), 'norm_w': jnp.ones((D_INNER,), jnp.float32), 'out_proj_w': s(ks[3], (D_INNER, D_MODEL), D_INNER ** (-0.5))}
    _L2_attn_all = _L2_attn_setup()
    _L2_attn_in = {k: v for k, v in _L2_attn_all.items() if k in ('in_proj_w', 'conv_w', 'conv_b', 'dt_bias', 'A_log', 'D_param', 'norm_w', 'out_proj_w')}
    del _L2_attn_all

    def _L2_xattn_setup():
        import jax, jax.numpy as jnp
        import numpy as np
        B, S, L = (2, 128, 128)
        DIM_Q, H, K, D_C, D_CQ, R = (256, 16, 128, 64, 192, 64)

        def _rope_tables(length, dim):
            inv = 1.0 / 10000.0 ** (jnp.arange(0, dim, 2, dtype=jnp.float32) / dim)
            f = jnp.arange(length, dtype=jnp.float32)[:, None] * inv[None, :]
            sin = jnp.repeat(jnp.sin(f), 2, axis=-1)
            cos = jnp.repeat(jnp.cos(f), 2, axis=-1)
            return (sin, cos)

        def _rotate_half(x):
            half = x.shape[-1] // 2
            return jnp.concatenate([-x[..., half:], x[..., :half]], axis=-1)

        def _apply_rope(x, sin, cos):
            return x * cos + _rotate_half(x) * sin
        key = jax.random.key(seed)
        ks = jax.random.split(key, 8)
        return {'hidden_q': jax.random.normal(ks[0], (B, S, DIM_Q), jnp.float32), 'kv_c': jax.random.normal(ks[1], (B, L, D_C), jnp.float32), 'Wq': jax.random.normal(ks[2], (H * K, DIM_Q), jnp.float32) / np.sqrt(DIM_Q).astype(np.float32), 'w_kc_q': jax.random.normal(ks[3], (H, K, D_CQ), jnp.float32) / np.sqrt(K).astype(np.float32), 'w_kc_kv': jax.random.normal(ks[4], (H, K, D_C), jnp.float32) / np.sqrt(K).astype(np.float32), 'W_qr': jax.random.normal(ks[5], (H, D_CQ, R), jnp.float32) / np.float32(np.sqrt(D_CQ) * np.sqrt(R)), 'W_kr': jax.random.normal(ks[6], (H, D_C, R), jnp.float32) / np.sqrt(D_C).astype(np.float32), 'Wo': jax.random.normal(ks[7], (DIM_Q, H * K), jnp.float32) / np.sqrt(H * K).astype(np.float32)}
    _L2_xattn_all = _L2_xattn_setup()
    _L2_xattn_in = {k: v for k, v in _L2_xattn_all.items() if k in ('Wq', 'w_kc_q', 'w_kc_kv', 'W_qr', 'W_kr', 'Wo')}
    del _L2_xattn_all

    def _L2_ffn_setup():
        import jax, jax.numpy as jnp
        import numpy as np
        HIDDEN = 256
        INTER = 1024
        BATCH, LOCAL_SEQ = (2, 512)
        key = jax.random.key(seed)
        k1, k2, k3 = jax.random.split(key, 3)
        h_shard = jax.random.normal(k1, (BATCH, LOCAL_SEQ, HIDDEN), dtype=jnp.float32)
        w_gate_up = jax.random.normal(k2, (2 * INTER, HIDDEN), dtype=jnp.float32) * 0.02
        w_down = jax.random.normal(k3, (HIDDEN, INTER), dtype=jnp.float32) * 0.02
        return {'h_shard': h_shard, 'w_gate_up': w_gate_up, 'w_down': w_down}
    _L2_ffn_all = _L2_ffn_setup()
    _L2_ffn_in = {k: v for k, v in _L2_ffn_all.items() if k in ('w_gate_up', 'w_down')}
    del _L2_ffn_all

    def _L3_attn_setup():
        import jax, jax.numpy as jnp
        import numpy as np
        EMBED_DIM = 256
        NUM_HEADS = 16
        HEAD_DIM = EMBED_DIM // NUM_HEADS

        def _apply_rope(q, k, seq_len):
            hd = q.shape[-1]
            theta = 10000.0 ** (-jnp.arange(0, hd, 2, dtype=jnp.float32) / hd)
            pos = jnp.arange(seq_len, dtype=jnp.float32)
            freqs = pos[:, None] * theta[None, :]
            sin = jnp.sin(freqs)[None, None]
            cos = jnp.cos(freqs)[None, None]
            q_rot = q[..., ::2] * cos - q[..., 1::2] * sin
            k_rot = k[..., ::2] * cos - k[..., 1::2] * sin
            q = jnp.concatenate([q_rot, q[..., 1::2]], axis=-1)
            k = jnp.concatenate([k_rot, k[..., 1::2]], axis=-1)
            return (q, k)
        key = jax.random.key(seed)
        ks = jax.random.split(key, 9)
        D = EMBED_DIM
        s = 1.0 / np.sqrt(D)
        inp = {'x': jax.random.normal(ks[0], (2, 256, D), dtype=jnp.float32), 'wq': jax.random.uniform(ks[1], (D, D), jnp.float32, -s, s), 'bq': jax.random.uniform(ks[2], (D,), jnp.float32, -s, s), 'wk': jax.random.uniform(ks[3], (D, D), jnp.float32, -s, s), 'bk': jax.random.uniform(ks[4], (D,), jnp.float32, -s, s), 'wv': jax.random.uniform(ks[5], (D, D), jnp.float32, -s, s), 'bv': jax.random.uniform(ks[6], (D,), jnp.float32, -s, s), 'wo': jax.random.uniform(ks[7], (D, D), jnp.float32, -s, s), 'bo': jax.random.uniform(ks[8], (D,), jnp.float32, -s, s)}
        return inp
    _L3_attn_all = _L3_attn_setup()
    _L3_attn_in = {k: v for k, v in _L3_attn_all.items() if k in ('wq', 'bq', 'wk', 'bk', 'wv', 'bv', 'wo', 'bo')}
    del _L3_attn_all

    def _L3_xattn_setup():
        import jax, jax.numpy as jnp
        import numpy as np
        import math
        NUM_Q_HEADS = 32
        NUM_KV_HEADS = 8
        key = jax.random.key(seed)
        k1, k2, k3 = jax.random.split(key, 3)
        B, S, E = (2, 256, 256)
        kv_E = NUM_KV_HEADS * (E // NUM_Q_HEADS)
        q = jax.random.normal(k1, (B, S, E), dtype=jnp.float32)
        k = jax.random.normal(k2, (B, S, kv_E), dtype=jnp.float32)
        v = jax.random.normal(k3, (B, S, kv_E), dtype=jnp.float32)
        return {'q': q, 'k': k, 'v': v}
    _L3_xattn_all = _L3_xattn_setup()
    _L3_xattn_in = {k: v for k, v in _L3_xattn_all.items() if k in ()}
    del _L3_xattn_all

    def _L3_ffn_setup():
        import jax, jax.numpy as jnp
        import numpy as np
        B, S, D = (4, 256, 256)
        E = 8
        H = 352
        CAP_F = 1.0

        def _moe(x, Wg, W1, W3, W2, sw1, sw3, sw2):
            b, sl, d = x.shape
            T = b * sl
            C = int(CAP_F * T / E)
            xt = x.reshape(T, d)
            probs = jax.nn.softmax(xt @ Wg, axis=-1)
            eidx = jnp.argmax(probs, axis=-1)
            gate = jnp.take_along_axis(probs, eidx[:, None], 1)[:, 0]
            oh = jax.nn.one_hot(eidx, E, dtype=jnp.int32)
            pos = (jnp.cumsum(oh, axis=0) * oh).sum(-1) - 1
            keep = pos < C
            flat = jnp.where(keep, eidx * C + pos, E * C)
            xd = jnp.zeros((E * C, d), x.dtype).at[flat].set(xt, mode='drop')
            xd = xd.reshape(E, C, d)
            h = jax.nn.silu(jnp.einsum('ecd,edh->ech', xd, W1)) * jnp.einsum('ecd,edh->ech', xd, W3)
            oe = jnp.einsum('ech,ehd->ecd', h, W2).reshape(E * C, d)
            out = jnp.take(oe, jnp.minimum(flat, E * C - 1), axis=0)
            out = out * (gate * keep.astype(x.dtype))[:, None]
            shared = jax.nn.silu(xt @ sw1) * (xt @ sw3) @ sw2
            return (out + shared).reshape(b, sl, d)
        key = jax.random.key(seed)
        ks = jax.random.split(key, 8)
        s = lambda fan: 1.0 / np.sqrt(fan)
        return {'x': jax.random.normal(ks[0], (B, S, D), jnp.float32), 'Wg': jax.random.normal(ks[1], (D, E), jnp.float32) * s(D), 'W1': jax.random.normal(ks[2], (E, D, H), jnp.float32) * s(D), 'W3': jax.random.normal(ks[3], (E, D, H), jnp.float32) * s(D), 'W2': jax.random.normal(ks[4], (E, H, D), jnp.float32) * s(H), 'sw1': jax.random.normal(ks[5], (D, H), jnp.float32) * s(D), 'sw3': jax.random.normal(ks[6], (D, H), jnp.float32) * s(D), 'sw2': jax.random.normal(ks[7], (H, D), jnp.float32) * s(H)}
    _L3_ffn_all = _L3_ffn_setup()
    _L3_ffn_in = {k: v for k, v in _L3_ffn_all.items() if k in ('Wg', 'W1', 'W3', 'W2', 'sw1', 'sw3', 'sw2')}
    del _L3_ffn_all
    return {'x': x, 'ctx_512': ctx_512, 'L0_attn_wq': _L0_attn_in['wq'], 'L0_attn_bq': _L0_attn_in['bq'], 'L0_attn_wk': _L0_attn_in['wk'], 'L0_attn_bk': _L0_attn_in['bk'], 'L0_attn_wv': _L0_attn_in['wv'], 'L0_attn_bv': _L0_attn_in['bv'], 'L0_attn_wg': _L0_attn_in['wg'], 'L0_attn_bg': _L0_attn_in['bg'], 'L0_attn_wo': _L0_attn_in['wo'], 'L0_attn_bo': _L0_attn_in['bo'], 'L0_attn_gn_w': _L0_attn_in['gn_w'], 'L0_attn_gn_b': _L0_attn_in['gn_b'], 'L0_attn_gamma': _L0_attn_in['gamma'], 'L0_xattn_q_norm_w': _L0_xattn_in['q_norm_w'], 'L0_xattn_k_norm_w': _L0_xattn_in['k_norm_w'], 'L0_xattn_w_out': _L0_xattn_in['w_out'], 'L0_ffn_router_w': _L0_ffn_in['router_w'], 'L0_ffn_w1': _L0_ffn_in['w1'], 'L0_ffn_v1': _L0_ffn_in['v1'], 'L0_ffn_w2': _L0_ffn_in['w2'], 'L1_attn_Wq': _L1_attn_in['Wq'], 'L1_attn_Wk': _L1_attn_in['Wk'], 'L1_attn_Wv': _L1_attn_in['Wv'], 'L1_attn_Wo': _L1_attn_in['Wo'], 'L1_attn_gate': _L1_attn_in['gate'], 'L1_xattn_Wq': _L1_xattn_in['Wq'], 'L1_xattn_Wkv_expand': _L1_xattn_in['Wkv_expand'], 'L1_xattn_Wout': _L1_xattn_in['Wout'], 'L1_ffn_weight': _L1_ffn_in['weight'], 'L1_ffn_bias': _L1_ffn_in['bias'], 'L2_attn_in_proj_w': _L2_attn_in['in_proj_w'], 'L2_attn_conv_w': _L2_attn_in['conv_w'], 'L2_attn_conv_b': _L2_attn_in['conv_b'], 'L2_attn_dt_bias': _L2_attn_in['dt_bias'], 'L2_attn_A_log': _L2_attn_in['A_log'], 'L2_attn_D_param': _L2_attn_in['D_param'], 'L2_attn_norm_w': _L2_attn_in['norm_w'], 'L2_attn_out_proj_w': _L2_attn_in['out_proj_w'], 'L2_xattn_Wq': _L2_xattn_in['Wq'], 'L2_xattn_w_kc_q': _L2_xattn_in['w_kc_q'], 'L2_xattn_w_kc_kv': _L2_xattn_in['w_kc_kv'], 'L2_xattn_W_qr': _L2_xattn_in['W_qr'], 'L2_xattn_W_kr': _L2_xattn_in['W_kr'], 'L2_xattn_Wo': _L2_xattn_in['Wo'], 'L2_ffn_w_gate_up': _L2_ffn_in['w_gate_up'], 'L2_ffn_w_down': _L2_ffn_in['w_down'], 'L3_attn_wq': _L3_attn_in['wq'], 'L3_attn_bq': _L3_attn_in['bq'], 'L3_attn_wk': _L3_attn_in['wk'], 'L3_attn_bk': _L3_attn_in['bk'], 'L3_attn_wv': _L3_attn_in['wv'], 'L3_attn_bv': _L3_attn_in['bv'], 'L3_attn_wo': _L3_attn_in['wo'], 'L3_attn_bo': _L3_attn_in['bo'], 'L3_ffn_Wg': _L3_ffn_in['Wg'], 'L3_ffn_W1': _L3_ffn_in['W1'], 'L3_ffn_W3': _L3_ffn_in['W3'], 'L3_ffn_W2': _L3_ffn_in['W2'], 'L3_ffn_sw1': _L3_ffn_in['sw1'], 'L3_ffn_sw3': _L3_ffn_in['sw3'], 'L3_ffn_sw2': _L3_ffn_in['sw2']}

def reference(x, ctx_512, L0_attn_wq, L0_attn_bq, L0_attn_wk, L0_attn_bk, L0_attn_wv, L0_attn_bv, L0_attn_wg, L0_attn_bg, L0_attn_wo, L0_attn_bo, L0_attn_gn_w, L0_attn_gn_b, L0_attn_gamma, L0_xattn_q_norm_w, L0_xattn_k_norm_w, L0_xattn_w_out, L0_ffn_router_w, L0_ffn_w1, L0_ffn_v1, L0_ffn_w2, L1_attn_Wq, L1_attn_Wk, L1_attn_Wv, L1_attn_Wo, L1_attn_gate, L1_xattn_Wq, L1_xattn_Wkv_expand, L1_xattn_Wout, L1_ffn_weight, L1_ffn_bias, L2_attn_in_proj_w, L2_attn_conv_w, L2_attn_conv_b, L2_attn_dt_bias, L2_attn_A_log, L2_attn_D_param, L2_attn_norm_w, L2_attn_out_proj_w, L2_xattn_Wq, L2_xattn_w_kc_q, L2_xattn_w_kc_kv, L2_xattn_W_qr, L2_xattn_W_kr, L2_xattn_Wo, L2_ffn_w_gate_up, L2_ffn_w_down, L3_attn_wq, L3_attn_bq, L3_attn_wk, L3_attn_bk, L3_attn_wv, L3_attn_bv, L3_attn_wo, L3_attn_bo, L3_ffn_Wg, L3_ffn_W1, L3_ffn_W3, L3_ffn_W2, L3_ffn_sw1, L3_ffn_sw3, L3_ffn_sw2):
    import jax
    import jax.numpy as jnp

    def _L0_attn_ref(x, wq, bq, wk, bk, wv, bv, wg, bg, wo, bo, gn_w, gn_b, gamma):
        import jax, jax.numpy as jnp
        import numpy as np
        B, S, HID, QK, H = (2, 256, 256, 256, 16)
        DK, DV = (QK // H, HID // H)
        EPS = 1e-05
        b, s, hid = x.shape
        h = gamma.shape[0]
        dk = wq.shape[1] // h
        dv = hid // h
        q = (x @ wq + bq).reshape(b, s, h, dk).transpose(0, 2, 1, 3)
        k = (x @ wk + bk).reshape(b, s, h, dk).transpose(0, 2, 1, 3)
        v = (x @ wv + bv).reshape(b, s, h, dv).transpose(0, 2, 1, 3)
        idx = jnp.arange(s)
        diff = idx[:, None] - idx[None, :]
        expn = jnp.maximum(diff, 0).astype(x.dtype)
        dmask = jnp.where(diff >= 0, gamma[:, None, None] ** expn, 0.0)
        scores = jnp.einsum('bhnd,bhmd->bhnm', q, k) * dmask
        ret = jnp.einsum('bhnm,bhmv->bhnv', scores, v)
        mean = ret.mean(axis=(2, 3), keepdims=True)
        var = ((ret - mean) ** 2).mean(axis=(2, 3), keepdims=True)
        norm = (ret - mean) * jax.lax.rsqrt(var + EPS)
        norm = norm * gn_w.reshape(h, dv)[None, :, None, :] + gn_b.reshape(h, dv)[None, :, None, :]
        ro = norm.transpose(0, 2, 1, 3).reshape(b, s, hid)
        gate = jax.nn.silu(x @ wg + bg)
        out = gate * ro @ wo + bo
        return out

    def _L0_xattn_ref(q, k, v, q_norm_w, k_norm_w, w_out):
        import jax, jax.numpy as jnp
        import numpy as np
        N_HEADS = 16
        N_KV_HEADS = 4
        ROPE_THETA = 10000.0
        EPS = 1e-05

        def _rms_norm(x, w):
            var = jnp.mean(x * x, axis=-1, keepdims=True)
            return x * jax.lax.rsqrt(var + EPS) * w

        def _rope_sin_cos(T, head_dim, dtype):
            inv_freq = 1.0 / ROPE_THETA ** (jnp.arange(0, head_dim, 2, dtype=jnp.float32) / head_dim)
            t = jnp.arange(T, dtype=jnp.float32)
            freqs = jnp.outer(t, inv_freq)
            emb = jnp.concatenate([freqs, freqs], -1)
            return (jnp.sin(emb).astype(dtype)[None, None], jnp.cos(emb).astype(dtype)[None, None])

        def _rotate_half(x):
            h = x.shape[-1] // 2
            x1, x2 = (x[..., :h], x[..., h:])
            return jnp.concatenate([-x2, x1], axis=-1)
        B, T, C = q.shape
        hd = C // N_HEADS
        g = N_HEADS // N_KV_HEADS
        q = _rms_norm(q, q_norm_w)
        k = _rms_norm(k, k_norm_w)
        q = q.reshape(B, T, N_HEADS, hd).transpose(0, 2, 1, 3)
        k = k.reshape(B, T, N_KV_HEADS, hd).transpose(0, 2, 1, 3)
        v = v.reshape(B, T, N_KV_HEADS, hd).transpose(0, 2, 1, 3)
        sin, cos = _rope_sin_cos(T, hd, q.dtype)
        q = q * cos + _rotate_half(q) * sin
        k = k * cos + _rotate_half(k) * sin
        qg = q.reshape(B, N_KV_HEADS, g, T, hd)
        scale = 1.0 / jnp.sqrt(jnp.asarray(hd, q.dtype))
        scores = jnp.einsum('bgnqd,bgkd->bgnqk', qg, k) * scale
        causal = jnp.tril(jnp.ones((T, T), bool))
        scores = jnp.where(causal, scores, jnp.asarray(-1e+30, scores.dtype))
        attn = jax.nn.softmax(scores, axis=-1)
        out = jnp.einsum('bgnqk,bgkd->bgnqd', attn, v)
        out = out.reshape(B, N_HEADS, T, hd).transpose(0, 2, 1, 3).reshape(B, T, C)
        return out @ w_out.T

    def _L0_ffn_ref(hidden_states, router_w, w1, v1, w2):
        import jax, jax.numpy as jnp
        import numpy as np
        B, S, D = (1, 128, 256)
        E, K, F = (64, 8, 96)
        C = 32

        def _moe(x, router_w, w1, v1, w2):
            T = x.shape[0]
            logits = x @ router_w.T
            probs = jax.nn.softmax(logits, axis=-1)
            wts, idx = jax.lax.top_k(probs, K)
            wts = wts / jnp.sum(wts, axis=-1, keepdims=True)
            R = T * K
            e_flat = idx.reshape(-1)
            tok = jnp.arange(R) // K
            order = jnp.argsort(e_flat)
            e_s, tok_s = (e_flat[order], tok[order])
            w_s = wts.reshape(-1)[order]
            counts = jnp.bincount(e_flat, length=E)
            starts = jnp.cumsum(counts) - counts
            pos = jnp.arange(R) - starts[e_s]
            valid = pos < C
            pos_c = jnp.minimum(pos, C - 1)
            xg = jnp.zeros((E, C, D), x.dtype).at[e_s, pos_c].add(jnp.where(valid[:, None], x[tok_s], 0.0))
            h = jax.nn.silu(jnp.einsum('ecd,efd->ecf', xg, w1)) * jnp.einsum('ecd,efd->ecf', xg, v1)
            y = jnp.einsum('ecf,efd->ecd', h, w2)
            yr = y[e_s, pos_c] * jnp.where(valid, w_s, 0.0)[:, None]
            return jnp.zeros((T, D), x.dtype).at[tok_s].add(yr)
        b, s, d = hidden_states.shape
        x = hidden_states.transpose(1, 0, 2).reshape(s * b, d)
        out = _moe(x, router_w, w1, v1, w2)
        return out.reshape(s, b, d).transpose(1, 0, 2)

    def _L1_attn_ref(hidden_states, Wq, Wk, Wv, Wo, gate):
        import jax, jax.numpy as jnp
        import numpy as np
        HIDDEN = 256
        N_HEADS = 16
        HEAD_DIM = HIDDEN // N_HEADS

        def rotate_half(x):
            x1, x2 = jnp.split(x, 2, axis=-1)
            return jnp.concatenate([-x2, x1], axis=-1)
        B, S, H = hidden_states.shape
        q = hidden_states @ Wq.T
        k = hidden_states @ Wk.T
        v = hidden_states @ Wv.T
        inv_freq = 1.0 / 10000.0 ** (jnp.arange(0, H, 2, dtype=jnp.float32) / H)
        t = jnp.arange(S, dtype=jnp.float32)
        freqs = t[:, None] * inv_freq[None, :]
        emb = jnp.concatenate([freqs, freqs], axis=-1)[None]
        cos, sin = (jnp.cos(emb), jnp.sin(emb))
        q = q * cos + rotate_half(q) * sin
        k = k * cos + rotate_half(k) * sin

        def split_heads(x):
            return x.reshape(B, S, N_HEADS, HEAD_DIM).transpose(0, 2, 1, 3)
        q, k, v = (split_heads(q), split_heads(k), split_heads(v))
        k_feat = jax.nn.elu(k) + 1.0
        memory = jnp.einsum('bhsd,bhse->bhde', k_feat, v)
        norm_term = k_feat.sum(axis=2)
        q_feat = jax.nn.elu(q) + 1.0
        mem_out = jnp.einsum('bhsd,bhde->bhse', q_feat, memory)
        denom = jnp.einsum('bhsd,bhd->bhs', q_feat, norm_term)[..., None]
        mem_out = mem_out / denom
        scale = 1.0 / jnp.sqrt(jnp.float32(HEAD_DIM))
        scores = jnp.einsum('bhqd,bhkd->bhqk', q, k) * scale
        attn = jnp.einsum('bhqk,bhkd->bhqd', jax.nn.softmax(scores, axis=-1), v)
        g = jax.nn.sigmoid(gate)
        combined = g * mem_out + (1.0 - g) * attn
        combined = combined.transpose(0, 2, 1, 3).reshape(B, S, H)
        return combined @ Wo.T

    def _L1_xattn_ref(q, latent_kv, Wq, Wkv_expand, Wout):
        import jax, jax.numpy as jnp
        import numpy as np
        B, S, H, NH, L = (2, 256, 256, 16, 64)
        HD = H // NH
        b, sq, _ = q.shape
        sk = latent_kv.shape[1]
        qp = q @ Wq.T
        kv = latent_kv @ Wkv_expand.T
        k, v = jnp.split(kv, 2, axis=-1)
        qh = qp.reshape(b, sq, NH, HD).transpose(0, 2, 1, 3)
        kh = k.reshape(b, sk, NH, HD).transpose(0, 2, 1, 3)
        vh = v.reshape(b, sk, NH, HD).transpose(0, 2, 1, 3)
        inv_sqrt_d = 1.0 / jnp.sqrt(jnp.float32(HD))
        scores = jnp.einsum('bhqd,bhkd->bhqk', qh, kh) * inv_sqrt_d
        causal = jnp.tril(jnp.ones((sq, sk), dtype=bool))
        scores = jnp.where(causal, scores, jnp.finfo(scores.dtype).min)
        attn = jax.nn.softmax(scores, axis=-1)
        out = jnp.einsum('bhqk,bhkd->bhqd', attn, vh)
        out = out.transpose(0, 2, 1, 3).reshape(b, sq, H)
        return out @ Wout.T

    def _L1_ffn_ref(x, weight, bias):
        import jax, jax.numpy as jnp
        import numpy as np
        EPS = 1e-08

        def ternary_quantize(w):
            threshold = 0.7 * jnp.mean(jnp.abs(w), axis=-1, keepdims=True)
            q = jnp.where(w > threshold, 1.0, jnp.where(w < -threshold, -1.0, 0.0)).astype(w.dtype)
            return w + jax.lax.stop_gradient(q - w)
        q_weight = ternary_quantize(weight)
        return jnp.einsum('bsi,oi->bso', x, q_weight) + bias

    def _L2_attn_ref(hidden_states, in_proj_w, conv_w, conv_b, dt_bias, A_log, D_param, norm_w, out_proj_w):
        import jax, jax.numpy as jnp
        import numpy as np
        from jax import lax
        H, P, N, G, K, CHUNK = (64, 64, 128, 1, 4, 32)
        D_MODEL = 256
        D_INNER = H * P
        CONV_DIM = D_INNER + 2 * G * N
        EPS = 1e-05

        def _mamba2_forward(hidden_states, in_proj_w, conv_w, conv_b, dt_bias, A_log, D_param, norm_w, out_proj_w):
            b, l, _ = hidden_states.shape
            c = l // CHUNK
            proj = hidden_states @ in_proj_w
            gate = proj[..., :D_INNER]
            hbc = proj[..., D_INNER:D_INNER + CONV_DIM]
            dt = proj[..., D_INNER + CONV_DIM:]
            xt = hbc.transpose(0, 2, 1)
            y = lax.conv_general_dilated(xt, conv_w[:, None, :], window_strides=(1,), padding=[(K - 1, 0)], feature_group_count=CONV_DIM, dimension_numbers=('NCH', 'OIH', 'NCH'))
            hbc = jax.nn.silu(y + conv_b[None, :, None]).transpose(0, 2, 1)
            per_g = D_INNER // G
            hg = hbc.reshape(b, l, G, per_g + 2 * N)
            x = hg[..., :per_g].reshape(b, l, H, P)
            Bm = hg[..., per_g:per_g + N]
            Cm = hg[..., per_g + N:]
            hpg = H // G
            Bh = jnp.repeat(Bm, hpg, axis=2)
            Ch = jnp.repeat(Cm, hpg, axis=2)
            dt = jax.nn.softplus(dt + dt_bias)
            A = -jnp.exp(A_log)
            x_c = x.reshape(b, c, CHUNK, H, P)
            B_c = Bh.reshape(b, c, CHUNK, H, N)
            C_c = Ch.reshape(b, c, CHUNK, H, N)
            dt_c = dt.reshape(b, c, CHUNK, H)
            dA = dt_c * A[None, None, None, :]
            cum = jnp.cumsum(dA, axis=2)
            diff = cum[:, :, :, None, :] - cum[:, :, None, :, :]
            i = jnp.arange(CHUNK)
            mask = i[:, None] >= i[None, :]
            decay = jnp.exp(jnp.where(mask[None, None, :, :, None], diff, -jnp.inf))
            scores = jnp.einsum('bcihn,bcjhn->bcijh', C_c, B_c) * decay * dt_c[:, :, None, :, :]
            Y_diag = jnp.einsum('bcijh,bcjhp->bcihp', scores, x_c)
            decay_states = jnp.exp(cum[:, :, -1:, :] - cum)
            states = jnp.einsum('bclh,bclhn,bclhp->bchpn', decay_states * dt_c, B_c, x_c)
            chunk_decay = jnp.exp(cum[:, :, -1, :])

            def step(prev, inp):
                st, cd = inp
                new = cd[:, :, None, None] * prev + st
                return (new, prev)
            init = jnp.zeros((b, H, P, N), hidden_states.dtype)
            _, prev_states = lax.scan(step, init, (jnp.moveaxis(states, 1, 0), jnp.moveaxis(chunk_decay, 1, 0)))
            prev_states = jnp.moveaxis(prev_states, 0, 1)
            state_decay_out = jnp.exp(cum)
            Y_off = jnp.einsum('bclhn,bchpn,bclh->bclhp', C_c, prev_states, state_decay_out)
            yh = (Y_diag + Y_off).reshape(b, l, H, P) + D_param[None, None, :, None] * x
            yr = yh.reshape(b, l, D_INNER)
            hidden = yr * jax.nn.silu(gate)
            var = jnp.mean(hidden * hidden, axis=-1, keepdims=True)
            hidden = hidden * lax.rsqrt(var + EPS) * norm_w
            return hidden @ out_proj_w
        return _mamba2_forward(hidden_states, in_proj_w, conv_w, conv_b, dt_bias, A_log, D_param, norm_w, out_proj_w)

    def _L2_xattn_ref(hidden_q, kv_c, Wq, w_kc_q, w_kc_kv, W_qr, W_kr, Wo):
        import jax, jax.numpy as jnp
        import numpy as np
        B, S, L = (2, 128, 128)
        DIM_Q, H, K, D_C, D_CQ, R = (256, 16, 128, 64, 192, 64)

        def _rope_tables(length, dim):
            inv = 1.0 / 10000.0 ** (jnp.arange(0, dim, 2, dtype=jnp.float32) / dim)
            f = jnp.arange(length, dtype=jnp.float32)[:, None] * inv[None, :]
            sin = jnp.repeat(jnp.sin(f), 2, axis=-1)
            cos = jnp.repeat(jnp.cos(f), 2, axis=-1)
            return (sin, cos)

        def _rotate_half(x):
            half = x.shape[-1] // 2
            return jnp.concatenate([-x[..., half:], x[..., :half]], axis=-1)

        def _apply_rope(x, sin, cos):
            return x * cos + _rotate_half(x) * sin
        Bv, Sv, _ = hidden_q.shape
        _, Lv, _ = kv_c.shape
        q_hk = (hidden_q @ Wq.T).reshape(Bv, Sv, H, K)
        q_big = jnp.einsum('bshk,hkq->bshq', q_hk, w_kc_q)
        sin_q, cos_q = _rope_tables(Sv, D_CQ)
        q_big = _apply_rope(q_big, sin_q[None, :, None, :], cos_q[None, :, None, :])
        sin_k, cos_k = _rope_tables(Lv, D_C)
        kv_r = _apply_rope(kv_c, sin_k[None], cos_k[None])
        q_r = jnp.einsum('bshq,hqr->bhsr', q_big, W_qr)
        k_r = jnp.einsum('bld,hdr->bhlr', kv_r, W_kr)
        scores = jnp.einsum('bhsr,bhlr->bhsl', q_r, k_r)
        attn = jax.nn.softmax(scores, axis=-1)
        ctx_c = jnp.einsum('bhsl,bld->bhsd', attn, kv_r)
        ctx_lat = jnp.einsum('bhsd,hkd->bhsk', ctx_c, w_kc_kv)
        ctx = ctx_lat.transpose(0, 2, 1, 3).reshape(Bv, Sv, H * K)
        return ctx @ Wo.T

    def _L2_ffn_ref(h_shard, w_gate_up, w_down):
        import jax, jax.numpy as jnp
        import numpy as np
        HIDDEN = 256
        INTER = 1024
        BATCH, LOCAL_SEQ = (2, 512)
        batch, local_seq, hidden = h_shard.shape
        gate_up = jnp.einsum('bsh,oh->bso', h_shard, w_gate_up)
        gate, up = jnp.split(gate_up, 2, axis=-1)
        h = jax.nn.silu(gate) * up
        out = jnp.einsum('bsi,hi->bsh', h, w_down)
        return out

    def _L3_attn_ref(x, wq, bq, wk, bk, wv, bv, wo, bo):
        import jax, jax.numpy as jnp
        import numpy as np
        EMBED_DIM = 256
        NUM_HEADS = 16
        HEAD_DIM = EMBED_DIM // NUM_HEADS

        def _apply_rope(q, k, seq_len):
            hd = q.shape[-1]
            theta = 10000.0 ** (-jnp.arange(0, hd, 2, dtype=jnp.float32) / hd)
            pos = jnp.arange(seq_len, dtype=jnp.float32)
            freqs = pos[:, None] * theta[None, :]
            sin = jnp.sin(freqs)[None, None]
            cos = jnp.cos(freqs)[None, None]
            q_rot = q[..., ::2] * cos - q[..., 1::2] * sin
            k_rot = k[..., ::2] * cos - k[..., 1::2] * sin
            q = jnp.concatenate([q_rot, q[..., 1::2]], axis=-1)
            k = jnp.concatenate([k_rot, k[..., 1::2]], axis=-1)
            return (q, k)
        B, S, D = x.shape
        H, hd = (NUM_HEADS, HEAD_DIM)

        def proj(w, b):
            return (x @ w.T + b).reshape(B, S, H, hd).transpose(0, 2, 1, 3)
        q = proj(wq, bq)
        k = proj(wk, bk)
        v = proj(wv, bv)
        q, k = _apply_rope(q, k, S)
        scores = jnp.einsum('bhqd,bhkd->bhqk', q, k) / jnp.sqrt(jnp.float32(hd))
        attn = jax.nn.softmax(scores, axis=-1)
        ctx = jnp.einsum('bhqk,bhkd->bhqd', attn, v)
        ctx = ctx.transpose(0, 2, 1, 3).reshape(B, S, D)
        return ctx @ wo.T + bo

    def _L3_xattn_ref(q, k, v):
        import jax, jax.numpy as jnp
        import numpy as np
        import math
        NUM_Q_HEADS = 32
        NUM_KV_HEADS = 8
        B, S, E = q.shape
        H, KV = (NUM_Q_HEADS, NUM_KV_HEADS)
        D = E // H
        G = H // KV
        scale = math.sqrt(D)
        qh = q.reshape(B, S, KV, G, D).transpose(0, 2, 3, 1, 4)
        kh = k.reshape(B, S, KV, D).transpose(0, 2, 1, 3)
        vh = v.reshape(B, S, KV, D).transpose(0, 2, 1, 3)
        scores = jnp.einsum('bkgsd,bktd->bkgst', qh, kh) / scale
        weights = jax.nn.softmax(scores, axis=-1)
        out = jnp.einsum('bkgst,bktd->bkgsd', weights, vh)
        return out.transpose(0, 3, 1, 2, 4).reshape(B, S, E)

    def _L3_ffn_ref(x, Wg, W1, W3, W2, sw1, sw3, sw2):
        import jax, jax.numpy as jnp
        import numpy as np
        B, S, D = (4, 256, 256)
        E = 8
        H = 352
        CAP_F = 1.0

        def _moe(x, Wg, W1, W3, W2, sw1, sw3, sw2):
            b, sl, d = x.shape
            T = b * sl
            C = int(CAP_F * T / E)
            xt = x.reshape(T, d)
            probs = jax.nn.softmax(xt @ Wg, axis=-1)
            eidx = jnp.argmax(probs, axis=-1)
            gate = jnp.take_along_axis(probs, eidx[:, None], 1)[:, 0]
            oh = jax.nn.one_hot(eidx, E, dtype=jnp.int32)
            pos = (jnp.cumsum(oh, axis=0) * oh).sum(-1) - 1
            keep = pos < C
            flat = jnp.where(keep, eidx * C + pos, E * C)
            xd = jnp.zeros((E * C, d), x.dtype).at[flat].set(xt, mode='drop')
            xd = xd.reshape(E, C, d)
            h = jax.nn.silu(jnp.einsum('ecd,edh->ech', xd, W1)) * jnp.einsum('ecd,edh->ech', xd, W3)
            oe = jnp.einsum('ech,ehd->ecd', h, W2).reshape(E * C, d)
            out = jnp.take(oe, jnp.minimum(flat, E * C - 1), axis=0)
            out = out * (gate * keep.astype(x.dtype))[:, None]
            shared = jax.nn.silu(xt @ sw1) * (xt @ sw3) @ sw2
            return (out + shared).reshape(b, sl, d)
        return _moe(x, Wg, W1, W3, W2, sw1, sw3, sw2)
    x = _layernorm(x + _L0_attn_ref(x, L0_attn_wq, L0_attn_bq, L0_attn_wk, L0_attn_bk, L0_attn_wv, L0_attn_bv, L0_attn_wg, L0_attn_bg, L0_attn_wo, L0_attn_bo, L0_attn_gn_w, L0_attn_gn_b, L0_attn_gamma), axis=-1)
    x = _layernorm(x + _L0_xattn_ref(x, ctx_512, ctx_512, L0_xattn_q_norm_w, L0_xattn_k_norm_w, L0_xattn_w_out), axis=-1)
    x = _layernorm(x + _L0_ffn_ref(x, L0_ffn_router_w, L0_ffn_w1, L0_ffn_v1, L0_ffn_w2), axis=-1)
    x = _layernorm(x + _L1_attn_ref(x, L1_attn_Wq, L1_attn_Wk, L1_attn_Wv, L1_attn_Wo, L1_attn_gate), axis=-1)
    x = _layernorm(x + _L1_xattn_ref(x, ctx_512, L1_xattn_Wq, L1_xattn_Wkv_expand, L1_xattn_Wout), axis=-1)
    x = _layernorm(x + _L1_ffn_ref(x, L1_ffn_weight, L1_ffn_bias), axis=-1)
    x = _layernorm(x + _L2_attn_ref(x, L2_attn_in_proj_w, L2_attn_conv_w, L2_attn_conv_b, L2_attn_dt_bias, L2_attn_A_log, L2_attn_D_param, L2_attn_norm_w, L2_attn_out_proj_w), axis=-1)
    x = _layernorm(x + _L2_xattn_ref(x, ctx_512, L2_xattn_Wq, L2_xattn_w_kc_q, L2_xattn_w_kc_kv, L2_xattn_W_qr, L2_xattn_W_kr, L2_xattn_Wo), axis=-1)
    x = _layernorm(x + _L2_ffn_ref(x, L2_ffn_w_gate_up, L2_ffn_w_down), axis=-1)
    x = _layernorm(x + _L3_attn_ref(x, L3_attn_wq, L3_attn_bq, L3_attn_wk, L3_attn_bk, L3_attn_wv, L3_attn_bv, L3_attn_wo, L3_attn_bo), axis=-1)
    x = _layernorm(x + _L3_xattn_ref(x, ctx_512, ctx_512), axis=-1)
    x = _layernorm(x + _L3_ffn_ref(x, L3_ffn_Wg, L3_ffn_W1, L3_ffn_W3, L3_ffn_W2, L3_ffn_sw1, L3_ffn_sw3, L3_ffn_sw2), axis=-1)
    return x

_drawn_inputs = setup_inputs


def setup_inputs(seed=0):
    import zlib

    import numpy as np

    out = dict(_drawn_inputs(seed))
    spreads = {'L0_attn_bq': (0.0, 0.1),
     'L0_attn_bk': (0.0, 0.1),
     'L0_attn_bv': (0.0, 0.1),
     'L0_attn_bg': (0.0, 0.1),
     'L0_attn_bo': (0.0, 0.1),
     'L0_attn_gn_w': (1.0, 0.2),
     'L0_attn_gn_b': (0.0, 0.1),
     'L0_xattn_q_norm_w': (1.0, 0.2),
     'L0_xattn_k_norm_w': (1.0, 0.2),
     'L1_attn_gate': (0.0, 0.795),
     'L2_attn_conv_b': (0.0, 0.1),
     'L2_attn_dt_bias': (1.0, 0.2),
     'L2_attn_D_param': (1.0, 0.2),
     'L2_attn_norm_w': (1.0, 0.2)}
    factors = {'L0_ffn_router_w': 8.0,
     'L0_ffn_w1': 8.0,
     'L0_ffn_v1': 8.0,
     'L0_ffn_w2': 7.652,
     'L1_xattn_Wq': 25.37,
     'L1_ffn_bias': 18.971,
     'L3_attn_bq': 24.318,
     'L3_attn_bk': 32.174}
    for name, (base, spread) in spreads.items():
        noise = np.random.default_rng([zlib.crc32(name.encode()), seed]).standard_normal(out[name].shape)
        drawn = base * np.exp(spread * noise) if base else spread * noise
        out[name] = jnp.asarray(drawn.astype(out[name].dtype))
    for name, factor in factors.items():
        out[name] = (out[name] * factor).astype(out[name].dtype)
    return out
```

```python
from contextlib import ExitStack

import numpy as np

import concourse.bass as bass
from concourse import mybir

LAYERS = (0, 1, 2, 3, 4, 5, 6, 7, 8, 9, 10, 11)

F32 = mybir.dt.float32
ALU = mybir.AluOpType
ACT = mybir.ActivationFunctionType
AX = mybir.AxisListType

B, S, D, DC = 32, 64, 256, 64
TOK = B * S
P = 128
NT = TOK // P
H, HD = 16, 16
LN_EPS = 1e-5
NEG = -1e30


class Layer:

    def __init__(self, sems, base):
        self.sems, self.base, self.used = sems, base, set()

    def s(self, name):
        assert name in self.base, name
        self.used.add(name)
        return self.sems[name]

    def after(self, name, n):
        return self.sems[name], self.base[name] + n


OWN_DMA = ("gathered", "scattered", "fetched", "slot_y_out0", "slot_y_out1", "ctx_loaded0", "ctx_loaded1")


def stage_semaphores(nc, ctx, layers):
    slots, of = [], {}
    for names in layers:
        free = [slot for slot in slots if not any(n in names or n in OWN_DMA for n in slot)]
        for name in names:
            if name not in of:
                slot = next((slot for slot in free if name not in OWN_DMA and not any(name in other and any(n in other for n in slot)
                                                              for other in layers)), None)
                if slot is None:
                    slots.append([name])
                    of[name] = slots[-1]
                else:
                    slot.append(name)
                    free.remove(slot)
                    of[name] = slot
    sem = {id(slot): ctx.enter_context(nc.semaphore("_or_".join(slot))) for slot in slots}
    value = {id(slot): 0 for slot in slots}
    made = []
    for names in layers:
        made.append(Layer({n: sem[id(of[n])] for n in names}, {n: value[id(of[n])] for n in names}))
        for n, count in names.items():
            value[id(of[n])] += count
    return made


class Mem:
    pass


class Arena:

    def __init__(self, tensor):
        self.tensor, self.at = tensor, 0

    def take(self, dims, rows=P):
        n = int(np.prod(dims))
        assert self.at + n <= self.tensor.shape[1], (self.at, n, self.tensor.shape)
        ap = self.tensor[0:rows, self.at:self.at + n]
        self.at += n
        if len(dims) > 1:
            names = "abcdef"[:len(dims)]
            ap = ap.rearrange("p (" + " ".join(names) + ") -> p " + " ".join(names),
                              **{k: v for k, v in zip(names[1:], dims[1:])})
        return ap



TILE = ("x_written", "x_copied", "r_kept", "stats_ready", "aggr_ready", "var_ready", "rstd_ready")
CORE = TILE + ("qm_ready", "kT_kept", "scores_ready", "pT_ready", "pT_kept0", "pT_kept1", "v_kept", "o_ready",
               "o_kept", "oT_ready", "oT_kept", "y_ready")
SOFTMAX = ("max_ready", "shift_ready", "exp_ready", "sum_ready", "rinv_ready")


def per_tile(*names):
    return {n: NT for n in names}


def attn_places(m, ar):
    m.xc, m.xT, m.r = ar.take([2, D]), ar.take([2, 2, P]), ar.take([2, D])
    m.bn, m.stat = ar.take([2, 6]), ar.take([2, 16])
    m.qm, m.qT, m.kT, m.v = ar.take([2, 2, 2, 4, S]), ar.take([2, 2, P]), ar.take([2, 2, P]), ar.take([2, D])
    m.pr, m.pT = ar.take([2, 1024]), ar.take([2, 1024])
    m.o, m.o2, m.oT = ar.take([2, D]), ar.take([2, D]), ar.take([2, D])
    m.mx, m.sums, m.rinv = ar.take([2, 16]), ar.take([2, 16]), ar.take([2, 16])
    m.cb = ar.take([2, DC])


def l0_places(m, ar):
    attn_places(m, ar)
    m.s1, m.lng, m.decay = ar.take([2, 16]), ar.take([8]), ar.take([8 * S])
    m.gT, m.gE = ar.take([2, 2, P]), ar.take([2, 2, P])


def l1_places(m, ar):
    attn_places(m, ar)
    m.qn, m.qt1, m.qt2, m.qk = ar.take([2, D + DC]), ar.take([2, D + DC]), ar.take([2, D + DC]), ar.take([2, 2 * D])


def l3_places(m, ar):
    attn_places(m, ar)
    m.qf, m.pr2 = ar.take([2, 2, 2, 4, S]), ar.take([2, 1024])
    m.rt1, m.rt2, m.ft = ar.take([2, 2 * D]), ar.take([2, 2 * D]), ar.take([2, 2 * D])
    m.lsum, m.linv, m.gsig, m.grest = ar.take([2, 16]), ar.take([2, 16]), ar.take([16]), ar.take([16])


def l4_places(m, ar):
    attn_places(m, ar)
    m.ctxT = ar.take([2, P], DC)


def l5_places(m, ar):
    attn_places(m, ar)
    m.ta, m.tb, m.tern, m.ternT, m.tstat = (ar.take([2, D]), ar.take([2, D]), ar.take([2, D]), ar.take([2, D]),
                                            ar.take([2, 4]))


def l9_places(m, ar):
    attn_places(m, ar)
    m.rt1, m.rt2 = ar.take([2, 2 * D]), ar.take([2, 2 * D])


def l10_places(m, ar):
    attn_places(m, ar)
    m.qm8 = ar.take([2, 2, 8, S])


def pool_copy_x(pool, m, L, T, j):
    pool.wait_ge(*L.after("x_written", T - 1))
    pool.tensor_copy(m.xc[:, j, :], m.x[:, T, :]).then_inc(L.s("x_copied"), 1)


def pool_rstd(pool, m, L, T, j):
    pool.wait_ge(*L.after("var_ready", T + 1))
    pool.tensor_tensor(m.stat[:, j, 3:4], m.stat[:, j, 2:3], m.mhalf[:, 0:1], ALU.pow).then_inc(L.s("rstd_ready"), 1)


def dve_residual_norm(dve, m, L, i, y_name, y_of, scale_of=None):
    for j in range(2):
        T = 2 * i + j
        dve.wait_ge(*L.after(y_name, T + 1))
        dve.tensor_tensor(m.r[:, j, :], y_of(j), m.xc[:, j, :], ALU.add).then_inc(L.s("r_kept"), 1)
    dve_norm_tail(dve, m, L, i)


def dve_norm_tail(dve, m, L, i):
    for j in range(2):
        T = 2 * i + j
        dve.wait_ge(*L.after("r_kept", T + 1))
        dve.bn_stats(m.bn[:, j, :], m.r[:, j, :]).then_inc(L.s("stats_ready"), 1)
    dve.wait_ge(*L.after("stats_ready", 2 * i + 2))
    dve.memset(m.pause[:, :], 0.0)
    for j in range(2):
        dve.bn_aggr(m.stat[:, j, 0:2], m.bn[:, j, :]).then_inc(L.s("aggr_ready"), 1)
    for j in range(2):
        T = 2 * i + j
        dve.wait_ge(*L.after("aggr_ready", T + 1))
        dve.tensor_scalar(m.stat[:, j, 2:3], m.stat[:, j, 1:2], LN_EPS, None, ALU.add).then_inc(L.s("var_ready"), 1)
    for j in range(2):
        T = 2 * i + j
        dve.wait_ge(*L.after("rstd_ready", T + 1))
        dve.tensor_scalar(m.x[:, T, :], m.r[:, j, :], m.stat[:, j, 0:1], m.stat[:, j, 3:4],
                          ALU.subtract, ALU.mult).then_inc(L.s("x_written"), 1)


def pe_xT(pe, m, L, i):
    for j in range(2):
        pe.wait_ge(*L.after("x_copied", 2 * i + j + 1))
        for h in range(2):
            ins = pe.transpose(m.work(j)[:, h * P:(h + 1) * P], m.xc[:, j, h * P:(h + 1) * P], m.ident[:])
        ins.then_inc(L.s("xT_ready"), 1)


def act_xT(act, m, L, i):
    for j in range(2):
        act.wait_ge(*L.after("xT_ready", 2 * i + j + 1))
        act.copy(m.xT[:, j], m.work(j)[:, 0:D].rearrange("p (h t) -> p h t", h=2)).then_inc(L.s("xT_kept"), 1)


def pe_projT(pe, m, out, w, j, dup=None):
    for h in range(2):
        for k in range(2):
            ins = pe.matmul(out[:, h * P:(h + 1) * P], w[:, k, h * P:(h + 1) * P], m.xT[:, j, k, :],
                            start=(k == 0), stop=(k == 1))
    return ins


def pe_proj(pe, m, out, w, j, bias=None):
    for k in range(2):
        ins = pe.matmul(out, m.xT[:, j, k, :], w[:, k, :], start=(k == 0), stop=(k == 1 and bias is None))
    if bias is not None:
        ins = pe.matmul(out, m.ones_row[0:1, :], bias, start=False, stop=True)
    return ins


def pe_scores_of(pe, m, j, qm, kT):
    for half in range(2):
        for g in range(2):
            rows = slice(64 * g, 64 * g + 64)
            for p2 in range(2):
                for b in range(2):
                    at = ((half * 2 + p2) * 2 + b) * S
                    ins = pe.matmul(m.bank(j, g)[:, at:at + S],
                                    qm[rows, j, half, b, 2 * p2:2 * p2 + 2, :].rearrange("p e s -> p (e s)"),
                                    kT[rows, j, half, b * S:(b + 1) * S], start=True, stop=True)
    return ins


def dve_qmask(dve, m, L, j, src, mask, qm=None, name="qm_ready", heads=4):
    qm = m.qm if qm is None else qm
    for half in range(2):
        ins = dve.tensor_tensor(qm[:, j, half],
                                src[:, half * P:(half + 1) * P].rearrange("p (b s) -> p b s", b=2).unsqueeze(2)
                                .to_broadcast([P, 2, heads, S]),
                                mask[:, 0:heads].unsqueeze(1).unsqueeze(3).to_broadcast([P, 2, heads, S]), ALU.mult)
    ins.then_inc(L.s(name), 1)


def pe_scores(pe, m, L, i):
    for j in range(2):
        T = 2 * i + j
        pe.wait_ge(*L.after("qm_ready", T + 1))
        pe.wait_ge(*L.after("kT_kept", T + 1))
        pe_scores_of(pe, m, j, m.qm, m.kT).then_inc(L.s("scores_ready"), 1)


def pe_pT(pe, m, L, i, name="exp_ready"):
    for j in range(2):
        pe.wait_ge(*L.after(name, 2 * i + j + 1))
        for u in range(8):
            ins = pe.transpose(m.bank(j, u // 4)[:, (u % 4) * P:(u % 4 + 1) * P], m.pr[:, j, u * P:(u + 1) * P], m.ident[:])
        ins.then_inc(L.s("pT_ready"), 1)


def act_pT(act, m, L, i):
    for j in range(2):
        act.wait_ge(*L.after("pT_ready", 2 * i + j + 1))
        act.copy(m.pT[:, j, 0:512], m.bank(j, 0)).then_inc(L.s("pT_kept0"), 1)


def dve_pT(dve, m, L, i):
    for j in range(2):
        dve.wait_ge(*L.after("pT_ready", 2 * i + j + 1))
        dve.tensor_copy(m.pT[:, j, 512:1024], m.bank(j, 1)).then_inc(L.s("pT_kept1"), 1)


def pe_pv(pe, m, L, i, width, v_of):
    for j in range(2):
        T = 2 * i + j
        pe.wait_ge(*L.after("pT_kept0", T + 1))
        pe.wait_ge(*L.after("pT_kept1", T + 1))
        pe.wait_ge(*L.after("v_kept", T + 1))
        for u in range(8):
            for b in range(2):
                rows = slice(64 * b, 64 * b + 64)
                ins = pe.matmul(m.obank(j, b)[:, u * width:(u + 1) * width], m.pT[rows, j, u * P:(u + 1) * P],
                                v_of(rows, j, u), start=True, stop=True)
        ins.then_inc(L.s("o_ready"), 1)


def v_mha(m):
    return lambda rows, j, u: m.v[rows, j, u * 32:(u + 1) * 32]


def dve_o(dve, m, L, i, shared, scaled=True):
    for j in range(2):
        T = 2 * i + j
        dve.wait_ge(*L.after("o_ready", T + 1))
        if scaled:
            dve.wait_ge(*L.after("rinv_ready", T + 1))
        for b in range(2):
            for h2 in range(2):
                rows = slice(64 * h2, 64 * h2 + 64)
                if shared:
                    if h2:
                        continue
                    rows = slice(0, P)
                    src = m.obank(j, b)[rows, 0:P].rearrange("p (u d) -> p u d", u=8)
                else:
                    src = m.obank(j, b)[rows, 0:D].rearrange("p (u e d) -> p u e d", u=8, e=2)[:, :, h2, :]
                dst = m.o[rows, j, b * P:(b + 1) * P].rearrange("p (u d) -> p u d", u=8)
                if scaled:
                    r = m.rinv[rows, j, :].rearrange("p (u b) -> p u b", b=2)[:, :, b].unsqueeze(2)
                    ins = dve.tensor_tensor(dst, src, r.to_broadcast([rows.stop - rows.start, 8, HD]), ALU.mult)
                else:
                    ins = dve.tensor_copy(dst, src)
        ins.then_inc(L.s("o_kept"), 1)


def pe_oT(pe, m, L, i, name="o_kept"):
    for j in range(2):
        pe.wait_ge(*L.after(name, 2 * i + j + 1))
        for b in range(2):
            ins = pe.transpose(m.bank(j, 1)[:, b * P:(b + 1) * P], m.o[:, j, b * P:(b + 1) * P], m.ident[:])
        ins.then_inc(L.s("oT_ready"), 1)


def act_oT(act, m, L, i):
    for j in range(2):
        act.wait_ge(*L.after("oT_ready", 2 * i + j + 1))
        act.copy(m.oT[:, j, :], m.bank(j, 1)[:, 0:D]).then_inc(L.s("oT_kept"), 1)


def pe_out(pe, m, L, i, wo, bias=None):
    for j in range(2):
        pe.wait_ge(*L.after("oT_kept", 2 * i + j + 1))
        for b in range(2):
            out = m.work(j)[b * 64:(b + 1) * 64, 0:D]
            for h2 in range(2):
                ins = pe.matmul(out, m.oT[:, j, b * P + h2 * 64:b * P + h2 * 64 + 64], wo[:, h2, :],
                                start=(h2 == 0), stop=(h2 == 1 and bias is None))
            if bias is not None:
                ins = pe.matmul(out, m.ones_row[0:1, 0:64], bias, start=False, stop=True)
        ins.then_inc(L.s("y_ready"), 1)


def dve_softmax(dve, m, L, i, causal):
    for j in range(2):
        T = 2 * i + j
        dve.wait_ge(*L.after("scores_ready", T + 1))
        for g in range(2):
            sc = m.bank(j, g)[:, :].rearrange("p (f r k) -> p f r k", f=2, r=4)
            pr = m.pr[:, j, :].rearrange("p (f g r k) -> p f g r k", f=2, g=2, r=4)[:, :, g]
            mx = m.mx[:, j, :].rearrange("p (f g r) -> p f g r", f=2, g=2)[:, :, g]
            if causal:
                ins = dve.tensor_tensor(pr, sc, m.causal[:, :].unsqueeze(1).unsqueeze(1).to_broadcast([P, 2, 4, S]), ALU.add)
            else:
                ins = dve.tensor_reduce(mx, sc, AX.X, ALU.max)
        ins.then_inc(L.s("scores_kept" if causal else "max_ready"), 1)
    if causal:
        for j in range(2):
            dve.wait_ge(*L.after("scores_kept", 2 * i + j + 1))
            dve.tensor_reduce(m.mx[:, j, :], m.pr[:, j, :].rearrange("p (r k) -> p r k", k=S), AX.X, ALU.max)\
               .then_inc(L.s("max_ready"), 1)
    for j in range(2):
        T = 2 * i + j
        dve.wait_ge(*L.after("max_ready", T + 1))
        if causal:
            pr = m.pr[:, j, :].rearrange("p (r k) -> p r k", k=S)
            ins = dve.tensor_tensor(pr, pr, m.mx[:, j, :].unsqueeze(2).to_broadcast([P, 16, S]), ALU.subtract)
        else:
            for g in range(2):
                sc = m.bank(j, g)[:, :].rearrange("p (f r k) -> p f r k", f=2, r=4)
                pr = m.pr[:, j, :].rearrange("p (f g r k) -> p f g r k", f=2, g=2, r=4)[:, :, g]
                mx = m.mx[:, j, :].rearrange("p (f g r) -> p f g r", f=2, g=2)[:, :, g]
                ins = dve.tensor_tensor(pr, sc, mx.unsqueeze(3).to_broadcast([P, 2, 4, S]), ALU.subtract)
        ins.then_inc(L.s("shift_ready"), 1)


def act_exp(act, m, L, i):
    for j in range(2):
        act.wait_ge(*L.after("shift_ready", 2 * i + j + 1))
        ins = act.activation(m.pr[:, j, :], m.pr[:, j, :], ACT.Exp)
        ins.then_inc(L.s("exp_ready"), 1)


def dve_sums(dve, m, L, i):
    for j in range(2):
        dve.wait_ge(*L.after("exp_ready", 2 * i + j + 1))
        dve.tensor_reduce(m.sums[:, j, :], m.pr[:, j, :].rearrange("p (r k) -> p r k", k=S), AX.X, ALU.add)\
           .then_inc(L.s("sum_ready"), 1)
    for j in range(2):
        dve.wait_ge(*L.after("sum_ready", 2 * i + j + 1))
        dve.reciprocal(m.rinv[:, j, :], m.sums[:, j, :]).then_inc(L.s("rinv_ready"), 1)



def l0_names():
    n = per_tile(*CORE, "xT_ready", "xT_kept", "q_ready", "v_ready", "p_ready", "s1_ready", "mean_ready", "centred",
                 "sq_ready", "s2_ready", "gvar_ready", "gvar_kept", "grstd_ready", "normed", "g_ready", "g_kept",
                 "g_exp", "gate_ready", "affine_ready")
    n.update({"lng_ready": 1, "dist_ready": 8, "decay_exp": 1, "decay_ready": 1, "qT_part": 2 * NT})
    return n


def l0_pe(pe, m, L):
    pe.wait_ge(m.s_w[0], 16 * m.n_w[0])
    w = m.w
    with pe.Fori(0, NT // 2) as i:
        pe_xT(pe, m, L, i)
        for j in range(2):
            pe.wait_ge(*L.after("xT_kept", 2 * i + j + 1))
            pe_projT(pe, m, m.proj(j)[:, 0:D], w["l0_wq"], j)
            pe_projT(pe, m, m.proj(j)[:, D:2 * D], w["l0_wk"], j).then_inc(L.s("q_ready"), 1)
            pe_proj(pe, m, m.work(j)[:, 0:D], w["l0_wv"], j, w["l0_bv"][0:1, :]).then_inc(L.s("v_ready"), 1)
        pe_scores(pe, m, L, i)
        for j in range(2):
            pe_projT(pe, m, m.proj(j)[:, 0:D], w["l0_wg"], j).then_inc(L.s("g_ready"), 1)
        pe_pT(pe, m, L, i, "p_ready")
        pe_pv(pe, m, L, i, 32, v_mha(m))
        for j in range(2):
            pe.wait_ge(*L.after("s1_ready", 2 * i + j + 1))
            pe.matmul(m.bank(j, 0)[:, 0:16], m.blk[:, :], m.s1[:, j, :], start=True, stop=True).then_inc(L.s("mean_ready"), 1)
        for j in range(2):
            pe.wait_ge(*L.after("s2_ready", 2 * i + j + 1))
            pe.matmul(m.bank(j, 0)[:, 32:48], m.blk[:, :], m.s1[:, j, :], start=True, stop=True).then_inc(L.s("gvar_ready"), 1)
        pe_oT(pe, m, L, i, "normed")
        pe_out(pe, m, L, i, w["l0_wo"], w["l0_bo"][0:1, :])


def l0_act(act, m, L):
    w = m.w
    act.wait_ge(m.s_w[0], 16 * m.n_w[0])
    act.activation(m.lng[:, :], m.gam[:, :], ACT.Ln).then_inc(L.s("lng_ready"), 1)
    act.wait_ge(*L.after("dist_ready", 8))
    act.activation(m.decay[:, :], m.decay[:, :], ACT.Exp).then_inc(L.s("decay_exp"), 1)
    with act.Fori(0, NT // 2) as i:
        act_xT(act, m, L, i)
        for j in range(2):
            act.wait_ge(*L.after("q_ready", 2 * i + j + 1))
            for h in range(2):
                act.activation(m.qT[:, j, h, :], m.proj(j)[:, h * P:(h + 1) * P], ACT.Identity,
                               bias=m.w["l0_bq"][:, h:h + 1]).then_inc(L.s("qT_part"), 1)
            for h in range(2):
                ins = act.activation(m.kT[:, j, h, :], m.proj(j)[:, D + h * P:D + (h + 1) * P], ACT.Identity,
                                     bias=m.w["l0_bk"][:, h:h + 1])
            ins.then_inc(L.s("kT_kept"), 1)
        for j in range(2):
            act.wait_ge(*L.after("v_ready", 2 * i + j + 1))
            act.copy(m.v[:, j, :], m.work(j)[:, 0:D]).then_inc(L.s("v_kept"), 1)
        for j in range(2):
            act.wait_ge(*L.after("g_ready", 2 * i + j + 1))
            for h in range(2):
                ins = act.activation(m.gT[:, j, h, :], m.proj(j)[:, h * P:(h + 1) * P], ACT.Identity,
                                     bias=m.w["l0_bg"][:, h:h + 1])
            ins.then_inc(L.s("g_kept"), 1)
        for j in range(2):
            act.wait_ge(*L.after("g_kept", 2 * i + j + 1))
            act.activation(m.gE[:, j], m.gT[:, j], ACT.Tanh, scale=0.5).then_inc(L.s("g_exp"), 1)
        act_pT(act, m, L, i)


def l0_dve(dve, m, L):
    w = m.w
    dve.wait_ge(*L.after("lng_ready", 1))
    for u in range(8):
        dve.tensor_scalar(m.decay[:, u * S:(u + 1) * S], m.dist[:, :], m.lng[:, u:u + 1], None, ALU.mult)\
           .then_inc(L.s("dist_ready"), 1)
    dve.wait_ge(*L.after("decay_exp", 1))
    dec = m.decay[:, :].rearrange("p (u k) -> p u k", k=S)
    dve.tensor_tensor(dec, dec, m.tril[:, :].unsqueeze(1).to_broadcast([P, 8, S]), ALU.mult).then_inc(L.s("decay_ready"), 1)
    dve.wait_ge(*L.after("decay_ready", 1))
    with dve.Fori(0, NT // 2) as i:
        for j in range(2):
            dve.wait_ge(*L.after("qT_part", (2 * i + j + 1) * 2))
            dve_qmask(dve, m, L, j, m.qT[:, j].rearrange("p h t -> p (h t)"), m.w["hmask_one"])
        for j in range(2):
            dve.wait_ge(*L.after("scores_ready", 2 * i + j + 1))
            for g in range(2):
                for f in range(2):
                    sc = m.bank(j, g)[:, f * 256:(f + 1) * 256].rearrange("p (a b k) -> p a b k", a=2, b=2)
                    u = f * 4 + g * 2
                    pr = m.pr[:, j, u * P:(u + 2) * P].rearrange("p (a b k) -> p a b k", a=2, b=2)
                    dm = m.decay[:, u * S:(u + 2) * S].rearrange("p (a k) -> p a k", a=2).unsqueeze(2).to_broadcast([P, 2, 2, S])
                    ins = dve.tensor_tensor(pr, sc, dm, ALU.mult)
            ins.then_inc(L.s("p_ready"), 1)
        for j in range(2):
            dve.wait_ge(*L.after("g_exp", 2 * i + j + 1))
            dve.scalar_tensor_tensor(m.gE[:, j], m.gE[:, j], 1.0, m.gT[:, j], ALU.add, ALU.mult).then_inc(L.s("gate_ready"), 1)
        dve_pT(dve, m, L, i)
        dve_o(dve, m, L, i, False, scaled=False)
        for j in range(2):
            dve.wait_ge(*L.after("o_kept", 2 * i + j + 1))
            o3 = m.o[:, j, :].rearrange("p (r d) -> p r d", d=HD)
            dve.tensor_reduce(m.s1[:, j, :], o3, AX.X, ALU.add).then_inc(L.s("s1_ready"), 1)
        for j in range(2):
            dve.wait_ge(*L.after("mean_ready", 2 * i + j + 1))
            o3 = m.o[:, j, :].rearrange("p (r d) -> p r d", d=HD)
            dve.tensor_tensor(o3, o3, m.bank(j, 0)[:, 0:16].unsqueeze(2).to_broadcast([P, 16, HD]), ALU.subtract)\
               .then_inc(L.s("centred"), 1)
        for j in range(2):
            dve.wait_ge(*L.after("centred", 2 * i + j + 1))
            dve.tensor_tensor(m.o2[:, j, :], m.o[:, j, :], m.o[:, j, :], ALU.mult).then_inc(L.s("sq_ready"), 1)
        for j in range(2):
            dve.wait_ge(*L.after("sq_ready", 2 * i + j + 1))
            dve.tensor_reduce(m.s1[:, j, :], m.o2[:, j, :].rearrange("p (r d) -> p r d", d=HD), AX.X, ALU.add)\
               .then_inc(L.s("s2_ready"), 1)
        for j in range(2):
            dve.wait_ge(*L.after("gvar_ready", 2 * i + j + 1))
            dve.tensor_scalar(m.sums[:, j, :], m.bank(j, 0)[:, 32:48], LN_EPS, None, ALU.add).then_inc(L.s("gvar_kept"), 1)
        for j in range(2):
            dve.wait_ge(*L.after("grstd_ready", 2 * i + j + 1))
            o3 = m.o[:, j, :].rearrange("p (r d) -> p r d", d=HD)
            dve.tensor_tensor(o3, o3, m.rinv[:, j, :].unsqueeze(2).to_broadcast([P, 16, HD]), ALU.mult)\
               .then_inc(L.s("normed"), 1)
        for j in range(2):
            dve.wait_ge(*L.after("oT_ready", 2 * i + j + 1))
            src = m.bank(j, 1)[:, 0:D].rearrange("p (b e q) -> p b e q", b=2, e=2)
            dst = m.o2[:, j, :].rearrange("p (b e q) -> p b e q", b=2, e=2)
            for e in range(2):
                ins = dve.tensor_scalar(dst[:, :, e], src[:, :, e], w["l0_gnw"][:, e:e + 1], w["l0_gnb"][:, e:e + 1],
                                        ALU.mult, ALU.add)
            ins.then_inc(L.s("affine_ready"), 1)
        for j in range(2):
            dve.wait_ge(*L.after("affine_ready", 2 * i + j + 1))
            dve.wait_ge(*L.after("gate_ready", 2 * i + j + 1))
            a = m.o2[:, j, :].rearrange("p (b e q) -> p b e q", b=2, e=2)
            gt = m.gE[:, j].rearrange("p e (b q) -> p b e q", b=2)
            dst = m.oT[:, j, :].rearrange("p (b e q) -> p b e q", b=2, e=2)
            for e in range(2):
                ins = dve.scalar_tensor_tensor(dst[:, :, e], a[:, :, e], 0.5, gt[:, :, e], ALU.mult, ALU.mult)
            ins.then_inc(L.s("oT_kept"), 1)
        dve_residual_norm(dve, m, L, i, "y_ready", lambda j: m.work(j)[:, 0:D])


def l0_pool(pool, m, L):
    with pool.Fori(0, NT // 2) as i:
        for j in range(2):
            pool_copy_x(pool, m, L, 2 * i + j, j)
        for j in range(2):
            pool.wait_ge(*L.after("gvar_kept", 2 * i + j + 1))
            pool.tensor_tensor(m.rinv[:, j, :], m.sums[:, j, :], m.mhalf[:, 0:16], ALU.pow).then_inc(L.s("grstd_ready"), 1)
        for j in range(2):
            pool_rstd(pool, m, L, 2 * i + j, j)




def l1_names():
    n = per_tile(*CORE, *SOFTMAX, "scores_kept", "xss_ready", "ms_ready", "rms_ready", "qn_ready", "sin_part",
                 "qk_roped", "qkT_ready")
    n.update({"ctx_loaded0": 8 * NT, "ctx_loaded1": 8 * NT})
    return n


def ctx_after(L, i, j):
    return L.after("ctx_loaded%d" % j, 16 * (i + 1))


def l1_sync(sp, m, L):
    with sp.Fori(0, NT // 2) as i:
        for j in range(2):
            T = 2 * i + j
            sp.wait_ge(*L.after("x_written", T - 1))
            sp.dma_start(m.cb[:, j, :], m.ctx_tiles[T]).then_inc(L.s("ctx_loaded%d" % j), 16)


def l1_pe(pe, m, L):
    pe.wait_ge(m.s_w[1], 16 * m.n_w[1])
    with pe.Fori(0, NT // 2) as i:
        for j in range(2):
            pe.wait_ge(*L.after("qk_roped", 2 * i + j + 1))
            for c in range(4):
                ins = pe.transpose(m.proj(j)[:, c * P:(c + 1) * P], m.qk[:, j, c * P:(c + 1) * P], m.ident[:])
            ins.then_inc(L.s("qkT_ready"), 1)
        pe_scores(pe, m, L, i)
        pe_pT(pe, m, L, i)
        pe_pv(pe, m, L, i, HD, lambda rows, j, u: m.cb[rows, j, (u // 2) * HD:(u // 2 + 1) * HD])
        pe_oT(pe, m, L, i)
        pe_out(pe, m, L, i, m.w["l1_wo"])


def l1_act(act, m, L):
    with act.Fori(0, NT // 2) as i:
        for j in range(2):
            T = 2 * i + j
            act.wait_ge(*L.after("x_copied", T + 1))
            act.activation(m.o2[:, j, :], m.xc[:, j, :], ACT.Square, accum_out=m.stat[:, j, 4:5]).then_inc(L.s("xss_ready"), 1)
            act.wait_ge(*ctx_after(L, i, j))
            act.activation(m.r[:, j, 0:DC], m.cb[:, j, :], ACT.Square, accum_out=m.stat[:, j, 5:6]).then_inc(L.s("v_kept"), 1)
        for j in range(2):
            act.wait_ge(*L.after("qkT_ready", 2 * i + j + 1))
            act.copy(m.kT[:, j], m.proj(j)[:, D:2 * D].rearrange("p (h t) -> p h t", h=2)).then_inc(L.s("kT_kept"), 1)
        act_exp(act, m, L, i)
        act_pT(act, m, L, i)
        act_oT(act, m, L, i)


def l1_dve(dve, m, L):
    w = m.w
    dve.wait_ge(m.s_w[1], 16 * m.n_w[1])
    with dve.Fori(0, NT // 2) as i:
        for j in range(2):
            dve.wait_ge(*L.after("xss_ready", 2 * i + j + 1))
            dve.wait_ge(*L.after("v_kept", 2 * i + j + 1))
            dve.tensor_scalar(m.stat[:, j, 6:7], m.stat[:, j, 4:5], 1.0 / D, 1e-5, ALU.mult, ALU.add)
            dve.tensor_scalar(m.stat[:, j, 7:8], m.stat[:, j, 5:6], 1.0 / DC, 1e-5, ALU.mult, ALU.add).then_inc(L.s("ms_ready"), 1)
        for j in range(2):
            dve.wait_ge(*L.after("rms_ready", 2 * i + j + 1))
            dve.scalar_tensor_tensor(m.qn[:, j, 0:D], m.xc[:, j, :], m.stat[:, j, 8:9], w["l1_qw"][:, :], ALU.mult, ALU.mult)
            dve.scalar_tensor_tensor(m.qn[:, j, D:D + DC], m.cb[:, j, :], m.stat[:, j, 9:10], w["l1_kw"][:, :],
                                     ALU.mult, ALU.mult).then_inc(L.s("qn_ready"), 1)
        for j in range(2):
            dve.wait_ge(*L.after("qn_ready", 2 * i + j + 1))
            q3 = m.qn[:, j, :].rearrange("p (h d) -> p h d", d=HD)
            t1 = m.qt1[:, j, :].rearrange("p (h d) -> p h d", d=HD)
            t2 = m.qt2[:, j, :].rearrange("p (h d) -> p h d", d=HD)
            dve.tensor_tensor(t1, q3, w["l1_cos"][:, :].unsqueeze(1).to_broadcast([P, 20, HD]), ALU.mult)
            for half in range(2):
                ins = dve.tensor_tensor(t2[:, :, 8 * half:8 * half + 8], q3[:, :, 8 - 8 * half:16 - 8 * half],
                                        w["l1_sin"][:, 8 * half:8 * half + 8].unsqueeze(1).to_broadcast([P, 20, 8]), ALU.mult)
            ins.then_inc(L.s("sin_part"), 1)
        for j in range(2):
            dve.wait_ge(*L.after("sin_part", 2 * i + j + 1))
            dve.tensor_tensor(m.qk[:, j, 0:D], m.qt1[:, j, 0:D], m.qt2[:, j, 0:D], ALU.add)
            a, c = (t[:, j, D:D + DC].rearrange("p (v d) -> p v d", d=HD).unsqueeze(2).to_broadcast([P, 4, 4, HD])
                    for t in (m.qt1, m.qt2))
            dve.tensor_tensor(m.qk[:, j, D:2 * D].rearrange("p (v g d) -> p v g d", v=4, g=4), a, c, ALU.add)\
               .then_inc(L.s("qk_roped"), 1)
        for j in range(2):
            dve.wait_ge(*L.after("kT_kept", 2 * i + j + 1))
            dve_qmask(dve, m, L, j, m.proj(j)[:, 0:D], w["hmask_q"])
        dve_softmax(dve, m, L, i, True)
        dve_sums(dve, m, L, i)
        dve_pT(dve, m, L, i)
        dve_o(dve, m, L, i, True)
        dve_residual_norm(dve, m, L, i, "y_ready", lambda j: m.work(j)[:, 0:D])


def l1_pool(pool, m, L):
    with pool.Fori(0, NT // 2) as i:
        for j in range(2):
            pool_copy_x(pool, m, L, 2 * i + j, j)
        for j in range(2):
            pool.wait_ge(*L.after("ms_ready", 2 * i + j + 1))
            pool.tensor_tensor(m.stat[:, j, 8:10], m.stat[:, j, 6:8], m.mhalf[:, 0:2], ALU.pow).then_inc(L.s("rms_ready"), 1)
        for j in range(2):
            pool_rstd(pool, m, L, 2 * i + j, j)



def l3_names():
    n = per_tile(*CORE, *SOFTMAX, "xT_ready", "xT_kept", "q_ready", "v_ready", "p_ready", "rope_parts", "qT_kept",
                 "neg_ready", "negexp_ready", "feat_ready", "qf_ready", "lin_ready", "lsum_ready", "linv_ready",
                 "coef_ready", "soft_part", "lin_part")
    n.update({"gate_exp": 1, "gate_one": 1, "gate_sig": 1, "gate_rest": 1})
    return n


def l3_pe(pe, m, L):
    w = m.w
    pe.wait_ge(m.s_w[3], 16 * m.n_w[3])
    with pe.Fori(0, NT // 2) as i:
        pe_xT(pe, m, L, i)
        for j in range(2):
            pe.wait_ge(*L.after("xT_kept", 2 * i + j + 1))
            pe_projT(pe, m, m.proj(j)[:, 0:D], w["l3_wq"], j)
            pe_projT(pe, m, m.proj(j)[:, D:2 * D], w["l3_wk"], j).then_inc(L.s("q_ready"), 1)
            pe_proj(pe, m, m.work(j)[:, 0:D], w["l3_wv"], j).then_inc(L.s("v_ready"), 1)
        pe_scores(pe, m, L, i)
        for j in range(2):
            T = 2 * i + j
            pe.wait_ge(*L.after("qf_ready", T + 1))
            pe.wait_ge(*L.after("v_kept", T + 1))
            for half in range(2):
                for g in range(2):
                    rows = slice(64 * g, 64 * g + 64)
                    for p2 in range(2):
                        for b in range(2):
                            at = ((half * 2 + p2) * 2 + b) * S
                            ins = pe.matmul(m.bank(j, 2 + g)[:, at:at + S],
                                            m.qf[rows, j, half, b, 2 * p2:2 * p2 + 2, :].rearrange("p e s -> p (e s)"),
                                            m.ft[rows, j, D + half * P + b * S:D + half * P + (b + 1) * S],
                                            start=True, stop=True)
            ins.then_inc(L.s("lin_ready"), 1)
        pe_pT(pe, m, L, i, "p_ready")
        pe_pv(pe, m, L, i, 32, v_mha(m))
        pe_oT(pe, m, L, i)
        pe_out(pe, m, L, i, w["l3_wo"])


def l3_act(act, m, L):
    act.wait_ge(m.s_w[3], 16 * m.n_w[3])
    act.activation(m.gsig[:, :], m.w["l3_gate"][:, :], ACT.Exp, scale=-1.0).then_inc(L.s("gate_exp"), 1)
    with act.Fori(0, NT // 2) as i:
        act_xT(act, m, L, i)
        for j in range(2):
            act.wait_ge(*L.after("v_ready", 2 * i + j + 1))
            act.copy(m.v[:, j, :], m.work(j)[:, 0:D]).then_inc(L.s("v_kept"), 1)
        for j in range(2):
            act.wait_ge(*L.after("neg_ready", 2 * i + j + 1))
            act.activation(m.ft[:, j, :], m.ft[:, j, :], ACT.Exp).then_inc(L.s("negexp_ready"), 1)
        act_exp(act, m, L, i)
        act_pT(act, m, L, i)
        act_oT(act, m, L, i)


def l3_dve(dve, m, L):
    w = m.w
    dve.wait_ge(m.s_w[3], 16 * m.n_w[3])
    dve.wait_ge(*L.after("gate_exp", 1))
    dve.tensor_scalar(m.gsig[:, :], m.gsig[:, :], 1.0, None, ALU.add).then_inc(L.s("gate_one"), 1)
    dve.wait_ge(*L.after("gate_one", 1))
    dve.reciprocal(m.gsig[:, :], m.gsig[:, :]).then_inc(L.s("gate_sig"), 1)
    dve.wait_ge(*L.after("gate_sig", 1))
    dve.tensor_scalar(m.grest[:, :], m.gsig[:, :], -1.0, 1.0, ALU.mult, ALU.add).then_inc(L.s("gate_rest"), 1)
    dve.wait_ge(*L.after("gate_rest", 1))
    with dve.Fori(0, NT // 2) as i:
        for j in range(2):
            dve.wait_ge(*L.after("q_ready", 2 * i + j + 1))
            src = m.proj(j)[:, :].rearrange("p (x h b s) -> p x h b s", x=2, h=2, b=2)
            dve.tensor_tensor(m.rt1[:, j, :].rearrange("p (a s) -> p a s", s=S), m.proj(j)[:, :].rearrange("p (a s) -> p a s", s=S),
                              w["l3_cos"][:, :].unsqueeze(1).to_broadcast([P, 8, S]), ALU.mult)
            dst = m.rt2[:, j, :].rearrange("p (x h b s) -> p x h b s", x=2, h=2, b=2)
            for half in range(2):
                for x in range(2):
                    ins = dve.tensor_tensor(dst[:, x, half], src[:, x, 1 - half],
                                            w["l3_sin"][:, half * S:(half + 1) * S].unsqueeze(1).to_broadcast([P, 2, S]), ALU.mult)
            ins.then_inc(L.s("rope_parts"), 1)
        for j in range(2):
            dve.wait_ge(*L.after("rope_parts", 2 * i + j + 1))
            dve.tensor_tensor(m.qT[:, j].rearrange("p h t -> p (h t)"), m.rt1[:, j, 0:D], m.rt2[:, j, 0:D], ALU.add)\
               .then_inc(L.s("qT_kept"), 1)
            dve.tensor_tensor(m.kT[:, j].rearrange("p h t -> p (h t)"), m.rt1[:, j, D:2 * D], m.rt2[:, j, D:2 * D], ALU.add)\
               .then_inc(L.s("kT_kept"), 1)
        for j in range(2):
            dve.wait_ge(*L.after("kT_kept", 2 * i + j + 1))
            dve.tensor_scalar(m.ft[:, j, 0:D], m.qT[:, j].rearrange("p h t -> p (h t)"), 0.0, None, ALU.min)
            dve.tensor_scalar(m.ft[:, j, D:2 * D], m.kT[:, j].rearrange("p h t -> p (h t)"), 0.0, None, ALU.min)\
               .then_inc(L.s("neg_ready"), 1)
            dve_qmask(dve, m, L, j, m.qT[:, j].rearrange("p h t -> p (h t)"), w["hmask_q"])
        for j in range(2):
            dve.wait_ge(*L.after("negexp_ready", 2 * i + j + 1))
            dve.scalar_tensor_tensor(m.ft[:, j, 0:D], m.qT[:, j].rearrange("p h t -> p (h t)"), 0.0, m.ft[:, j, 0:D], ALU.max, ALU.add)
            dve.scalar_tensor_tensor(m.ft[:, j, D:2 * D], m.kT[:, j].rearrange("p h t -> p (h t)"), 0.0, m.ft[:, j, D:2 * D],
                                     ALU.max, ALU.add).then_inc(L.s("feat_ready"), 1)
        for j in range(2):
            dve.wait_ge(*L.after("feat_ready", 2 * i + j + 1))
            dve_qmask(dve, m, L, j, m.ft[:, j, 0:D], w["hmask_one"], m.qf, "qf_ready")
        dve_softmax(dve, m, L, i, False)
        for j in range(2):
            dve.wait_ge(*L.after("lin_ready", 2 * i + j + 1))
            for g in range(2):
                ins = dve.tensor_reduce(m.lsum[:, j, :].rearrange("p (f g r) -> p f g r", f=2, g=2)[:, :, g],
                                        m.bank(j, 2 + g)[:, :].rearrange("p (f r k) -> p f r k", f=2, r=4), AX.X, ALU.add)
            ins.then_inc(L.s("lsum_ready"), 1)
        for j in range(2):
            dve.wait_ge(*L.after("lsum_ready", 2 * i + j + 1))
            dve.reciprocal(m.linv[:, j, :], m.lsum[:, j, :]).then_inc(L.s("linv_ready"), 1)
        dve_sums(dve, m, L, i)
        for j in range(2):
            dve.wait_ge(*L.after("linv_ready", 2 * i + j + 1))
            dve.wait_ge(*L.after("rinv_ready", 2 * i + j + 1))
            dve.tensor_tensor(m.linv[:, j, :], m.linv[:, j, :], m.gsig[:, :], ALU.mult)
            dve.tensor_tensor(m.rinv[:, j, :], m.rinv[:, j, :], m.grest[:, :], ALU.mult).then_inc(L.s("coef_ready"), 1)
        for j in range(2):
            dve.wait_ge(*L.after("coef_ready", 2 * i + j + 1))
            pr = m.pr[:, j, :].rearrange("p (r k) -> p r k", k=S)
            dve.tensor_tensor(pr, pr, m.rinv[:, j, :].unsqueeze(2).to_broadcast([P, 16, S]), ALU.mult).then_inc(L.s("soft_part"), 1)
            for g in range(2):
                ins = dve.tensor_tensor(m.pr2[:, j, :].rearrange("p (f g r k) -> p f g r k", f=2, g=2, r=4)[:, :, g],
                                        m.bank(j, 2 + g)[:, :].rearrange("p (f r k) -> p f r k", f=2, r=4),
                                        m.linv[:, j, :].rearrange("p (f g r) -> p f g r", f=2, g=2)[:, :, g].unsqueeze(3)
                                        .to_broadcast([P, 2, 4, S]), ALU.mult)
            ins.then_inc(L.s("lin_part"), 1)
        for j in range(2):
            dve.wait_ge(*L.after("lin_part", 2 * i + j + 1))
            dve.wait_ge(*L.after("soft_part", 2 * i + j + 1))
            dve.tensor_tensor(m.pr[:, j, :], m.pr[:, j, :], m.pr2[:, j, :], ALU.add).then_inc(L.s("p_ready"), 1)
        dve_pT(dve, m, L, i)
        dve_o(dve, m, L, i, False, scaled=False)
        dve_residual_norm(dve, m, L, i, "y_ready", lambda j: m.work(j)[:, 0:D])


def plain_pool(pool, m, L):
    with pool.Fori(0, NT // 2) as i:
        for j in range(2):
            pool_copy_x(pool, m, L, 2 * i + j, j)
        for j in range(2):
            pool_rstd(pool, m, L, 2 * i + j, j)



def l4_names():
    n = per_tile(*CORE, *SOFTMAX, "scores_kept", "xT_ready", "xT_kept", "q_ready", "v_ready")
    n.update({"ctx_loaded0": 8 * NT, "ctx_loaded1": 8 * NT})
    return n


def l4_sync(sp, m, L):
    with sp.Fori(0, NT // 2) as i:
        for j in range(2):
            T = 2 * i + j
            sp.wait_ge(*L.after("x_written", T - 1))
            sp.dma_start(m.ctxT[:, j, :], m.ctxT_d[:, bass.ds(T * P, P)]).then_inc(L.s("ctx_loaded%d" % j), 16)


def l4_pe(pe, m, L):
    w = m.w
    pe.wait_ge(m.s_w[4], 16 * m.n_w[4])
    with pe.Fori(0, NT // 2) as i:
        pe_xT(pe, m, L, i)
        for j in range(2):
            pe.wait_ge(*L.after("xT_kept", 2 * i + j + 1))
            pe_projT(pe, m, m.proj(j)[:, 0:D], w["l4_wq"], j)
            pe.wait_ge(*ctx_after(L, i, j))
            for h in range(2):
                ins = pe.matmul(m.proj(j)[:, D + h * P:D + (h + 1) * P], w["l4_wkv"][:, h * P:(h + 1) * P], m.ctxT[:, j, :],
                                start=True, stop=True)
            ins.then_inc(L.s("q_ready"), 1)
            pe.matmul(m.work(j)[:, 0:D], m.ctxT[:, j, :], w["l4_wkv"][:, D:2 * D], start=True, stop=True).then_inc(L.s("v_ready"), 1)
        pe_scores(pe, m, L, i)
        pe_pT(pe, m, L, i)
        pe_pv(pe, m, L, i, 32, v_mha(m))
        pe_oT(pe, m, L, i)
        pe_out(pe, m, L, i, w["l4_wo"])


def l4_act(act, m, L):
    with act.Fori(0, NT // 2) as i:
        act_xT(act, m, L, i)
        for j in range(2):
            act.wait_ge(*L.after("q_ready", 2 * i + j + 1))
            act.copy(m.kT[:, j], m.proj(j)[:, D:2 * D].rearrange("p (h t) -> p h t", h=2)).then_inc(L.s("kT_kept"), 1)
        for j in range(2):
            act.wait_ge(*L.after("v_ready", 2 * i + j + 1))
            act.copy(m.v[:, j, :], m.work(j)[:, 0:D]).then_inc(L.s("v_kept"), 1)
        act_exp(act, m, L, i)
        act_pT(act, m, L, i)
        act_oT(act, m, L, i)


def l4_dve(dve, m, L):
    with dve.Fori(0, NT // 2) as i:
        for j in range(2):
            dve.wait_ge(*L.after("kT_kept", 2 * i + j + 1))
            dve_qmask(dve, m, L, j, m.proj(j)[:, 0:D], m.w["hmask_q"])
        dve_softmax(dve, m, L, i, True)
        dve_sums(dve, m, L, i)
        dve_pT(dve, m, L, i)
        dve_o(dve, m, L, i, False)
        dve_residual_norm(dve, m, L, i, "y_ready", lambda j: m.work(j)[:, 0:D])



def l5_names():
    n = per_tile(*TILE, "xT_ready", "xT_kept", "y_ready")
    n.update({"abs_ready": 2, "abs_sum": 2, "thr_ready": 2, "nthr_ready": 2, "above_ready": 2, "below_ready": 2,
              "tern_ready": 2, "off_ready": 2, "ternw_ready": 2, "ternT_ready": 1, "ternT_kept": 1})
    return n


def l5_pe(pe, m, L):
    pe.wait_ge(*L.after("ternw_ready", 2))
    pe.wait_ge(*L.after("x_written", 0))
    for k in range(2):
        for h in range(2):
            ins = pe.transpose(m.bank(0, 0)[:, (k * 2 + h) * P:(k * 2 + h + 1) * P], m.tern[:, h, k * P:(k + 1) * P], m.ident[:])
    ins.then_inc(L.s("ternT_ready"), 1)
    pe.wait_ge(*L.after("ternT_kept", 1))
    with pe.Fori(0, NT // 2) as i:
        pe_xT(pe, m, L, i)
        for j in range(2):
            pe.wait_ge(*L.after("xT_kept", 2 * i + j + 1))
            pe_proj(pe, m, m.proj(j)[:, 0:D], m.ternT, j, m.w["l5_b"][0:1, :]).then_inc(L.s("y_ready"), 1)


def l5_act(act, m, L):
    act.wait_ge(*L.after("ternT_ready", 1))
    act.copy(m.ternT[:, :, :], m.bank(0, 0)[:, :].rearrange("p (k o) -> p k o", k=2)).then_inc(L.s("ternT_kept"), 1)
    with act.Fori(0, NT // 2) as i:
        act_xT(act, m, L, i)


def l5_dve(dve, m, L):
    w = m.w["l5_w"]
    dve.wait_ge(m.s_w[5], 16 * m.n_w[5])
    for h in range(2):
        dve.scalar_tensor_tensor(m.ta[:, h, :], w[:, h, :], -1.0, w[:, h, :], ALU.mult, ALU.max).then_inc(L.s("abs_ready"), 1)
    for h in range(2):
        dve.wait_ge(*L.after("abs_ready", h + 1))
        dve.tensor_reduce(m.tstat[:, h, 0:1], m.ta[:, h, :], AX.X, ALU.add).then_inc(L.s("abs_sum"), 1)
    for h in range(2):
        dve.wait_ge(*L.after("abs_sum", h + 1))
        dve.tensor_scalar(m.tstat[:, h, 1:2], m.tstat[:, h, 0:1], 1.0 / D, 0.7, ALU.mult, ALU.mult).then_inc(L.s("thr_ready"), 1)
    for h in range(2):
        dve.wait_ge(*L.after("thr_ready", h + 1))
        dve.tensor_scalar(m.tstat[:, h, 2:3], m.tstat[:, h, 1:2], -1.0, None, ALU.mult).then_inc(L.s("nthr_ready"), 1)
        dve.tensor_scalar(m.ta[:, h, :], w[:, h, :], m.tstat[:, h, 1:2], None, ALU.is_gt).then_inc(L.s("above_ready"), 1)
    for h in range(2):
        dve.wait_ge(*L.after("nthr_ready", h + 1))
        dve.tensor_scalar(m.tb[:, h, :], w[:, h, :], m.tstat[:, h, 2:3], None, ALU.is_lt).then_inc(L.s("below_ready"), 1)
    for h in range(2):
        dve.wait_ge(*L.after("below_ready", h + 1))
        dve.wait_ge(*L.after("above_ready", h + 1))
        dve.tensor_tensor(m.ta[:, h, :], m.ta[:, h, :], m.tb[:, h, :], ALU.subtract).then_inc(L.s("tern_ready"), 1)
    for h in range(2):
        dve.wait_ge(*L.after("tern_ready", h + 1))
        dve.tensor_tensor(m.ta[:, h, :], m.ta[:, h, :], w[:, h, :], ALU.subtract).then_inc(L.s("off_ready"), 1)
    for h in range(2):
        dve.wait_ge(*L.after("off_ready", h + 1))
        dve.tensor_tensor(m.tern[:, h, :], m.ta[:, h, :], w[:, h, :], ALU.add).then_inc(L.s("ternw_ready"), 1)
    with dve.Fori(0, NT // 2) as i:
        dve_residual_norm(dve, m, L, i, "y_ready", lambda j: m.proj(j)[:, 0:D])



def l9_names():
    return per_tile(*CORE, *SOFTMAX, "xT_ready", "xT_kept", "q_ready", "k_ready", "v_ready", "rope_parts",
                    "krope_parts", "qT_kept")


def l9_pe(pe, m, L):
    w = m.w
    pe.wait_ge(m.s_w[9], 16 * m.n_w[9])
    with pe.Fori(0, NT // 2) as i:
        pe_xT(pe, m, L, i)
        for j in range(2):
            pe.wait_ge(*L.after("xT_kept", 2 * i + j + 1))
            pe_projT(pe, m, m.proj(j)[:, 0:D], w["l9_wq"], j)
            pe_projT(pe, m, m.proj(j)[:, D:2 * D], w["l9_wqp"], j).then_inc(L.s("q_ready"), 1)
            pe_projT(pe, m, m.bank(j, 0)[:, 0:D], w["l9_wk"], j)
            pe_projT(pe, m, m.bank(j, 0)[:, D:2 * D], w["l9_wkp"], j).then_inc(L.s("k_ready"), 1)
            pe_proj(pe, m, m.work(j)[:, 0:D], w["l9_wv"], j, w["l9_bv"][0:1, :]).then_inc(L.s("v_ready"), 1)
        pe_scores(pe, m, L, i)
        pe_pT(pe, m, L, i)
        pe_pv(pe, m, L, i, 32, v_mha(m))
        pe_oT(pe, m, L, i)
        pe_out(pe, m, L, i, w["l9_wo"], w["l9_bo"][0:1, :])


def l9_act(act, m, L):
    with act.Fori(0, NT // 2) as i:
        act_xT(act, m, L, i)
        for j in range(2):
            act.wait_ge(*L.after("v_ready", 2 * i + j + 1))
            act.copy(m.v[:, j, :], m.work(j)[:, 0:D]).then_inc(L.s("v_kept"), 1)
        act_exp(act, m, L, i)
        act_pT(act, m, L, i)
        act_oT(act, m, L, i)


def l9_dve(dve, m, L):
    w = m.w
    dve.wait_ge(m.s_w[9], 16 * m.n_w[9])
    with dve.Fori(0, NT // 2) as i:
        for name, ready, bias, bank, t in (("rope_parts", "q_ready", "l9_bq", lambda j: m.proj(j), m.rt1),
                                           ("krope_parts", "k_ready", "l9_bk", lambda j: m.bank(j, 0), m.rt2)):
            for j in range(2):
                dve.wait_ge(*L.after(ready, 2 * i + j + 1))
                for c in range(4):
                    tab = w["l9_cos"] if c < 2 else w["l9_sin"]
                    ins = dve.scalar_tensor_tensor(
                        t[:, j, c * P:(c + 1) * P].rearrange("p (b s) -> p b s", b=2),
                        bank(j)[:, c * P:(c + 1) * P].rearrange("p (b s) -> p b s", b=2), w[bias][:, c:c + 1],
                        tab[:, :].unsqueeze(1).to_broadcast([P, 2, S]), ALU.add, ALU.mult)
                ins.then_inc(L.s(name), 1)
        for j in range(2):
            dve.wait_ge(*L.after("rope_parts", 2 * i + j + 1))
            dve.tensor_tensor(m.qT[:, j].rearrange("p h t -> p (h t)"), m.rt1[:, j, 0:D], m.rt1[:, j, D:2 * D], ALU.add)\
               .then_inc(L.s("qT_kept"), 1)
            dve.wait_ge(*L.after("krope_parts", 2 * i + j + 1))
            dve.tensor_tensor(m.kT[:, j].rearrange("p h t -> p (h t)"), m.rt2[:, j, 0:D], m.rt2[:, j, D:2 * D], ALU.add)\
               .then_inc(L.s("kT_kept"), 1)
        for j in range(2):
            dve.wait_ge(*L.after("qT_kept", 2 * i + j + 1))
            dve_qmask(dve, m, L, j, m.qT[:, j].rearrange("p h t -> p (h t)"), w["hmask_q"])
        dve_softmax(dve, m, L, i, False)
        dve_sums(dve, m, L, i)
        dve_pT(dve, m, L, i)
        dve_o(dve, m, L, i, False)
        dve_residual_norm(dve, m, L, i, "y_ready", lambda j: m.work(j)[:, 0:D])



E2, K2, F2, C2 = 64, 8, 96, 32
SLOTS = E2 * C2
NS = SLOTS // P


def l2_names():
    n = per_tile(*TILE)
    n.update({k: GROUPS for k in ("xs_copied", "xsT_ready", "xsT_kept", "logits_ready", "logits_kept")})
    n.update({k: NT for k in ("place_matrix", "slot_sums", "slot_x_kept", "slot_x_T", "slot_xT_kept", "hidden_ready",
                              "tanh_ready", "silu_ready", "h_kept", "slot_y_ready", "slot_y_kept", "back_matrix", "y_ready")})
    n.update({"expert_w0": 16 * NT, "expert_w1": 16 * NT, "x_in_dram": 16, "gathered": 16 * NS})
    n.update({"route_step": 20, "shifted": 1, "route_exp": 1, "prefix_ready": 1, "places_ready": 1,
              "slots_known": 1})
    return n


def l2_places(m, ar):
    group_places(m, ar)
    m.xc, m.r, m.bn, m.stat = ar.take([2, D]), ar.take([2, D]), ar.take([2, 6]), ar.take([2, 16])
    m.lg, m.sel, m.wt, m.top = ar.take([NT, E2]), ar.take([NT, E2]), ar.take([NT, E2]), ar.take([NT, 8])
    m.pre, m.pre2 = ar.take([NT + 1, E2]), ar.take([NT + 1, E2])
    m.tmp, m.posm = ar.take([NT, E2]), ar.take([NT, E2])
    m.rsum, m.rrec = ar.take([NT]), ar.take([NT])
    m.big = ar.take([2, SLOTS])
    m.rh = ar.take([NT, NS, 5])
    m.info, m.wsl4, m.wsl = ar.take([NS, 5]), ar.take([NS, 4]), ar.take([NS])
    m.tid, m.tidT = ar.take([NS]), ar.take([NT, NS])
    m.xg, m.yw = ar.take([NS, D]), ar.take([NS, D])
    m.sgT, m.th2, m.sg2, m.hT2 = ar.take([2, 2, P]), ar.take([2, P]), ar.take([2, P]), ar.take([2, P])


def l2_sync(sp, m, L):
    sp.dma_start(m.scratch["x_rows"].rearrange("(t p) d -> p t d", p=P), m.x[:, :, :]).then_inc(L.s("x_in_dram"), 16)
    for j in range(2):
        sp.dma_start(m.w["l2_ring"][:, j, 0:1536], m.dram["moe_w1v1"][j]).then_inc(L.s("expert_w%d" % j), 16)
        sp.dma_start(m.w["l2_ring"][0:F2, j, 1536:2560], m.dram["moe_w2"][j]).then_inc(L.s("expert_w%d" % j), 16)
    with sp.Fori(1, NS // 2) as i:
        for j in range(2):
            s = 2 * i + j
            sp.wait_ge(*L.after("slot_y_ready", s - 1))
            sp.dma_start(m.w["l2_ring"][:, j, 0:1536], m.dram["moe_w1v1"][bass.ds(s, 1)].rearrange("a p n -> (a p) n")).then_inc(L.s("expert_w%d" % j), 16)
            sp.dma_start(m.w["l2_ring"][0:F2, j, 1536:2560], m.dram["moe_w2"][bass.ds(s, 1)].rearrange("a p n -> (a p) n")).then_inc(L.s("expert_w%d" % j), 16)


def l2_pe(pe, m, L):
    w = m.w
    pe.wait_ge(m.s_w[2], 16 * m.n_w[2])
    with pe.Fori(0, GROUPS) as g:
        pe_group_T(pe, m, L, g, [m.flat(0), m.flat(1)])
        pe.wait_ge(*L.after("xsT_kept", g + 1))
        for q in range(4):
            for k in range(2):
                ins = pe.matmul(m.flat(2)[:, q * E2:(q + 1) * E2], m.xsT[:, k, q * P:(q + 1) * P], w["l2_rw"][:, k, :],
                                start=(k == 0), stop=(k == 1))
        ins.then_inc(L.s("logits_ready"), 1)
    pe.wait_ge(*L.after("prefix_ready", 1))
    for c in range(2):
        out = m.flat(3 + c)
        pe.matmul(out, w["l2_before"][:, :], m.pre2[:, NT:NT + 1, :].to_broadcast([P, 8, E2]), start=True, stop=False)
        pe.matmul(out, w["l2_same"][:, :], m.pre2[:, 8 * c:8 * c + 8, :], start=False, stop=False)
        ins = pe.matmul(out, w["l2_first_half"][:, :], m.sel[:, 8 * c:8 * c + 8, :], start=False, stop=True)
    ins.then_inc(L.s("places_ready"), 1)
    for T in range(NT):
        pe.wait_ge(*L.after("place_matrix", T + 1))
        for s in range(NS):
            ins = pe.matmul(m.flat(5)[:, s * 5:(s + 1) * 5], m.big[:, T % 2, s * P:(s + 1) * P], m.rh[:, T, s, :],
                            start=(T == 0 and s == 0), stop=(T == NT - 1), skip_group_check=True)
        ins.then_inc(L.s("slot_sums"), 1)
    with pe.Fori(0, NS // 2) as i:
        for j in range(2):
            pe.wait_ge(*L.after("slot_x_kept", 2 * i + j + 1))
            for h in range(2):
                ins = pe.transpose(m.bank(j, 0)[:, h * P:(h + 1) * P], m.xc[:, j, h * P:(h + 1) * P], m.ident[:])
            ins.then_inc(L.s("slot_x_T"), 1)
        for j in range(2):
            ring = m.w["l2_ring"][:, j, 0:1536].rearrange("p (e v k f) -> p e v k f", e=4, v=2, k=2)
            pe.wait_ge(*L.after("slot_xT_kept", 2 * i + j + 1))
            pe.wait_ge(*L.after("expert_w%d" % j, 32 * (i + 1)))
            for v in range(2):
                for e in range(4):
                    for k in range(2):
                        ins = pe.matmul(m.bank(j, 1)[0:F2, v * P + e * C2:v * P + (e + 1) * C2], ring[:, e, v, k, :],
                                        m.sgT[:, j, k, e * C2:(e + 1) * C2], start=(k == 0), stop=(k == 1))
            ins.then_inc(L.s("hidden_ready"), 1)
        for j in range(2):
            pe.wait_ge(*L.after("h_kept", 2 * i + j + 1))
            for e in range(4):
                ins = pe.matmul(m.bank(j, 2)[e * C2:(e + 1) * C2, 0:D], m.hT2[0:F2, j, e * C2:(e + 1) * C2],
                                m.w["l2_ring"][0:F2, j, 1536 + e * D:1536 + (e + 1) * D], start=True, stop=True)
            ins.then_inc(L.s("slot_y_ready"), 1)
    pe.wait_ge(*L.after("slot_y_kept", NS))
    with pe.Fori(0, NT // 2) as i:
        for j in range(2):
            pe.wait_ge(*L.after("back_matrix", 2 * i + j + 1))
            for s in range(NS):
                ins = pe.matmul(m.bank(j, 3)[:, 0:D], m.big[:, j, s * P:(s + 1) * P], m.yw[:, s, :],
                                start=(s == 0), stop=(s == NS - 1))
            ins.then_inc(L.s("y_ready"), 1)


def l2_act(act, m, L):
    with act.Fori(0, GROUPS) as g:
        act.copy(m.xs[:, :, :], m.x[:, bass.ds(4 * g, 4), :]).then_inc(L.s("xs_copied"), 1)
        act_group_T(act, m, L, g, [m.flat(0), m.flat(1)])
        act.wait_ge(*L.after("logits_ready", g + 1))
        act.copy(m.lg[:, bass.ds(4 * g, 4), :], m.flat(2)[:, 0:4 * E2].rearrange("p (q e) -> p q e", q=4))\
           .then_inc(L.s("logits_kept"), 1)
    act.wait_ge(*L.after("shifted", 1))
    act.activation(m.wt[:, :, :], m.wt[:, :, :], ACT.Exp).then_inc(L.s("route_exp"), 1)
    with act.Fori(0, NS // 2) as i:
        for j in range(2):
            s = 2 * i + j
            act.wait_ge(*L.after("gathered", 16 * NS))
            act.copy(m.xc[:, j, :], m.xg[:, s, :]).then_inc(L.s("slot_x_kept"), 1)
        for j in range(2):
            act.wait_ge(*L.after("slot_x_T", 2 * i + j + 1))
            act.copy(m.sgT[:, j], m.bank(j, 0)[:, 0:D].rearrange("p (h t) -> p h t", h=2)).then_inc(L.s("slot_xT_kept"), 1)
        for j in range(2):
            act.wait_ge(*L.after("hidden_ready", 2 * i + j + 1))
            act.activation(m.th2[0:F2, j, :], m.bank(j, 1)[0:F2, 0:P], ACT.Tanh, scale=0.5).then_inc(L.s("tanh_ready"), 1)


def l2_dve(dve, m, L):
    w = m.w
    done = [0]

    def then(ins):
        done[0] += 1
        ins.then_inc(L.s("route_step"), 1)
        dve.wait_ge(*L.after("route_step", done[0]))

    dve.wait_ge(m.s_w[2], 16 * m.n_w[2])
    dve.wait_ge(*L.after("logits_kept", GROUPS))
    for T in range(NT):
        ins = dve.max(m.top[:, T, :], m.lg[:, T, :])
    then(ins)
    for T in range(NT):
        ins = dve.match_replace(out=m.tmp[:, T, :], in_to_replace=m.top[:, T, :], in_values=m.lg[:, T, :], imm_value=-3e38)
    dve.tensor_tensor(m.wt[:, :, :], m.lg[:, :, :], m.top[:, :, 0:1].to_broadcast([P, NT, E2]), ALU.subtract)\
       .then_inc(L.s("shifted"), 1)
    then(dve.memset(m.pre[:, 0, :], 0.0))
    then(dve.tensor_tensor(m.sel[:, :, :], m.tmp[:, :, :], m.lg[:, :, :], ALU.not_equal))
    then(dve.tensor_copy(m.pre[:, 1:NT + 1, :], m.sel[:, :, :]))
    a, b = m.pre, m.pre2
    for shift in (1, 2, 4, 8):
        dve.tensor_copy(b[:, 0:shift, :], a[:, 0:shift, :])
        then(dve.tensor_tensor(b[:, shift:NT + 1, :], a[:, shift:NT + 1, :], a[:, 0:NT + 1 - shift, :], ALU.add))
        a, b = b, a
    then(dve.tensor_copy(m.pre2[:, :, :], m.pre[:, :, :]))
    dve.memset(m.pause[:, :], 0.0).then_inc(L.s("prefix_ready"), 1)
    dve.wait_ge(*L.after("route_exp", 1))
    then(dve.tensor_tensor(m.wt[:, :, :], m.wt[:, :, :], m.sel[:, :, :], ALU.mult))
    then(dve.tensor_reduce(m.rsum[:, :], m.wt[:, :, :], AX.X, ALU.add))
    then(dve.reciprocal(m.rrec[:, :], m.rsum[:, :]))
    then(dve.tensor_tensor(m.wt[:, :, :], m.wt[:, :, :], m.rrec[:, :].unsqueeze(2).to_broadcast([P, NT, E2]), ALU.mult))
    dve.tensor_copy(m.rh[:, :, :, 0], w["l2_token"][:, :].unsqueeze(2).to_broadcast([P, NT, NS]))
    then(dve.tensor_copy(m.rh[:, :, :, 1:5], m.wt[:, :, :].rearrange("p t (s e) -> p t s e", e=4)))
    dve.wait_ge(*L.after("places_ready", 1))
    for c in range(2):
        ins = dve.scalar_tensor_tensor(m.tmp[:, 8 * c:8 * c + 8, :].rearrange("p t e -> p (t e)"), m.flat(3 + c), 1.0,
                                       m.sel[:, 8 * c:8 * c + 8, :].rearrange("p t e -> p (t e)"), ALU.add, ALU.mult)
    then(ins)
    then(dve.tensor_scalar(m.posm[:, :, :], m.tmp[:, :, :], -1.0, None, ALU.add))
    for T in range(NT):
        if T >= 2:
            dve.wait_ge(*L.after("slot_sums", T - 1))
        dve.tensor_tensor(m.big[:, T % 2, :].rearrange("p (e c) -> p e c", c=C2),
                          m.posm[:, T, :].unsqueeze(2).to_broadcast([P, E2, C2]),
                          w["l2_iota"][:, 0:C2].unsqueeze(1).to_broadcast([P, E2, C2]), ALU.is_equal)\
           .then_inc(L.s("place_matrix"), 1)
    dve.wait_ge(*L.after("slot_sums", NT))
    then(dve.tensor_copy(m.info[:, :, :], m.flat(5)[:, 0:NS * 5].rearrange("p (s c) -> p s c", c=5)))
    then(dve.tensor_tensor(m.wsl4[:, :, :], m.info[:, :, 1:5], w["l2_own"][:, :].unsqueeze(1).to_broadcast([P, NS, 4]), ALU.mult))
    then(dve.tensor_reduce(m.wsl[:, :], m.wsl4[:, :, :], AX.X, ALU.add))
    then(dve.tensor_copy(m.tid[:, :].bitcast(mybir.dt.uint32), m.info[:, :, 0]))
    dve.tensor_tensor(m.tidT[:, :, :], m.info[:, :, 0].unsqueeze(1).to_broadcast([P, NT, NS]),
                      w["l2_tile_start"][:, :].unsqueeze(2).to_broadcast([P, NT, NS]), ALU.subtract).then_inc(L.s("slots_known"), 1)
    dve.wait_ge(*L.after("slots_known", 1))
    assert done[0] == 20, done
    with dve.Fori(0, NS // 2) as i:
        for j in range(2):
            dve.wait_ge(*L.after("tanh_ready", 2 * i + j + 1))
            dve.scalar_tensor_tensor(m.sg2[0:F2, j, :], m.th2[0:F2, j, :], 1.0, m.bank(j, 1)[0:F2, 0:P], ALU.add, ALU.mult)\
               .then_inc(L.s("silu_ready"), 1)
        for j in range(2):
            dve.wait_ge(*L.after("silu_ready", 2 * i + j + 1))
            dve.scalar_tensor_tensor(m.hT2[0:F2, j, :], m.sg2[0:F2, j, :], 0.5, m.bank(j, 1)[0:F2, P:2 * P], ALU.mult, ALU.mult)\
               .then_inc(L.s("h_kept"), 1)
        for j in range(2):
            s = 2 * i + j
            dve.wait_ge(*L.after("slot_y_ready", s + 1))
            dve.tensor_scalar(m.yw[:, s, :], m.bank(j, 2)[:, 0:D], m.wsl[:, bass.ds(s, 1)], None, ALU.mult)\
               .then_inc(L.s("slot_y_kept"), 1)
    with dve.Fori(0, NT // 2) as i:
        for j in range(2):
            T = 2 * i + j
            dve.wait_ge(*L.after("x_written", T - 1))
            dve.tensor_tensor(m.big[:, j, :].rearrange("p (s t) -> p s t", t=P),
                              m.tidT[:, T, :].unsqueeze(2).to_broadcast([P, NS, P]),
                              w["l2_iota"][:, :].unsqueeze(1).to_broadcast([P, NS, P]), ALU.is_equal)\
               .then_inc(L.s("back_matrix"), 1)
        dve.wait_ge(*L.after("x_copied", 2 * i + 2))
        dve_residual_norm(dve, m, L, i, "y_ready", lambda j: m.bank(j, 3)[:, 0:D])


def l2_pool(pool, m, L):
    pool.wait_ge(*L.after("slots_known", 1))
    pool.wait_ge(*L.after("x_in_dram", 16))
    for s in range(NS):
        pool.indirect_dma_start(m.xg[:, s, :], None, m.scratch["x_rows"],
                                bass.IndirectOffsetOnAxis(ap=m.tid[:, s:s + 1].bitcast(mybir.dt.uint32), axis=0))\
            .then_inc(L.s("gathered"), 16)
    with pool.Fori(0, NT // 2) as i:
        for j in range(2):
            T = 2 * i + j
            pool.wait_ge(*L.after("slot_y_kept", NS))
            pool_copy_x(pool, m, L, T, j)
        for j in range(2):
            pool_rstd(pool, m, L, 2 * i + j, j)



E11, F11 = 8, 352
C11 = TOK // E11
CHUNKS = ((0, 128), (128, 128), (256, 96))
NC = len(CHUNKS)


def l11_names():
    n = {k: NT for k in ("x_written", "r_kept", "stats_ready", "aggr_ready", "var_ready", "rstd_ready")}
    n.update({k: GROUPS for k in ("xs_copied", "xsT_ready", "xsT_kept", "logits_ready", "logits_kept", "shared_ready",
                                  "shared_kept")})
    n.update({k: GROUPS * NC + E11 * NC for k in ("gu_ready", "tanh_ready", "silu_ready", "h_kept")})
    n.update({k: E11 for k in ("slot_x_T", "slot_xT_kept", "slot_y_ready", "slot_y_kept")})
    for j in range(2):
        n.update({"slot_x%d" % j: 16 * E11 // 2, "slot_y_out%d" % j: 16 * E11 // 2, "expert_w%d" % j: 64 * E11 // 2})
    n.update({"zeros_ready": 1, "slots_zeroed": 16, "scattered": 16 * NT, "fetched": 16 * NT, "route_step": 17,
              "shifted": 1, "route_exp": 1, "prefix_ready": 1, "places_ready": 1, "slots_known": 1})
    return n


def l11_places(m, ar):
    group_places(m, ar)
    m.r, m.bn, m.stat = ar.take([2, D]), ar.take([2, 6]), ar.take([2, 16])
    m.th, m.sg, m.hT = ar.take([2, 512]), ar.take([2, 512]), ar.take([NC, 512])
    m.sh = ar.take([NT, D])
    m.og = ar.take([NT, D])
    m.lg, m.cand, m.oh, m.tmp = (ar.take([NT, E11]) for _ in range(4))
    m.pre, m.pre2 = ar.take([NT + 1, E11]), ar.take([NT + 1, E11])
    (m.mx, m.eidx, m.rsum, m.gate, m.place, m.keep, m.slot, m.a1, m.a2, m.idx_put, m.idx_get) = (
        ar.take([NT]) for _ in range(11))
    m.xd, m.xdT, m.ys = ar.take([2, 2, D]), ar.take([2, 2 * P]), ar.take([2, 2, D])
    m.zeros = ar.take([D])


def l11_sync(sp, m, L):
    sp.wait_ge(*L.after("zeros_ready", 1))
    xd = m.scratch["slot_x"]
    sp.dma_start(xd[0:TOK, :].rearrange("(t p) d -> p t d", p=P), m.zeros.unsqueeze(1).to_broadcast([P, NT, D]))\
      .then_inc(L.s("slots_zeroed"), 16)
    ring = m.w["l11_ring"]
    slots = xd[0:TOK, :].rearrange("(e h p) d -> e p h d", h=2, p=P)
    w1, w3, w2a, w2b = (m.dram["moe8_" + n] for n in ("w1", "w3", "w2a", "w2b"))

    def expert(ap, e):
        return ap[bass.ds(e, 1)].rearrange("a p n -> (a p) n")

    def weights(j, e):
        done = L.s("expert_w%d" % j)
        sp.dma_start(ring[:, j, 0:704], expert(w1, e)).then_inc(done, 16)
        sp.dma_start(ring[:, j, 704:1408], expert(w3, e)).then_inc(done, 16)
        sp.dma_start(ring[:, j, 1408:1920], expert(w2a, e)).then_inc(done, 16)
        sp.dma_start(ring[0:96, j, 1920:2176], expert(w2b, e)).then_inc(done, 16)

    def rows(j, e):
        sp.dma_start(m.xd[:, j], slots[bass.ds(e, 1)].rearrange("a p h d -> (a p) h d")).then_inc(L.s("slot_x%d" % j), 16)

    for j in range(2):
        weights(j, j)
    sp.wait_ge(*L.after("scattered", 16 * NT))
    for j in range(2):
        rows(j, j)
    with sp.Fori(1, E11 // 2) as i:
        for j in range(2):
            sp.wait_ge(*L.after("slot_y_ready", 2 * i + j - 1))
            weights(j, 2 * i + j)
            rows(j, 2 * i + j)


def l11_gate_up(pe, m, L, n, c, w1, w3, moving, width):
    at, rows = CHUNKS[c]
    for side, w in enumerate((w1, w3)):
        for k in range(2):
            ins = pe.matmul(m.flat(2 * side + c % 2)[0:rows, 0:width], w[:, k, at:at + rows], moving[:, k, :],
                            start=(k == 0), stop=(k == 1))
    ins.then_inc(L.s("gu_ready"), 1)


def l11_pe(pe, m, L):
    w = m.w
    pe.wait_ge(m.s_w[11], 16 * m.n_w[11])
    with pe.Fori(0, GROUPS) as g:
        pe_group_T(pe, m, L, g, [m.flat(6), m.flat(7)])
        pe.wait_ge(*L.after("xsT_kept", g + 1))
        for q in range(4):
            for k in range(2):
                ins = pe.matmul(m.flat(6)[:, q * E11:(q + 1) * E11], m.xsT[:, k, q * P:(q + 1) * P], w["l11_wg"][:, k, :],
                                start=(k == 0), stop=(k == 1))
        ins.then_inc(L.s("logits_ready"), 1)
        for c in range(NC):
            if c == 2:
                pe.wait_ge(*L.after("h_kept", NC * g + 1))
            l11_gate_up(pe, m, L, NC * g + c, c, w["l11_sw1"], w["l11_sw3"], m.xsT, 512)
        for c in range(NC):
            at, rows = CHUNKS[c]
            w2 = w["l11_sw2a"][:, c, :] if c < 2 else w["l11_sw2b"]
            pe.wait_ge(*L.after("h_kept", NC * g + c + 1))
            for q in range(4):
                ins = pe.matmul(m.flat(4 + q // 2)[:, (q % 2) * D:(q % 2 + 1) * D], m.hT[0:rows, c, q * P:(q + 1) * P],
                                w2, start=(c == 0 and q % 2 == 0), stop=(c == NC - 1), skip_group_check=True)
        ins.then_inc(L.s("shared_ready"), 1)
    pe.wait_ge(*L.after("prefix_ready", 1))
    pe.matmul(m.flat(0)[:, 0:P], w["l11_before"], m.oh.rearrange("p t e -> p (t e)"), start=True, stop=False)
    pe.matmul(m.flat(0)[:, 0:P], w["l11_ones"], m.pre2[:, 0:NT, :].rearrange("p t e -> p (t e)"), start=False, stop=True)\
      .then_inc(L.s("places_ready"), 1)
    with pe.Fori(0, E11 // 2) as i:
        for j in range(2):
            e = 2 * i + j
            ring = m.w["l11_ring"][:, j, :]
            w1, w3 = (ring[:, v * 704:(v + 1) * 704].rearrange("p (k f) -> p k f", k=2) for v in range(2))
            pe.wait_ge(*L.after("slot_x%d" % j, 16 * (i + 1)))
            for k in range(2):
                for h in range(2):
                    ins = pe.transpose(m.flat(6)[:, (2 * k + h) * P:(2 * k + h + 1) * P], m.xd[:, j, h, k * P:(k + 1) * P], m.ident[:])
            ins.then_inc(L.s("slot_x_T"), 1)
            pe.wait_ge(*L.after("slot_xT_kept", e + 1))
            pe.wait_ge(*L.after("expert_w%d" % j, 64 * (i + 1)))
            n0 = GROUPS * NC + NC * e
            for c in range(NC):
                if c == 2:
                    pe.wait_ge(*L.after("h_kept", n0 + 1))
                l11_gate_up(pe, m, L, n0 + c, c, w1, w3, m.xdT, 2 * P)
            for c in range(NC):
                at, rows = CHUNKS[c]
                pe.wait_ge(*L.after("h_kept", n0 + c + 1))
                for h in range(2):
                    ins = pe.matmul(m.flat(4)[:, h * D:(h + 1) * D], m.hT[0:rows, c, h * P:(h + 1) * P],
                                    ring[0:rows, 1408 + c * D:1408 + (c + 1) * D], start=(c == 0 and h == 0),
                                    stop=(c == NC - 1), skip_group_check=True)
            ins.then_inc(L.s("slot_y_ready"), 1)


def l11_act(act, m, L):
    with act.Fori(0, GROUPS) as g:
        act.copy(m.xs[:, :, :], m.x[:, bass.ds(4 * g, 4), :]).then_inc(L.s("xs_copied"), 1)
        act_group_T(act, m, L, g, [m.flat(6), m.flat(7)])
        act.wait_ge(*L.after("logits_ready", g + 1))
        act.copy(m.lg[:, bass.ds(4 * g, 4), :], m.flat(6)[:, 0:4 * E11].rearrange("p (q e) -> p q e", q=4))\
           .then_inc(L.s("logits_kept"), 1)
        for c in range(NC):
            rows = CHUNKS[c][1]
            act.wait_ge(*L.after("gu_ready", NC * g + c + 1))
            act.activation(m.th[0:rows, c % 2, :], m.flat(c % 2)[0:rows, :], ACT.Tanh, scale=0.5).then_inc(L.s("tanh_ready"), 1)
        act.wait_ge(*L.after("shared_kept", g + 1))
    act.wait_ge(*L.after("shifted", 1))
    act.activation(m.tmp, m.tmp, ACT.Exp).then_inc(L.s("route_exp"), 1)
    with act.Fori(0, E11 // 2) as i:
        for j in range(2):
            e = 2 * i + j
            act.wait_ge(*L.after("slot_x_T", e + 1))
            act.copy(m.xdT[:, :, :].rearrange("p k t -> p (k t)"), m.flat(6)).then_inc(L.s("slot_xT_kept"), 1)
            n0 = GROUPS * NC + NC * e
            for c in range(NC):
                rows = CHUNKS[c][1]
                act.wait_ge(*L.after("gu_ready", n0 + c + 1))
                act.activation(m.th[0:rows, c % 2, 0:2 * P], m.flat(c % 2)[0:rows, 0:2 * P], ACT.Tanh, scale=0.5)\
                   .then_inc(L.s("tanh_ready"), 1)


def l11_hidden(dve, m, L, n, c, width):
    rows = CHUNKS[c][1]
    dve.wait_ge(*L.after("tanh_ready", n + 1))
    dve.scalar_tensor_tensor(m.sg[0:rows, c % 2, 0:width], m.th[0:rows, c % 2, 0:width], 1.0,
                             m.flat(c % 2)[0:rows, 0:width], ALU.add, ALU.mult).then_inc(L.s("silu_ready"), 1)
    dve.wait_ge(*L.after("silu_ready", n + 1))
    dve.scalar_tensor_tensor(m.hT[0:rows, c, 0:width], m.sg[0:rows, c % 2, 0:width], 0.5,
                             m.flat(2 + c % 2)[0:rows, 0:width], ALU.mult, ALU.mult).then_inc(L.s("h_kept"), 1)


def l11_dve(dve, m, L):
    w = m.w
    done = [0]

    def then(ins):
        done[0] += 1
        ins.then_inc(L.s("route_step"), 1)
        dve.wait_ge(*L.after("route_step", done[0]))

    dve.memset(m.zeros, 0.0).then_inc(L.s("zeros_ready"), 1)
    with dve.Fori(0, GROUPS) as g:
        for c in range(NC):
            l11_hidden(dve, m, L, NC * g + c, c, 512)
        dve.wait_ge(*L.after("shared_ready", g + 1))
        for q in range(4):
            ins = dve.tensor_tensor(m.sh[:, 4 * g + q, :], m.flat(4 + q // 2)[:, (q % 2) * D:(q % 2 + 1) * D], m.xs[:, q, :], ALU.add)
        ins.then_inc(L.s("shared_kept"), 1)
    dve.wait_ge(m.s_w[11], 16 * m.n_w[11])
    dve.wait_ge(*L.after("logits_kept", GROUPS))
    then(dve.tensor_reduce(m.mx, m.lg, AX.X, ALU.max))
    mx = m.mx.unsqueeze(2).to_broadcast([P, NT, E11])
    dve.tensor_tensor(m.tmp, m.lg, mx, ALU.subtract).then_inc(L.s("shifted"), 1)
    then(dve.tensor_tensor(m.cand, m.lg, mx, ALU.not_equal))
    then(dve.scalar_tensor_tensor(m.cand, m.cand, 1000.0, w["l11_iota"].unsqueeze(1).to_broadcast([P, NT, E11]), ALU.mult, ALU.add))
    then(dve.tensor_reduce(m.eidx, m.cand, AX.X, ALU.min))
    then(dve.tensor_tensor(m.oh, m.cand, m.eidx.unsqueeze(2).to_broadcast([P, NT, E11]), ALU.is_equal))
    dve.memset(m.pre[:, 0, :], 0.0)
    then(dve.tensor_copy(m.pre[:, 1:NT + 1, :], m.oh))
    a, b = m.pre, m.pre2
    for shift in (1, 2, 4, 8):
        dve.tensor_copy(b[:, 0:shift, :], a[:, 0:shift, :])
        then(dve.tensor_tensor(b[:, shift:NT + 1, :], a[:, shift:NT + 1, :], a[:, 0:NT + 1 - shift, :], ALU.add))
        a, b = b, a
    dve.tensor_copy(m.pre2, m.pre).then_inc(L.s("prefix_ready"), 1)
    dve.wait_ge(*L.after("route_exp", 1))
    then(dve.tensor_reduce(m.rsum, m.tmp, AX.X, ALU.add))
    then(dve.reciprocal(m.gate, m.rsum))
    dve.wait_ge(*L.after("places_ready", 1))
    then(dve.tensor_tensor(m.cand, m.flat(0)[:, 0:P].rearrange("p (t e) -> p t e", e=E11), m.oh, ALU.mult))
    then(dve.tensor_reduce(m.place, m.cand, AX.X, ALU.add))
    dve.tensor_scalar(m.keep, m.place, float(C11), None, ALU.is_lt)
    then(dve.scalar_tensor_tensor(m.slot, m.eidx, float(C11), m.place, ALU.mult, ALU.add))
    dve.tensor_tensor(m.a1, m.slot, w["l11_overflow"], ALU.subtract)
    then(dve.tensor_scalar(m.a2, m.slot, 1.0 - TOK, None, ALU.add))
    dve.tensor_tensor(m.a1, m.a1, m.keep, ALU.mult)
    dve.tensor_tensor(m.gate, m.gate, m.keep, ALU.mult)
    then(dve.tensor_tensor(m.a2, m.a2, m.keep, ALU.mult))
    dve.tensor_tensor(m.idx_put.bitcast(mybir.dt.uint32), m.a1, w["l11_overflow"], ALU.add)
    dve.tensor_scalar(m.idx_get.bitcast(mybir.dt.uint32), m.a2, TOK - 1.0, None, ALU.add).then_inc(L.s("slots_known"), 1)
    assert done[0] == 17, done
    with dve.Fori(0, E11 // 2) as i:
        for j in range(2):
            e = 2 * i + j
            for c in range(NC):
                l11_hidden(dve, m, L, GROUPS * NC + NC * e + c, c, 2 * P)
            dve.wait_ge(*L.after("slot_y_ready", e + 1))
            dve.tensor_copy(m.ys[:, j].rearrange("p h d -> p (h d)"), m.flat(4)).then_inc(L.s("slot_y_kept"), 1)
        for j in range(2):
            dve.wait_ge(*L.after("slot_y_out%d" % j, 16 * (i + 1)))
    dve.wait_ge(*L.after("fetched", 16 * NT))
    with dve.Fori(0, NT // 2) as i:
        for j in range(2):
            T = 2 * i + j
            dve.wait_ge(*L.after("x_written", T - 1))
            dve.scalar_tensor_tensor(m.r[:, j, :], m.og[:, T, :], m.gate[:, bass.ds(T, 1)], m.sh[:, T, :], ALU.mult, ALU.add)\
               .then_inc(L.s("r_kept"), 1)
        dve_norm_tail(dve, m, L, i)


def l11_pool(pool, m, L):
    x_rows, y_rows = m.scratch["slot_x"], m.scratch["slot_y"]
    u32 = mybir.dt.uint32
    pool.wait_ge(*L.after("slots_known", 1))
    pool.wait_ge(*L.after("slots_zeroed", 16))
    for T in range(NT):
        pool.indirect_dma_start(x_rows, bass.IndirectOffsetOnAxis(ap=m.idx_put[:, T:T + 1].bitcast(u32), axis=0),
                                m.x[:, T, :], None).then_inc(L.s("scattered"), 16)
    y_out = y_rows.rearrange("(e h p) d -> e p h d", h=2, p=P)
    with pool.Fori(0, E11 // 2) as i:
        for j in range(2):
            pool.wait_ge(*L.after("slot_y_kept", 2 * i + j + 1))
            pool.dma_start(y_out[bass.ds(2 * i + j, 1)].rearrange("a p h d -> (a p) h d"), m.ys[:, j])\
                .then_inc(L.s("slot_y_out%d" % j), 16)
    for j in range(2):
        pool.wait_ge(*L.after("slot_y_out%d" % j, 16 * E11 // 2))
    for T in range(NT):
        pool.indirect_dma_start(m.og[:, T, :], None, y_rows,
                                bass.IndirectOffsetOnAxis(ap=m.idx_get[:, T:T + 1].bitcast(u32), axis=0))\
            .then_inc(L.s("fetched"), 16)
    with pool.Fori(0, NT // 2) as i:
        for j in range(2):
            pool_rstd(pool, m, L, 2 * i + j, j)



DI = 4096
CT = DI // P
MH = 64
W_IN, W_OUT = 2 * 2 * P + 5, D + 2


def l6_names():
    n = per_tile(*TILE4)
    n.update({k: GROUPS for k in ("var_ready", "rstd_ready", "xs_copied", "xsT_ready", "xsT_kept", "dt_ready", "dt_biased",
                                  "dt_abs", "dt_exp", "dt_ln", "dt_kept", "dA_kept", "bc_ready", "bc_conv1", "bc_conv2",
                                  "bc_conv3", "bc_conv0", "bc_tanh", "bc_kept", "cb_ready", "cb_kept", "ss_ready",
                                  "ms_kept", "scale_ready")})
    n.update({k: GROUPS * CT for k in ("x_ready6", "g_ready6", "x2T_ready", "diff_ready", "yT_ready", "out_added",
                                       "conv0", "x_tanh", "g_tanh", "decay_kept", "hid_sq", "conv1", "conv2", "conv3",
                                       "x2_kept", "g2_kept", "xdt_kept", "hid2_kept", "hid4_kept", "spread", "weighted",
                                       "wo_scaled", "sq_summed")})
    for u in range(4):
        n["in_loaded%d" % u] = n["out_loaded%d" % u] = 16 * GROUPS * CT // 4
    n["a_exp"] = 1
    return n


def l6_places(m, ar):
    group_places(m, ar)
    m.dtv, m.dta, m.dt, m.dA = (ar.take([4, MH]) for _ in range(4))
    m.aexp = ar.take([MH])
    m.bcy, m.bct, m.bc2, m.cbm = ar.take([2, 512]), ar.take([2, 512]), ar.take([2, 512]), ar.take([4, S])
    m.y, m.th, m.x2 = ar.take([2, 512]), ar.take([2, 512]), ar.take([4, 512])
    m.tg, m.g2 = ar.take([2, 512]), ar.take([4, 512])
    m.xdt, m.da_i, m.ed, m.sx = ar.take([2, 512]), ar.take([2, 512]), ar.take([2, 512]), ar.take([2, 512])
    m.h2, m.h4, m.sq, m.acc = ar.take([2, 512]), ar.take([4, 512]), ar.take([2, 512]), ar.take([2, 512])
    m.wos = ar.take([2, D])
    m.ms, m.rv, m.ones_col = ar.take([4]), ar.take([4]), ar.take([1])


def channel_steps(eng, body):
    for s in range(4):
        body(s, 0, s, lambda k, s=s: s >= k)
    with eng.Fori(1, CT // 4) as q:
        for u in range(4):
            body(4 * q + u, q, u, lambda k: True)
    for s in range(CT, CT + 3):
        body(s, s // 4, s % 4, lambda k, s=s: s - k < CT)


def l6_sync(sp, m, L):
    def quad(g, q, wait):
        for u in range(4):
            n = CT * g + 4 * q + u
            c = 4 * q + u
            if wait:
                sp.wait_ge(*L.after("g2_kept", n - 3))
            sp.dma_start(m.w["l6_in"][:, u, :], m.dram["mamba_in"][bass.ds(c, 1)].rearrange("a p n -> (a p) n"))\
              .then_inc(L.s("in_loaded%d" % u), 16)
            if wait:
                sp.wait_ge(*L.after("out_added", n - 3))
            sp.dma_start(m.w["l6_out"][:, u, :], m.dram["mamba_out"][bass.ds(c, 1)].rearrange("a p n -> (a p) n"))\
              .then_inc(L.s("out_loaded%d" % u), 16)

    quad(0, 0, False)
    with sp.Fori(1, CT // 4) as q:
        quad(0, q, True)
    with sp.Fori(1, GROUPS) as g:
        with sp.Fori(0, CT // 4) as q:
            quad(g, q, True)


def l6_pe(pe, m, L):
    w = m.w
    X, G, XT, DF, OUT = m.flat(0), m.flat(1), m.flat(2), m.flat(3), 6
    pe.wait_ge(m.s_w[6], 16 * m.n_w[6])
    with pe.Fori(0, GROUPS) as g:
        pe_group_T(pe, m, L, g, [m.flat(6), m.flat(7)])
        pe.wait_ge(*L.after("xsT_kept", g + 1))
        for q in range(4):
            for k in range(2):
                ins = pe.matmul(XT[:, q * MH:(q + 1) * MH], m.xsT[:, k, q * P:(q + 1) * P], w["l6_wdt"][:, k, :],
                                start=(k == 0), stop=(k == 1))
        ins.then_inc(L.s("dt_ready"), 1)
        for side, bank in enumerate((X, G)):
            for k in range(2):
                ins = pe.matmul(bank, w["l6_wbc"][:, k, side * P:(side + 1) * P], m.xsT[:, k, :], start=(k == 0), stop=(k == 1))
        ins.then_inc(L.s("bc_ready"), 1)
        pe.wait_ge(*L.after("bc_kept", g + 1))
        for b in range(8):
            ins = pe.matmul(DF[64 * (b % 2):64 * (b % 2) + 64, (b // 2) * S:(b // 2 + 1) * S], m.bc2[:, 0, b * S:(b + 1) * S],
                            m.bc2[:, 1, b * S:(b + 1) * S], start=True, stop=True)
        ins.then_inc(L.s("cb_ready"), 1)
        pe.wait_ge(*L.after("cb_kept", g + 1))

        def step(s, q, u, on):
            n = CT * g + s
            if on(0):
                ring = w["l6_in"][:, u, 0:512].rearrange("p (v k c) -> p v k c", v=2, k=2)
                pe.wait_ge(*L.after("in_loaded%d" % u, (q + 1 + 8 * g) * 16))
                if not (isinstance(s, int) and s == 0):
                    pe.wait_ge(*L.after("conv3", n))
                for k in range(2):
                    ins = pe.matmul(X, ring[:, 0, k, :], m.xsT[:, k, :], start=(k == 0), stop=(k == 1))
                ins.then_inc(L.s("x_ready6"), 1)
                if not (isinstance(s, int) and s == 0):
                    pe.wait_ge(*L.after("g2_kept", n))
                for k in range(2):
                    ins = pe.matmul(G, ring[:, 1, k, :], m.xsT[:, k, :], start=(k == 0), stop=(k == 1))
                ins.then_inc(L.s("g_ready6"), 1)
            if on(1):
                v = (u - 1) % 4
                pe.wait_ge(*L.after("spread", n))
                if on(2):
                    pe.wait_ge(*L.after("decay_kept", n - 1))
                pe.matmul(DF, w["l6_after"], m.da_i[:, v % 2, :], start=True, stop=True).then_inc(L.s("diff_ready"), 1)
                pe.wait_ge(*L.after("x2_kept", n))
                if on(2):
                    pe.wait_ge(*L.after("xdt_kept", n - 1))
                for t in range(4):
                    ins = pe.transpose(XT[:, t * P:(t + 1) * P], m.x2[:, v, t * P:(t + 1) * P], m.ident[:])
                ins.then_inc(L.s("x2T_ready"), 1)
            if on(2):
                v = (u - 2) % 4
                pe.wait_ge(*L.after("xdt_kept", n - 1))
                pe.wait_ge(*L.after("weighted", n - 1))
                if on(3):
                    pe.wait_ge(*L.after("hid2_kept", n - 2))
                pe.matmul(m.flat(4)[:, 511:512], m.ident[:, :], m.ident[:, 0:1], start=True, stop=True)
                for t in range(4):
                    for b in range(2):
                        rows = slice(64 * b, 64 * b + 64)
                        for e in range(2):
                            at = (2 * t + e) * S
                            ins = pe.matmul(m.flat(4 + b)[64 * e:64 * e + 64, t * S:(t + 1) * S], m.xdt[rows, v % 2, at:at + S],
                                            m.sx[rows, v % 2, at:at + S], start=True, stop=True)
                ins.then_inc(L.s("yT_ready"), 1)
            if on(3):
                v = (u - 3) % 4
                c0 = isinstance(s, int) and s == 3
                c31 = isinstance(s, int) and s == CT + 2
                pe.wait_ge(*L.after("wo_scaled", n - 2))
                pe.wait_ge(*L.after("hid4_kept", n - 2))
                for t in range(4):
                    ins = pe.matmul(m.flat(OUT + t // 2)[:, (t % 2) * D:(t % 2 + 1) * D], m.h4[:, v, t * P:(t + 1) * P],
                                    m.wos[:, v % 2, :], start=(c0 and t % 2 == 0), stop=c31, skip_group_check=True)
                ins.then_inc(L.s("out_added"), 1)

        channel_steps(pe, step)
        pe.wait_ge(*L.after("sq_summed", CT * (g + 1)))
        for t in range(4):
            ins = pe.matmul(X[:, t:t + 1], m.acc[:, (CT - 1) % 2, t * P:(t + 1) * P], m.ones_col, start=True, stop=True)
        ins.then_inc(L.s("ss_ready"), 1)


def l6_act(act, m, L):
    X, G, DF = m.flat(0), m.flat(1), m.flat(3)
    act.wait_ge(m.s_w[6], 16 * m.n_w[6])
    act.activation(m.aexp, m.w["l6_alog"], ACT.Exp).then_inc(L.s("a_exp"), 1)
    with act.Fori(0, GROUPS) as g:
        act_group_copy(act, m, L, g)
        act_group_T(act, m, L, g, [m.flat(6), m.flat(7)])
        act.wait_ge(*L.after("dt_abs", g + 1))
        act.activation(m.dta, m.dta, ACT.Exp, scale=-1.0).then_inc(L.s("dt_exp"), 1)
        act.wait_ge(*L.after("dt_exp", g + 1))
        act.activation(m.dta, m.dta, ACT.Ln, bias=1.0).then_inc(L.s("dt_ln"), 1)
        act.wait_ge(*L.after("bc_ready", g + 1))
        for side, bank in enumerate((X, G)):
            ins = act.activation(m.bcy[:, side, :], bank, ACT.Identity, bias=m.w["l6_cbc"][:, side, 4:5],
                                 scale=m.w["l6_cbc"][:, side, 3:4])
        ins.then_inc(L.s("bc_conv0"), 1)
        act.wait_ge(*L.after("bc_conv3", g + 1))
        act.activation(m.bct, m.bcy, ACT.Tanh, scale=0.5).then_inc(L.s("bc_tanh"), 1)

        def step(s, q, u, on):
            n = CT * g + s
            if on(0):
                conv = m.w["l6_in"][:, u, 512:517]
                act.wait_ge(*L.after("x_ready6", n + 1))
                act.activation(m.y[:, u % 2, :], X, ACT.Identity, bias=conv[:, 4:5], scale=conv[:, 3:4]).then_inc(L.s("conv0"), 1)
            if on(1):
                v = (u - 1) % 4
                act.wait_ge(*L.after("diff_ready", n))
                if on(3):
                    act.wait_ge(*L.after("weighted", n - 2))
                act.activation(m.ed[:, v % 2, :], DF, ACT.Exp).then_inc(L.s("decay_kept"), 1)
            if on(0):
                act.wait_ge(*L.after("g_ready6", n + 1))
                act.activation(m.tg[:, u % 2, :], G, ACT.Tanh, scale=0.5).then_inc(L.s("g_tanh"), 1)
                act.wait_ge(*L.after("conv3", n + 1))
                act.activation(m.th[:, u % 2, :], m.y[:, u % 2, :], ACT.Tanh, scale=0.5).then_inc(L.s("x_tanh"), 1)
            if on(2):
                v = (u - 2) % 4
                act.wait_ge(*L.after("hid4_kept", n - 1))
                if not (isinstance(s, int) and s < 4):
                    act.wait_ge(*L.after("sq_summed", n - 3))
                act.activation(m.sq[:, v % 2, :], m.h4[:, v, :], ACT.Square).then_inc(L.s("hid_sq"), 1)

        channel_steps(act, step)


def l6_conv(dve, m, L, name, n, taps, y, x):
    for shift in range(1, 4):
        dve.wait_ge(*L.after(name + str(shift - 1), n + 1))
        for a, (tap, yy, xx) in enumerate(zip(taps, y, x)):
            y3, x3 = yy.rearrange("p (b s) -> p b s", b=8), xx.rearrange("p (b s) -> p b s", b=8)
            ins = dve.scalar_tensor_tensor(y3[:, :, shift:S], x3[:, :, 0:S - shift], tap[:, 3 - shift:4 - shift],
                                           y3[:, :, shift:S], ALU.mult, ALU.add)
        ins.then_inc(L.s(name + str(shift)), 1)


def l6_dve(dve, m, L):
    w = m.w
    X, G, XT, DF = m.flat(0), m.flat(1), m.flat(2), m.flat(3)
    dve.memset(m.ones_col, 1.0)
    dve.wait_ge(m.s_w[6], 16 * m.n_w[6])
    dve.wait_ge(*L.after("a_exp", 1))
    with dve.Fori(0, GROUPS) as g:
        dve.wait_ge(*L.after("dt_ready", g + 1))
        dve.tensor_tensor(m.dtv, XT[:, 0:4 * MH].rearrange("p (t h) -> p t h", t=4), w["l6_dtb"].unsqueeze(1).to_broadcast([P, 4, MH]),
                          ALU.add).then_inc(L.s("dt_biased"), 1)
        dve.wait_ge(*L.after("dt_biased", g + 1))
        dve.scalar_tensor_tensor(m.dta, m.dtv, -1.0, m.dtv, ALU.mult, ALU.max).then_inc(L.s("dt_abs"), 1)
        dve.wait_ge(*L.after("dt_ln", g + 1))
        dve.scalar_tensor_tensor(m.dt, m.dtv, 0.0, m.dta, ALU.max, ALU.add).then_inc(L.s("dt_kept"), 1)
        dve.wait_ge(*L.after("dt_kept", g + 1))
        dve.scalar_tensor_tensor(m.dA, m.dt, -1.0, m.aexp.unsqueeze(1).to_broadcast([P, 4, MH]), ALU.mult, ALU.mult)\
           .then_inc(L.s("dA_kept"), 1)
        l6_conv(dve, m, L, "bc_conv", g, [w["l6_cbc"][:, a, :] for a in range(2)], [m.bcy[:, a, :] for a in range(2)], [X, G])
        dve.wait_ge(*L.after("bc_tanh", g + 1))
        dve.scalar_tensor_tensor(m.bc2, m.bct, 1.0, m.bcy, ALU.add, ALU.mult).then_inc(L.s("bc_kept"), 1)
        dve.wait_ge(*L.after("cb_ready", g + 1))
        dve.tensor_tensor(m.cbm, DF[:, 0:4 * S].rearrange("p (t i) -> p t i", t=4), w["l6_mask"].unsqueeze(1).to_broadcast([P, 4, S]),
                          ALU.mult).then_inc(L.s("cb_kept"), 1)

        def step(s, q, u, on):
            n = CT * g + s
            if on(0):
                l6_conv(dve, m, L, "conv", n, [w["l6_in"][:, u, 512:517]], [m.y[:, u % 2, :]], [X])
            if on(1):
                v = (u - 1) % 4
                dve.wait_ge(*L.after("x2T_ready", n))
                if on(3):
                    dve.wait_ge(*L.after("yT_ready", n - 2))
                c = s - 1
                dts = m.dt[:, :, bass.ds(2 * c, 2)].unsqueeze(3).to_broadcast([P, 4, 2, 64])
                dve.tensor_tensor(m.xdt[:, v % 2, :].rearrange("p (t e c) -> p t e c", t=4, e=2),
                                  XT.rearrange("p (t e c) -> p t e c", t=4, e=2), dts, ALU.mult).then_inc(L.s("xdt_kept"), 1)
            if on(0):
                dve.wait_ge(*L.after("g_tanh", n + 1))
                dve.scalar_tensor_tensor(m.g2[:, u, :], m.tg[:, u % 2, :], 1.0, G, ALU.add, ALU.mult).then_inc(L.s("g2_kept"), 1)
                dve.wait_ge(*L.after("x_tanh", n + 1))
                dve.scalar_tensor_tensor(m.x2[:, u, :], m.th[:, u % 2, :], 1.0, m.y[:, u % 2, :], ALU.add, ALU.mult)\
                   .then_inc(L.s("x2_kept"), 1)
            if on(2):
                v = (u - 2) % 4
                qq = q if u >= 2 else q - 1
                dve.wait_ge(*L.after("out_loaded%d" % v, (qq + 1 + 8 * g) * 16))
                dve.wait_ge(*L.after("yT_ready", n - 1))
                for b in range(2):
                    x4, h4 = (a.rearrange("p (t b i) -> p t b i", t=4, b=2)[:, :, b, :] for a in (m.x2[:, v, :], m.h2[:, v % 2, :]))
                    ins = dve.scalar_tensor_tensor(h4, x4, w["l6_out"][:, v, D:D + 1],
                                                   m.flat(4 + b)[:, 0:256].rearrange("p (t i) -> p t i", t=4), ALU.mult, ALU.add)
                ins.then_inc(L.s("hid2_kept"), 1)
                dve.wait_ge(*L.after("hid2_kept", n - 1))
                dve.tensor_tensor(m.h4[:, v, :], m.h2[:, v % 2, :], m.g2[:, v, :], ALU.mult).then_inc(L.s("hid4_kept"), 1)

        channel_steps(dve, step)
        dve.wait_ge(*L.after("ss_ready", g + 1))
        dve.tensor_scalar(m.ms, X[:, 0:4], 1.0 / DI, 16e-5, ALU.mult, ALU.add).then_inc(L.s("ms_kept"), 1)
        dve.wait_ge(*L.after("scale_ready", g + 1))
        for t in range(4):
            dve.scalar_tensor_tensor(m.r4[:, t, :], m.flat(6 + t // 2)[:, (t % 2) * D:(t % 2 + 1) * D], m.rv[:, t:t + 1],
                                     m.xs[:, t, :], ALU.mult, ALU.add).then_inc(L.s("r_kept"), 1)
        dve_norm4_tail(dve, m, L, g)


def l6_pool(pool, m, L):
    w = m.w
    pool.wait_ge(m.s_w[6], 16 * m.n_w[6])
    with pool.Fori(0, GROUPS) as g:
        pool.wait_ge(*L.after("dA_kept", g + 1))
        pool.wait_ge(*L.after("cb_kept", g + 1))

        def step(s, q, u, on):
            n = CT * g + s
            if on(0):
                if not (isinstance(s, int) and s < 2):
                    pool.wait_ge(*L.after("diff_ready", n - 1))
                das = m.dA[:, :, bass.ds(2 * s, 2)].unsqueeze(3).to_broadcast([P, 4, 2, S])
                pool.tensor_tensor(m.da_i[:, u % 2, :].rearrange("p (t e i) -> p t e i", t=4, e=2), das,
                                   w["l6_upto"].unsqueeze(1).unsqueeze(1).to_broadcast([P, 4, 2, S]), ALU.mult).then_inc(L.s("spread"), 1)
            if on(1):
                v = (u - 1) % 4
                pool.wait_ge(*L.after("decay_kept", n))
                if on(3):
                    pool.wait_ge(*L.after("yT_ready", n - 2))
                pool.tensor_tensor(m.sx[:, v % 2, :].rearrange("p (t e i) -> p t e i", t=4, e=2),
                                   m.ed[:, v % 2, :].rearrange("p (t e i) -> p t e i", t=4, e=2),
                                   m.cbm.unsqueeze(2).to_broadcast([P, 4, 2, S]), ALU.mult).then_inc(L.s("weighted"), 1)
            if on(2):
                v = (u - 2) % 4
                qq = q if u >= 2 else q - 1
                pool.wait_ge(*L.after("out_loaded%d" % v, (qq + 1 + 8 * g) * 16))
                if not (isinstance(s, int) and s < 4):
                    pool.wait_ge(*L.after("out_added", n - 3))
                pool.tensor_tensor(m.wos[:, v % 2, :], w["l6_out"][:, v, 0:D], w["l6_out"][:, v, D + 1:D + 2].to_broadcast([P, D]),
                                   ALU.mult).then_inc(L.s("wo_scaled"), 1)
                pool.wait_ge(*L.after("hid_sq", n - 1))
                if isinstance(s, int) and s == 2:
                    pool.tensor_tensor(m.acc[:, 0, :], m.sq[:, 0, :], m.ones_col.to_broadcast([P, 512]), ALU.mult).then_inc(L.s("sq_summed"), 1)
                else:
                    pool.wait_ge(*L.after("sq_summed", n - 2))
                    pool.tensor_tensor(m.acc[:, v % 2, :], m.acc[:, (v - 1) % 2, :], m.sq[:, v % 2, :], ALU.add)\
                        .then_inc(L.s("sq_summed"), 1)

        channel_steps(pool, step)
        pool.wait_ge(*L.after("ms_kept", g + 1))
        pool.tensor_tensor(m.rv, m.ms, m.mhalf[:, 0:4], ALU.pow).then_inc(L.s("scale_ready"), 1)
        pool.wait_ge(*L.after("var_ready", g + 1))
        pool.tensor_tensor(m.rs4[:, :], m.va4[:, :], m.mhalf[:, 0:4], ALU.pow).then_inc(L.s("rstd_ready"), 1)



QD, QH, RD = 192, 96, 64


def l7_names():
    n = per_tile(*TILE, "scores_ready", "max_ready", "shift_ready", "exp_ready", "sum_ready", "rinv_ready", "p_ready",
                 "pT_ready", "pT_kept0", "pT_kept1", "o_ready", "oT_kept", "y_ready")
    n.pop("x_copied")
    n.update({k: GROUPS for k in ("xs_copied", "xsT_ready", "xsT_kept", "kv_parts", "kv_roped", "kvT_ready", "kvT_kept")})
    n.update({k: GROUPS * H for k in ("big_ready", "rope_parts", "roped", "qc_ready", "qc_kept")})
    n.update({"weff_ready": H, "weff_kept": H, "wqk_ready": 4, "wqk_kept": 4, "wvo_ready": 4, "wvo_kept": 4})
    n.update({"raw_loaded": 16 * 3, "ctx_group": 16 * GROUPS})
    return n


def l7_places(m, ar):
    m.weff, m.wqk, m.wvo = ar.take([2, H * QD]), ar.take([H, 2, RD], QH), ar.take([8, D])
    start = ar.at
    m.kcq, m.qrT, m.woT = ar.take([H, QD]), ar.take([H, QD], RD), ar.take([H, D])
    ar.at = start
    m.xs, m.xsT = ar.take([4, D]), ar.take([2, 512])
    m.cbg, m.kt1, m.kt2, m.kvr, m.kvT = ar.take([4, DC]), ar.take([4, DC]), ar.take([4, DC]), ar.take([4, 2, DC]), ar.take([4, P])
    m.qp = ar.take([4, 8, 2, S])
    m.r, m.bn, m.stat = ar.take([2, D]), ar.take([2, 6]), ar.take([2, 16])
    m.mx, m.sums, m.rinv = ar.take([2, 16]), ar.take([2, 16]), ar.take([2, 16])
    start = ar.at
    m.rp, m.qr = ar.take([2, 4, 512], QH), ar.take([2, 2, 512], QH)
    ar.at = start
    m.pr, m.pT, m.oc = ar.take([2, 1024]), ar.take([2, 1024]), ar.take([2, 8, P])


def l7_sync(sp, m, L):
    for place, name in ((m.kcq, "raw_kcq"), (m.qrT, "raw_qrT"), (m.woT, "raw_woT")):
        sp.dma_start(place, m.dram[name]).then_inc(L.s("raw_loaded"), 16)
    l7_folded(sp, L)
    with sp.Fori(0, GROUPS) as g:
        sp.wait_ge(*L.after("x_written", 4 * g))
        sp.dma_start(m.cbg, m.dram["ctx"][bass.ds(g * 4 * P, 4 * P), :].rearrange("(t p) d -> p t d", p=P))\
          .then_inc(L.s("ctx_group"), 16)


def l7_folded(eng, L):
    eng.wait_ge(*L.after("weff_kept", H))
    eng.wait_ge(*L.after("wqk_kept", 4))
    eng.wait_ge(*L.after("wvo_kept", 4))


def l7_pe(pe, m, L):
    w = m.w
    pe.wait_ge(m.s_w[7], 16 * m.n_w[7])
    pe.wait_ge(*L.after("raw_loaded", 16 * 3))
    for h in range(H):
        if h >= 2:
            pe.wait_ge(*L.after("weff_kept", h - 1))
        for k in range(2):
            ins = pe.matmul(m.flat(h % 2)[:, k * QD:(k + 1) * QD], w["l7_wq"][:, h, k * P:(k + 1) * P], m.kcq[:, h, :],
                            start=True, stop=True)
        ins.then_inc(L.s("weff_ready"), 1)
        if h % 4 == 3:
            n = h // 4
            if n >= 2:
                pe.wait_ge(*L.after("wqk_kept", n - 1))
                pe.wait_ge(*L.after("wvo_kept", n - 1))
            for q in range(4):
                for side in range(2):
                    ins = pe.matmul(m.flat(2 + n % 2)[0:QH, (2 * q + side) * RD:(2 * q + side + 1) * RD],
                                    m.qrT[:, 4 * n + q, side * QH:(side + 1) * QH], w["l7_krT"][:, 4 * n + q, :],
                                    start=True, stop=True)
            ins.then_inc(L.s("wqk_ready"), 1)
            for q in range(4):
                hh = 4 * n + q
                ins = pe.matmul(m.flat(4 + n % 2)[64 * (q % 2):64 * (q % 2) + 64, (q // 2) * D:(q // 2 + 1) * D],
                                w["l7_kv"][:, hh, :], m.woT[:, hh, :], start=True, stop=True)
            ins.then_inc(L.s("wvo_ready"), 1)
    l7_folded(pe, L)
    with pe.Fori(0, GROUPS) as g:
        pe_group_T(pe, m, L, g, [m.flat(6), m.flat(7)])
        pe.wait_ge(*L.after("xsT_kept", g + 1))

        def big(h):
            if h >= 2:
                pe.wait_ge(*L.after("rope_parts", H * g + h - 1))
            for side in range(2):
                for k in range(2):
                    ins = pe.matmul(m.flat(2 * side + h % 2)[0:QH, :], m.weff[:, k, h * QD + side * QH:h * QD + (side + 1) * QH],
                                    m.xsT[:, k, :], start=(k == 0), stop=(k == 1))
            ins.then_inc(L.s("big_ready"), 1)

        def to_latent(h):
            pe.wait_ge(*L.after("roped", H * g + h + 1))
            if h >= 2:
                pe.wait_ge(*L.after("qc_kept", H * g + h - 1))
            for side in range(2):
                ins = pe.matmul(m.flat(4 + h % 2)[RD * (h // 8):RD * (h // 8) + RD, :], m.wqk[:, h, side, :], m.qr[:, h % 2, side, :],
                                start=(side == 0), stop=(side == 1))
            ins.then_inc(L.s("qc_ready"), 1)

        big(0)
        pe.wait_ge(*L.after("kv_roped", g + 1))
        for t in range(4):
            ins = pe.transpose(m.flat(6)[:, t * P:(t + 1) * P], m.kvr[:, t].rearrange("p a c -> p (a c)"), m.ident[:])
        ins.then_inc(L.s("kvT_ready"), 1)
        for h in range(1, H):
            big(h)
            to_latent(h - 1)
        to_latent(H - 1)
        pe.wait_ge(*L.after("qc_kept", H * g + H))
        pe.wait_ge(*L.after("kvT_kept", g + 1))
        for u in range(2):
            for j in range(2):
                t = 2 * u + j
                T = 4 * g + t
                if u:
                    pe.wait_ge(*L.after("pT_kept0", T - 1))
                    pe.wait_ge(*L.after("pT_kept1", T - 1))
                for hp in range(8):
                    for b in range(2):
                        at = (hp * 2 + b) * S
                        rows = slice(64 * (hp // 4), 64 * (hp // 4) + 64)
                        ins = pe.matmul(m.bank(j, at // 512)[:, at % 512:at % 512 + S],
                                        m.qp[rows, hp % 4, 2 * t + b].rearrange("p e s -> p (e s)"),
                                        m.kvT[rows, t, b * S:(b + 1) * S], start=True, stop=True)
                ins.then_inc(L.s("scores_ready"), 1)
            for j in range(2):
                T = 4 * g + 2 * u + j
                pe.wait_ge(*L.after("p_ready", T + 1))
                for hp in range(8):
                    ins = pe.transpose(m.bank(j, hp // 4)[:, (hp % 4) * P:(hp % 4 + 1) * P], m.pr[:, j, hp * P:(hp + 1) * P], m.ident[:])
                ins.then_inc(L.s("pT_ready"), 1)
            for j in range(2):
                t = 2 * u + j
                T = 4 * g + t
                pe.wait_ge(*L.after("pT_kept0", T + 1))
                pe.wait_ge(*L.after("pT_kept1", T + 1))
                if u:
                    pe.wait_ge(*L.after("r_kept", T - 1))
                pe.matmul(m.bank(j, 2)[:, 0:1], m.ident[:, :], m.ident[:, 0:1], start=True, stop=True)
                for b in range(2):
                    rows = slice(b * S, (b + 1) * S)
                    for h2 in range(2):
                        ins = pe.matmul(m.bank(j, 2 + b)[h2 * 64:(h2 + 1) * 64, :], m.kvr[rows, t, 0, :],
                                        m.pT[rows, j, :].rearrange("p (u e q) -> p u e q", u=8, e=2)[:, :, h2, :],
                                        start=True, stop=True)
                ins.then_inc(L.s("o_ready"), 1)
            for j in range(2):
                T = 4 * g + 2 * u + j
                pe.wait_ge(*L.after("oT_kept", T + 1))
                for hp in range(8):
                    ins = pe.matmul(m.bank(j, 2)[:, 0:D], m.oc[:, j, hp, :], m.wvo[:, hp, :], start=(hp == 0), stop=(hp == 7))
                ins.then_inc(L.s("y_ready"), 1)


def l7_act(act, m, L):
    for h in range(H):
        act.wait_ge(*L.after("weff_ready", h + 1))
        act.copy(m.weff[:, :, h * QD:(h + 1) * QD], m.flat(h % 2)[:, 0:2 * QD].rearrange("p (k q) -> p k q", k=2))\
           .then_inc(L.s("weff_kept"), 1)
    l7_folded(act, L)
    with act.Fori(0, GROUPS) as g:
        act_group_copy(act, m, L, g)
        act_group_T(act, m, L, g, [m.flat(6), m.flat(7)])
        act.wait_ge(*L.after("kvT_ready", g + 1))
        act.copy(m.kvT.rearrange("p t q -> p (t q)"), m.flat(6)).then_inc(L.s("kvT_kept"), 1)
        for h in range(H):
            act.wait_ge(*L.after("qc_ready", H * g + h + 1))
            rows = slice(RD * (h // 8), RD * (h // 8) + RD)
            act.copy(m.qp[rows, h // 2 % 4, :, h % 2, :], m.flat(4 + h % 2)[rows, :].rearrange("p (b s) -> p b s", b=8))\
               .then_inc(L.s("qc_kept"), 1)
        for u in range(2):
            for j in range(2):
                T = 4 * g + 2 * u + j
                act.wait_ge(*L.after("shift_ready", T + 1))
                act.activation(m.pr[:, j, :], m.pr[:, j, :], ACT.Exp).then_inc(L.s("exp_ready"), 1)
            for j in range(2):
                T = 4 * g + 2 * u + j
                act.wait_ge(*L.after("pT_ready", T + 1))
                act.copy(m.pT[:, j, 0:512], m.bank(j, 0)).then_inc(L.s("pT_kept0"), 1)
            for j in range(2):
                T = 4 * g + 2 * u + j
                act.wait_ge(*L.after("o_ready", T + 1))
                for b in range(2):
                    ins = act.copy(m.oc[:, j, :, b * S:(b + 1) * S], m.bank(j, 2 + b).rearrange("p (u q) -> p u q", u=8))
                ins.then_inc(L.s("oT_kept"), 1)


def l7_dve(dve, m, L):
    w = m.w
    for n in range(4):
        dve.wait_ge(*L.after("wqk_ready", n + 1))
        dve.tensor_copy(m.wqk[:, 4 * n:4 * n + 4].rearrange("p h a r -> p (h a r)"), m.flat(2 + n % 2)[0:QH, :])\
           .then_inc(L.s("wqk_kept"), 1)
        dve.wait_ge(*L.after("wvo_ready", n + 1))
        dve.tensor_copy(m.wvo[:, 2 * n:2 * n + 2].rearrange("p u o -> p (u o)"), m.flat(4 + n % 2)).then_inc(L.s("wvo_kept"), 1)
    l7_folded(dve, L)
    dve.wait_ge(m.s_w[7], 16 * m.n_w[7])
    with dve.Fori(0, GROUPS) as g:
        dve.wait_ge(*L.after("ctx_group", 16 * (g + 1)))
        dve.tensor_tensor(m.kt1, m.cbg, w["l7_kcos"].unsqueeze(1).to_broadcast([P, 4, DC]), ALU.mult)
        for half in range(2):
            ins = dve.tensor_tensor(m.kt2[:, :, 32 * half:32 * half + 32], m.cbg[:, :, 32 - 32 * half:64 - 32 * half],
                                    w["l7_ksin"][:, 32 * half:32 * half + 32].unsqueeze(1).to_broadcast([P, 4, 32]), ALU.mult)
        ins.then_inc(L.s("kv_parts"), 1)
        dve.wait_ge(*L.after("kv_parts", g + 1))
        dve.tensor_tensor(m.kvr, m.kt1.unsqueeze(2).to_broadcast([P, 4, 2, DC]), m.kt2.unsqueeze(2).to_broadcast([P, 4, 2, DC]), ALU.add).then_inc(L.s("kv_roped"), 1)
        for h in range(H):
            n = H * g + h
            dve.wait_ge(*L.after("big_ready", n + 1))
            if h >= 2:
                dve.wait_ge(*L.after("roped", n - 1))
            a, b = m.flat(h % 2)[0:QH, :], m.flat(2 + h % 2)[0:QH, :]
            for k, (src, tab) in enumerate(((a, 0), (b, 1), (b, 2), (a, 3))):
                ins = dve.tensor_tensor(m.rp[:, h % 2, k, :].rearrange("p (b s) -> p b s", b=8),
                                        src.rearrange("p (b s) -> p b s", b=8),
                                        w["l7_qtab"][:, tab, :].unsqueeze(1).to_broadcast([QH, 8, S]), ALU.mult)
            ins.then_inc(L.s("rope_parts"), 1)
            dve.wait_ge(*L.after("rope_parts", n + 1))
            if h >= 2:
                dve.wait_ge(*L.after("qc_ready", n - 1))
            dve.tensor_tensor(m.qr[:, h % 2], m.rp[:, h % 2, 0:4:2, :], m.rp[:, h % 2, 1:4:2, :], ALU.add)\
               .then_inc(L.s("roped"), 1)
        for u in range(2):
            for j in range(2):
                T = 4 * g + 2 * u + j
                dve.wait_ge(*L.after("scores_ready", T + 1))
                for f in range(2):
                    ins = dve.tensor_reduce(m.mx[:, j, 8 * f:8 * f + 8], m.bank(j, f).rearrange("p (r k) -> p r k", k=S), AX.X, ALU.max)
                ins.then_inc(L.s("max_ready"), 1)
            for j in range(2):
                T = 4 * g + 2 * u + j
                dve.wait_ge(*L.after("max_ready", T + 1))
                for f in range(2):
                    ins = dve.tensor_tensor(m.pr[:, j, 512 * f:512 * f + 512].rearrange("p (r k) -> p r k", k=S),
                                            m.bank(j, f).rearrange("p (r k) -> p r k", k=S),
                                            m.mx[:, j, 8 * f:8 * f + 8].unsqueeze(2).to_broadcast([P, 8, S]), ALU.subtract)
                ins.then_inc(L.s("shift_ready"), 1)
            for j in range(2):
                T = 4 * g + 2 * u + j
                dve.wait_ge(*L.after("exp_ready", T + 1))
                dve.tensor_reduce(m.sums[:, j, :], m.pr[:, j, :].rearrange("p (r k) -> p r k", k=S), AX.X, ALU.add)\
                   .then_inc(L.s("sum_ready"), 1)
            for j in range(2):
                T = 4 * g + 2 * u + j
                dve.wait_ge(*L.after("sum_ready", T + 1))
                dve.reciprocal(m.rinv[:, j, :], m.sums[:, j, :]).then_inc(L.s("rinv_ready"), 1)
            for j in range(2):
                T = 4 * g + 2 * u + j
                dve.wait_ge(*L.after("rinv_ready", T + 1))
                pr = m.pr[:, j, :].rearrange("p (r k) -> p r k", k=S)
                dve.tensor_tensor(pr, pr, m.rinv[:, j, :].unsqueeze(2).to_broadcast([P, 16, S]), ALU.mult).then_inc(L.s("p_ready"), 1)
            for j in range(2):
                T = 4 * g + 2 * u + j
                dve.wait_ge(*L.after("pT_ready", T + 1))
                dve.tensor_copy(m.pT[:, j, 512:1024], m.bank(j, 1)).then_inc(L.s("pT_kept1"), 1)
            for j in range(2):
                T = 4 * g + 2 * u + j
                dve.wait_ge(*L.after("y_ready", T + 1))
                dve.wait_ge(*L.after("x_written", T - 1))
                dve.tensor_tensor(m.r[:, j, :], m.bank(j, 2)[:, 0:D], m.xs[:, 2 * u + j, :], ALU.add).then_inc(L.s("r_kept"), 1)
            dve_norm_tail(dve, m, L, 2 * g + u)


def l7_pool(pool, m, L):
    with pool.Fori(0, NT // 2) as i:
        for j in range(2):
            pool_rstd(pool, m, L, 2 * i + j, j)



GROUPS = NT // 4
TILE4 = ("x_written", "r_kept", "stats_ready", "aggr_ready")


def act_group_copy(act, m, L, g):
    act.wait_ge(*L.after("x_written", 4 * g))
    act.copy(m.xs[:, :, :], m.x[:, bass.ds(4 * g, 4), :]).then_inc(L.s("xs_copied"), 1)


def pe_group_T(pe, m, L, g, banks):
    pe.wait_ge(*L.after("xs_copied", g + 1))
    for h in range(2):
        for q in range(4):
            ins = pe.transpose(banks[h][:, q * P:(q + 1) * P], m.xs[:, q, h * P:(h + 1) * P], m.ident[:])
    ins.then_inc(L.s("xsT_ready"), 1)


def act_group_T(act, m, L, g, banks):
    act.wait_ge(*L.after("xsT_ready", g + 1))
    for h in range(2):
        ins = act.copy(m.xsT[:, h, :], banks[h])
    ins.then_inc(L.s("xsT_kept"), 1)


def dve_norm4(dve, m, L, g, y_of):
    for q in range(4):
        dve.tensor_tensor(m.r4[:, q, :], y_of(q), m.xs[:, q, :], ALU.add).then_inc(L.s("r_kept"), 1)
    dve_norm4_tail(dve, m, L, g)


def dve_norm4_tail(dve, m, L, g):
    for q in range(4):
        dve.wait_ge(*L.after("r_kept", 4 * g + q + 1))
        dve.bn_stats(m.bn4[:, q, :], m.r4[:, q, :]).then_inc(L.s("stats_ready"), 1)
    dve.wait_ge(*L.after("stats_ready", 4 * g + 4))
    dve.memset(m.pause[:, :], 0.0)
    for q in range(4):
        dve.bn_aggr(m.mv4[:, q, :], m.bn4[:, q, :]).then_inc(L.s("aggr_ready"), 1)
    dve.wait_ge(*L.after("aggr_ready", 4 * g + 4))
    dve.tensor_scalar(m.va4[:, :], m.mv4[:, :, 1], LN_EPS, None, ALU.add).then_inc(L.s("var_ready"), 1)
    dve.wait_ge(*L.after("rstd_ready", g + 1))
    for q in range(4):
        dve.tensor_scalar(m.x[:, 4 * g + q, :], m.r4[:, q, :], m.mv4[:, q, 0:1], m.rs4[:, q:q + 1],
                          ALU.subtract, ALU.mult).then_inc(L.s("x_written"), 1)


def group_pool(pool, m, L):
    with pool.Fori(0, GROUPS) as g:
        pool.wait_ge(*L.after("var_ready", g + 1))
        pool.tensor_tensor(m.rs4[:, :], m.va4[:, :], m.mhalf[:, 0:4], ALU.pow).then_inc(L.s("rstd_ready"), 1)


def group_places(m, ar):
    m.xs, m.xsT, m.r4 = ar.take([4, D]), ar.take([2, 512]), ar.take([4, D])
    m.bn4, m.mv4, m.va4, m.rs4 = ar.take([4, 6]), ar.take([4, 2]), ar.take([4]), ar.take([4])



FI = 1024 // P


def l8_names():
    n = per_tile(*TILE4)
    n.update({k: GROUPS for k in ("var_ready", "rstd_ready", "xs_copied", "xsT_ready", "xsT_kept", "y_ready")})
    n.update({k: GROUPS * FI for k in ("gu_ready", "tanh_ready", "silu_ready", "h_kept")})
    return n


def l8_places(m, ar):
    group_places(m, ar)
    m.th, m.sg, m.hT = ar.take([2, 512]), ar.take([2, 512]), ar.take([FI, 512])


def l8_pe(pe, m, L):
    w = m.w
    pe.wait_ge(m.s_w[8], 16 * m.n_w[8])
    with pe.Fori(0, GROUPS) as g:
        pe_group_T(pe, m, L, g, [m.flat(6), m.flat(7)])
        pe.wait_ge(*L.after("xsT_kept", g + 1))

        def gate_up(c):
            if c >= 2:
                pe.wait_ge(*L.after("h_kept", FI * g + c - 1))
            for side in range(2):
                for k in range(2):
                    ins = pe.matmul(m.flat(2 * side + c % 2), w["l8_gu"][:, k, side * 1024 + c * P:side * 1024 + (c + 1) * P],
                                    m.xsT[:, k, :], start=(k == 0), stop=(k == 1))
            ins.then_inc(L.s("gu_ready"), 1)

        def down(c):
            pe.wait_ge(*L.after("h_kept", FI * g + c + 1))
            for q in range(4):
                ins = pe.matmul(m.flat(4 + q // 2)[:, (q % 2) * D:(q % 2 + 1) * D], m.hT[:, c, q * P:(q + 1) * P],
                                w["l8_down"][:, c, :], start=(c == 0 and q % 2 == 0), stop=(c == FI - 1), skip_group_check=True)
            return ins

        for c in range(FI):
            gate_up(c)
            if c >= 1:
                down(c - 1)
        down(FI - 1).then_inc(L.s("y_ready"), 1)


def l8_act(act, m, L):
    with act.Fori(0, GROUPS) as g:
        act_group_copy(act, m, L, g)
        act_group_T(act, m, L, g, [m.flat(6), m.flat(7)])
        for c in range(FI):
            act.wait_ge(*L.after("gu_ready", FI * g + c + 1))
            act.activation(m.th[:, c % 2, :], m.flat(c % 2), ACT.Tanh, scale=0.5).then_inc(L.s("tanh_ready"), 1)


def l8_dve(dve, m, L):
    with dve.Fori(0, GROUPS) as g:
        for c in range(FI):
            dve.wait_ge(*L.after("tanh_ready", FI * g + c + 1))
            dve.scalar_tensor_tensor(m.sg[:, c % 2, :], m.th[:, c % 2, :], 1.0, m.flat(c % 2), ALU.add, ALU.mult)\
               .then_inc(L.s("silu_ready"), 1)
            dve.wait_ge(*L.after("silu_ready", FI * g + c + 1))
            dve.scalar_tensor_tensor(m.hT[:, c, :], m.sg[:, c % 2, :], 0.5, m.flat(2 + c % 2), ALU.mult, ALU.mult)\
               .then_inc(L.s("h_kept"), 1)
        dve.wait_ge(*L.after("y_ready", g + 1))
        dve_norm4(dve, m, L, g, lambda q: m.flat(4 + q // 2)[:, (q % 2) * D:(q % 2 + 1) * D])



ROUNDS = 2


def l10_names():
    n = per_tile(*TILE, "xT_ready", "oT_ready", "oT_kept", "y_ready")
    n.update({k: ROUNDS * NT for k in ("qm_ready", "scores_ready", "max_ready", "shift_ready", "exp_ready", "sum_ready",
                                       "rinv_ready", "pT_ready", "pT_kept0", "pT_kept1", "o_ready", "o_kept")})
    n.update({"ctx_loaded0": 16 * NT, "ctx_loaded1": 16 * NT})
    return n


def l10_sync(sp, m, L):
    with sp.Fori(0, NT // 2) as i:
        for j in range(2):
            T = 2 * i + j
            sp.wait_ge(*L.after("x_written", T - 1))
            sp.dma_start(m.cb[:, j, :], m.ctx_tiles[T]).then_inc(L.s("ctx_loaded%d" % j), 16)
            sp.dma_start(m.kT[:, j], m.dram["ctxT32"][:, :, bass.ds(T * P, P)]).then_inc(L.s("ctx_loaded%d" % j), 16)


def l10_pe(pe, m, L):
    pe.wait_ge(m.s_w[10], 16 * m.n_w[10])
    with pe.Fori(0, NT // 2) as i:
        pe_xT(pe, m, L, i)
        for f in range(ROUNDS):
            for j in range(2):
                n = 4 * i + 2 * f + j
                pe.wait_ge(*L.after("qm_ready", n + 1))
                pe.wait_ge(*L.after("ctx_loaded%d" % j, 32 * (i + 1)))
                if f:
                    pe.wait_ge(*L.after("o_kept", n - 1))
                for g in range(2):
                    rows = slice(64 * g, 64 * g + 64)
                    for pp in range(4):
                        for b in range(2):
                            at = (pp * 2 + b) * S
                            ins = pe.matmul(m.bank(j, g)[:, at:at + S],
                                            m.qm8[rows, j, b, 2 * pp:2 * pp + 2, :].rearrange("p e s -> p (e s)"),
                                            m.kT[rows, j, f, b * S:(b + 1) * S], start=True, stop=True)
                ins.then_inc(L.s("scores_ready"), 1)
            for j in range(2):
                n = 4 * i + 2 * f + j
                pe.wait_ge(*L.after("exp_ready", n + 1))
                for u in range(8):
                    ins = pe.transpose(m.bank(j, u // 4)[:, (u % 4) * P:(u % 4 + 1) * P], m.pr[:, j, u * P:(u + 1) * P], m.ident[:])
                ins.then_inc(L.s("pT_ready"), 1)
            for j in range(2):
                n = 4 * i + 2 * f + j
                pe.wait_ge(*L.after("pT_kept0", n + 1))
                pe.wait_ge(*L.after("pT_kept1", n + 1))
                for u in range(8):
                    kv = (f * 8 + u) // 2
                    for b in range(2):
                        rows = slice(64 * b, 64 * b + 64)
                        ins = pe.matmul(m.o3bank(j, b)[:, u * 8:(u + 1) * 8], m.pT[rows, j, u * P:(u + 1) * P],
                                        m.cb[rows, j, kv * 8:(kv + 1) * 8], start=True, stop=True)
                ins.then_inc(L.s("o_ready"), 1)
        for j in range(2):
            pe.wait_ge(*L.after("o_kept", 4 * i + 2 + j + 1))
            for b in range(2):
                ins = pe.transpose(m.bank(j, 1)[:, b * P:(b + 1) * P], m.o[:, j, b * P:(b + 1) * P], m.ident[:])
            ins.then_inc(L.s("oT_ready"), 1)
        pe_out(pe, m, L, i, m.w["l10_perm"])


def l10_act(act, m, L):
    with act.Fori(0, NT // 2) as i:
        for f in range(ROUNDS):
            for j in range(2):
                n = 4 * i + 2 * f + j
                act.wait_ge(*L.after("shift_ready", n + 1))
                act.activation(m.pr[:, j, :], m.pr[:, j, :], ACT.Exp).then_inc(L.s("exp_ready"), 1)
            for j in range(2):
                n = 4 * i + 2 * f + j
                act.wait_ge(*L.after("pT_ready", n + 1))
                act.copy(m.pT[:, j, 0:512], m.bank(j, 0)).then_inc(L.s("pT_kept0"), 1)
        act_oT(act, m, L, i)


def l10_dve(dve, m, L):
    w = m.w
    dve.wait_ge(m.s_w[10], 16 * m.n_w[10])
    with dve.Fori(0, NT // 2) as i:
        for f in range(ROUNDS):
            for j in range(2):
                n = 4 * i + 2 * f + j
                dve.wait_ge(*L.after("xT_ready", 2 * i + j + 1))
                if f:
                    dve.wait_ge(*L.after("scores_ready", n - 1))
                dve.tensor_tensor(m.qm8[:, j], m.work(j)[:, f * P:(f + 1) * P].rearrange("p (b s) -> p b s", b=2).unsqueeze(2)
                                  .to_broadcast([P, 2, 8, S]),
                                  w["l10_hmask"][:, :].unsqueeze(1).unsqueeze(3).to_broadcast([P, 2, 8, S]), ALU.mult)\
                   .then_inc(L.s("qm_ready"), 1)
            for j in range(2):
                n = 4 * i + 2 * f + j
                dve.wait_ge(*L.after("scores_ready", n + 1))
                for g in range(2):
                    ins = dve.tensor_reduce(m.mx[:, j, g * 8:(g + 1) * 8], m.bank(j, g).rearrange("p (r k) -> p r k", k=S),
                                            AX.X, ALU.max)
                ins.then_inc(L.s("max_ready"), 1)
            for j in range(2):
                n = 4 * i + 2 * f + j
                dve.wait_ge(*L.after("max_ready", n + 1))
                for g in range(2):
                    ins = dve.tensor_tensor(m.pr[:, j, g * 512:(g + 1) * 512].rearrange("p (r k) -> p r k", k=S),
                                            m.bank(j, g).rearrange("p (r k) -> p r k", k=S),
                                            m.mx[:, j, g * 8:(g + 1) * 8].unsqueeze(2).to_broadcast([P, 8, S]), ALU.subtract)
                ins.then_inc(L.s("shift_ready"), 1)
            for j in range(2):
                n = 4 * i + 2 * f + j
                dve.wait_ge(*L.after("exp_ready", n + 1))
                dve.tensor_reduce(m.sums[:, j, :], m.pr[:, j, :].rearrange("p (r k) -> p r k", k=S), AX.X, ALU.add)\
                   .then_inc(L.s("sum_ready"), 1)
            for j in range(2):
                n = 4 * i + 2 * f + j
                dve.wait_ge(*L.after("sum_ready", n + 1))
                dve.reciprocal(m.rinv[:, j, :], m.sums[:, j, :]).then_inc(L.s("rinv_ready"), 1)
            for j in range(2):
                n = 4 * i + 2 * f + j
                dve.wait_ge(*L.after("pT_ready", n + 1))
                dve.tensor_copy(m.pT[:, j, 512:1024], m.bank(j, 1)).then_inc(L.s("pT_kept1"), 1)
            for j in range(2):
                n = 4 * i + 2 * f + j
                dve.wait_ge(*L.after("o_ready", n + 1))
                dve.wait_ge(*L.after("rinv_ready", n + 1))
                for b in range(2):
                    ins = dve.tensor_tensor(m.o[:, j, b * P + f * 64:b * P + f * 64 + 64].rearrange("p (u d) -> p u d", u=8),
                                            m.o3bank(j, b)[:, 0:64].rearrange("p (u d) -> p u d", u=8),
                                            m.rinv[:, j, :].rearrange("p (u b) -> p u b", b=2)[:, :, b].unsqueeze(2)
                                            .to_broadcast([P, 8, 8]), ALU.mult)
                ins.then_inc(L.s("o_kept"), 1)
        dve_residual_norm(dve, m, L, i, "y_ready", lambda j: m.work(j)[:, 0:D])



LAYER_PARTS = {
    0: (l0_names, l0_places, {"tensor": l0_pe, "scalar": l0_act, "vector": l0_dve, "gpsimd": l0_pool}),
    1: (l1_names, l1_places, {"sync": l1_sync, "tensor": l1_pe, "scalar": l1_act, "vector": l1_dve, "gpsimd": l1_pool}),
    3: (l3_names, l3_places, {"tensor": l3_pe, "scalar": l3_act, "vector": l3_dve, "gpsimd": plain_pool}),
    4: (l4_names, l4_places, {"sync": l4_sync, "tensor": l4_pe, "scalar": l4_act, "vector": l4_dve, "gpsimd": plain_pool}),
    5: (l5_names, l5_places, {"tensor": l5_pe, "scalar": l5_act, "vector": l5_dve, "gpsimd": plain_pool}),
    8: (l8_names, l8_places, {"tensor": l8_pe, "scalar": l8_act, "vector": l8_dve, "gpsimd": group_pool}),
    9: (l9_names, l9_places, {"tensor": l9_pe, "scalar": l9_act, "vector": l9_dve, "gpsimd": plain_pool}),
    10: (l10_names, l10_places, {"sync": l10_sync, "tensor": l10_pe, "scalar": l10_act, "vector": l10_dve, "gpsimd": plain_pool}),
    2: (l2_names, l2_places, {"sync": l2_sync, "tensor": l2_pe, "scalar": l2_act, "vector": l2_dve, "gpsimd": l2_pool}),
    11: (l11_names, l11_places, {"sync": l11_sync, "tensor": l11_pe, "scalar": l11_act, "vector": l11_dve, "gpsimd": l11_pool}),
    7: (l7_names, l7_places, {"sync": l7_sync, "tensor": l7_pe, "scalar": l7_act, "vector": l7_dve, "gpsimd": l7_pool}),
    6: (l6_names, l6_places, {"sync": l6_sync, "tensor": l6_pe, "scalar": l6_act, "vector": l6_dve, "gpsimd": l6_pool}),
}
SCRATCH = {"x_rows": (TOK, D), "slot_x": (2 * TOK, D), "slot_y": (TOK, D)}
WORK_WORDS = 27500
WEIGHT_WORDS = 6900


def layer_of(name):
    head = name[1:name.find("_")]
    return int(head) if name[0] == "l" and head.isdigit() else None


def build(nc, dram, out, scratch):
    with ExitStack() as ctx:
        def sb(name, shape, dt=F32):
            return ctx.enter_context(nc.sbuf_tensor(name, shape, dt))

        x_sb, ident, mhalf, ones_row, pause = (sb("x", [P, NT, D]), sb("ident", [P, P]), sb("mhalf", [P, 16]),
                                               sb("ones_row", [1, P]), sb("pause", [P, 1]))
        work_sb = sb("work", [P, WORK_WORDS])
        weight_sb = [sb("weights%d" % n, [P, WEIGHT_WORDS]) for n in range(2)]
        const_sb = {n[2:]: sb("sb_" + n, list(ap.shape)) for n, ap in dram.items() if n.startswith("c_")}
        psum = ctx.enter_context(nc.psum_tensor("banks", [P, 8, 512], F32))
        s_const = ctx.enter_context(nc.semaphore("constants_loaded"))
        s_out = ctx.enter_context(nc.semaphore("out_stored"))
        s_wt = [ctx.enter_context(nc.semaphore("weights_loaded%d" % n)) for n in range(2)]

        first, *stages = stage_semaphores(nc, ctx, [{"x_written": 16}] + [LAYER_PARTS[n][0]() for n in LAYERS])
        plan = []
        n_loaded = [0, 0]
        for at, layer in enumerate(LAYERS):
            _, places, parts = LAYER_PARTS[layer]
            m = Mem()
            m.x, m.ident, m.mhalf, m.ones_row, m.pause = x_sb, ident, mhalf, ones_row, pause
            m.bank = lambda j, n: psum[:, 4 * j + n]
            m.work = lambda j: psum[:, 4 * j + 2]
            m.proj = lambda j: psum[:, 4 * j + 3]
            m.obank = lambda j, b: psum[:, 4 * j + (2 if b == 0 else 0)]
            m.o3bank = lambda j, b: psum[:, 4 * j + (3 if b == 0 else 0)]
            m.flat = lambda n: psum[:, n]
            m.psum = psum
            places(m, Arena(work_sb))
            m.dram, m.scratch = dram, scratch
            m.ctx_tiles, m.ctxT_d = Tiles(dram["ctx"]), dram["ctxT"]
            m.s_const = s_const
            m.w = dict(const_sb)
            m.blk, m.tril, m.dist, m.causal = (m.w[k] for k in ("blk", "tril", "dist", "causal"))
            weights = Arena(weight_sb[at % 2])
            m.loads = []
            for name, ap in dram.items():
                if layer_of(name) == layer:
                    m.w[name] = weights.take(list(ap.shape[1:]), ap.shape[0])
                    m.loads.append(name)
            m.gam = m.w.get("l0_gam")
            if layer == 2:
                m.w["l2_ring"] = weights.take([2, 2560])
            if layer == 6:
                m.w["l6_in"], m.w["l6_out"] = weights.take([4, W_IN]), weights.take([4, W_OUT])
            if layer == 11:
                m.w["l11_ring"] = weights.take([2, 2176])
            n_loaded[at % 2] += len(m.loads)
            m.s_w, m.n_w = {layer: s_wt[at % 2]}, {layer: n_loaded[at % 2]}
            plan.append((parts, stages[at], m))
        n_const = len(const_sb) + 1
        block = ctx.enter_context(nc.Block())

        def load_weights(sp, at):
            m = plan[at][2]
            for name in m.loads:
                sp.dma_start(m.w[name], dram[name]).then_inc(s_wt[at % 2], 16)

        def run(eng, which):
            eng.wait_ge(*first.after("x_written", 16))
            eng.wait_ge(s_const, 16 * n_const + 2)
            for at, (parts, L, m) in enumerate(plan):
                eng.wait_ge(*L.after("x_written", 0))
                if which == "sync" and at + 1 < len(plan):
                    load_weights(eng, at + 1)
                if which in parts:
                    parts[which](eng, m, L)

        @block.sync
        def _(sp):
            sp.dma_start(x_sb[:, :, :], dram["x"].rearrange("(t p) d -> p t d", p=P)).then_inc(first.s("x_written"), 16)
            sp.dma_start(ident[:, :], dram["identity"]).then_inc(s_const, 16)
            for name in const_sb:
                sp.dma_start(const_sb[name][:], dram["c_" + name]).then_inc(s_const, 16)
            load_weights(sp, 0)
            run(sp, "sync")
            sp.wait_ge(*plan[-1][1].after("x_written", NT))
            sp.dma_start(out.rearrange("(t p) d -> p t d", p=P), x_sb[:, :, :]).then_inc(s_out, 16)
            sp.wait_ge(s_out, 16)
            for n in range(2):
                if n_loaded[n]:
                    sp.wait_ge(s_wt[n], 16 * n_loaded[n])

        @block.gpsimd
        def _(pool):
            pool.memset(mhalf[:, :], -0.5).then_inc(s_const, 1)
            pool.memset(ones_row[:, :], 1.0).then_inc(s_const, 1)
            run(pool, "gpsimd")

        @block.tensor
        def _(pe):
            run(pe, "tensor")

        @block.scalar
        def _(act):
            run(act, "scalar")

        @block.vector
        def _(dve):
            run(dve, "vector")

        for parts, L, m in plan:
            assert L.used == set(L.base), (sorted(set(L.base) - L.used), sorted(L.used - set(L.base)))


class Tiles:

    def __init__(self, ap):
        self.ap = ap

    def __getitem__(self, t):
        return self.ap[bass.ds(t * P, P), :]


def rope_angles(length, dim):
    inv = (1.0 / 10000.0 ** (np.arange(0, dim, 2, dtype=np.float32) / np.float32(dim))).astype(np.float32)
    return (np.arange(length, dtype=np.float32)[:, None] * inv[None, :]).astype(np.float32)


def constants():
    c = {"identity": np.eye(P, dtype=np.float32)}
    d = np.arange(P)
    one = ((d[:, None] // HD) % 4 == np.arange(4)[None, :]).astype(np.float32)
    c["c_hmask_one"] = one
    c["c_hmask_q"] = one * np.float32(1.0 / np.sqrt(HD))
    q = (d % S)[:, None]
    k = np.arange(S)[None, :]
    c["c_tril"] = (q >= k).astype(np.float32)
    c["c_causal"] = np.where(q >= k, 0.0, NEG).astype(np.float32)
    c["c_dist"] = np.maximum(q - k, 0).astype(np.float32)
    c["c_blk"] = ((d[:, None] // S) == (d[None, :] // S)).astype(np.float32) / np.float32(S * HD)
    a = rope_angles(S, HD)
    pos = d % S
    c["l1_cos"] = np.concatenate([np.cos(a), np.cos(a)], 1)[pos]
    c["l1_sin"] = np.concatenate([-np.sin(a), np.sin(a)], 1)[pos]
    a = rope_angles(S, D).T
    c["l3_cos"] = np.cos(a)
    c["l3_sin"] = np.concatenate([-np.sin(a), np.sin(a)], 1)
    theta = (10000.0 ** (-np.arange(0, HD, 2, dtype=np.float32) / np.float32(HD))).astype(np.float32)
    f = (np.arange(S, dtype=np.float32)[:, None] * theta[None, :]).T
    e = d % HD
    c["l9_cos"] = np.where((e < 8)[:, None], np.cos(f)[e % 8], 1.0)
    c["l9_sin"] = np.where((e < 8)[:, None], -np.sin(f)[e % 8], 0.0)
    c["l10_hmask"] = ((d[:, None] // 8) % 8 == np.arange(8)[None, :]) * np.float32(1.0 / np.sqrt(np.float32(8)))
    perm = np.zeros((P, 2, D))
    for h2 in range(2):
        perm[d, h2, (d // 8 * 2 + h2) * 8 + d % 8] = 1
    c["l10_perm"] = perm
    s = d % S
    a = np.repeat(rope_angles(S, QD), 2, axis=1).T
    c["l7_qtab"] = np.stack([np.cos(a[:QH]), -np.sin(a[:QH]), np.cos(a[QH:]), np.sin(a[QH:])], 1)
    a = np.repeat(rope_angles(S, DC), 2, axis=1)
    c["l7_kcos"] = np.cos(a)[pos]
    c["l7_ksin"] = np.concatenate([-np.sin(a[:, :32]), np.sin(a[:, 32:])], 1)[pos]
    c["l6_upto"] = (d % S)[:, None] <= np.arange(S)[None, :]
    c["l6_after"] = ((d // S)[:, None] == (d // S)[None, :]) & ((d % S)[:, None] > (d % S)[None, :])
    c["l6_mask"] = 0.25 * c["l6_upto"]
    c["l2_before"] = s[:, None] < s[None, :]
    c["l2_same"] = s[:, None] == s[None, :]
    c["l2_first_half"] = (s[:, None] == s[None, :]) & (d[:, None] < S) & (d[None, :] >= S)
    c["l2_iota"] = np.broadcast_to(d[None, :], (P, P))
    c["l2_token"] = d[:, None] + P * np.arange(NT)[None, :]
    c["l2_tile_start"] = np.broadcast_to(P * np.arange(NT)[None, :], (P, NT))
    c["l2_own"] = d[:, None] // C2 == np.arange(4)[None, :]
    c["l11_before"] = d[:, None] < d[None, :]
    c["l11_ones"] = np.ones((P, P))
    c["l11_iota"] = np.broadcast_to(np.arange(E11)[None, :], (P, E11))
    c["l11_overflow"] = TOK + c["l2_token"]
    return {n: np.ascontiguousarray(v, dtype=np.float32) for n, v in c.items()}


def layout(a):
    def kn(w):
        return w.reshape(-1, P, w.shape[1]).transpose(1, 0, 2)

    def cols(v):
        return v.reshape(-1, P).T

    def h2_major(w):
        return w.reshape(8, 2, HD, w.shape[1]).transpose(0, 2, 1, 3).reshape(P, 2, w.shape[1])

    def h2_cols(w):
        return w.reshape(w.shape[0], 8, 2, HD).transpose(0, 2, 1, 3).reshape(w.shape[0], D)

    def evens_first(w):
        return w.reshape(w.shape[0], H, 8, 2).transpose(0, 1, 3, 2).reshape(w.shape[0], D)

    def partner(w):
        return w.reshape(w.shape[0], H, 2, 8)[:, :, ::-1].reshape(w.shape[0], D)

    def all_rows(v):
        return np.broadcast_to(v.reshape(1, -1), (P, v.size))

    o = {"x": a["x"].reshape(TOK, D), "ctx": a["ctx_512"].reshape(TOK, DC), "ctxT": a["ctx_512"].reshape(TOK, DC).T}
    o["l0_wq"], o["l0_wk"], o["l0_wv"] = (kn(a["L0_attn_" + n]) for n in ("wq", "wk", "wv"))
    o["l0_wg"] = kn(h2_cols(a["L0_attn_wg"]))
    o["l0_wo"] = h2_major(a["L0_attn_wo"])
    o["l0_bq"], o["l0_bk"] = cols(a["L0_attn_bq"]), cols(a["L0_attn_bk"])
    o["l0_bg"], o["l0_gnw"], o["l0_gnb"] = (cols(h2_cols(a["L0_attn_" + n].reshape(1, D))) for n in ("bg", "gn_w", "gn_b"))
    o["l0_bv"], o["l0_bo"] = (a["L0_attn_" + n].reshape(1, D) for n in ("bv", "bo"))
    o["l0_gam"] = np.repeat(a["L0_attn_gamma"].reshape(8, 2).T, S, axis=0)
    o["l1_qw"], o["l1_kw"] = all_rows(a["L0_xattn_q_norm_w"]), all_rows(a["L0_xattn_k_norm_w"])
    o["l1_wo"] = h2_major(a["L0_xattn_w_out"].T)
    o["l3_wq"], o["l3_wk"], o["l3_wv"] = (kn(a["L1_attn_" + n].T) for n in ("Wq", "Wk", "Wv"))
    o["l3_wo"] = h2_major(a["L1_attn_Wo"].T)
    o["l3_gate"] = np.repeat(np.repeat(a["L1_attn_gate"].reshape(8, 2).T, 2, axis=1), S, axis=0)
    o["l4_wq"] = kn(a["L1_xattn_Wq"].T)
    o["l4_wkv"] = a["L1_xattn_Wkv_expand"].T
    o["l4_wo"] = h2_major(a["L1_xattn_Wout"].T)
    o["l5_w"] = kn(a["L1_ffn_weight"])
    o["l5_b"] = a["L1_ffn_bias"].reshape(1, D)
    wq, wk = evens_first(a["L3_attn_wq"].T), evens_first(a["L3_attn_wk"].T)
    bq, bk = (evens_first(a["L3_attn_" + n].reshape(1, D)) for n in ("bq", "bk"))
    o["l9_wq"], o["l9_wqp"], o["l9_wk"], o["l9_wkp"] = kn(wq), kn(partner(wq)), kn(wk), kn(partner(wk))
    o["l9_bq"] = np.concatenate([cols(bq), cols(partner(bq))], 1)
    o["l9_bk"] = np.concatenate([cols(bk), cols(partner(bk))], 1)
    o["l9_wv"], o["l9_bv"] = kn(a["L3_attn_wv"].T), a["L3_attn_bv"].reshape(1, D)
    o["l8_gu"] = kn(a["L2_ffn_w_gate_up"].T)
    o["l8_down"] = kn(a["L2_ffn_w_down"].T)
    o["l7_wq"] = a["L2_xattn_Wq"].reshape(H, P, D).transpose(1, 0, 2)
    o["l7_krT"], o["l7_kv"] = a["L2_xattn_W_kr"].transpose(2, 0, 1), a["L2_xattn_w_kc_kv"].transpose(1, 0, 2)
    o["raw_kcq"], o["raw_qrT"] = a["L2_xattn_w_kc_q"].transpose(1, 0, 2), a["L2_xattn_W_qr"].transpose(2, 0, 1)
    o["raw_woT"] = a["L2_xattn_Wo"].T.reshape(H, P, D).transpose(1, 0, 2)
    w = a["L2_attn_in_proj_w"]

    def by_step(v):
        return v.reshape(2, P, CT, P).transpose(2, 1, 0, 3).reshape(CT, P, 2 * P)

    conv = np.concatenate([a["L2_attn_conv_w"], a["L2_attn_conv_b"].reshape(-1, 1)], 1)
    o["mamba_in"] = np.concatenate([by_step(w[:, DI:2 * DI]), by_step(w[:, 0:DI]), conv[0:DI].reshape(CT, P, 5)], 2)
    per_channel = np.repeat(a["L2_attn_D_param"], 64).reshape(CT, P, 1)
    o["mamba_out"] = np.concatenate([a["L2_attn_out_proj_w"].reshape(CT, P, D), per_channel,
                                     a["L2_attn_norm_w"].reshape(CT, P, 1)], 2)
    o["l6_wbc"], o["l6_wdt"] = kn(w[:, 2 * DI:2 * DI + 2 * P]), kn(w[:, 2 * DI + 2 * P:])
    o["l6_cbc"] = conv[DI:].reshape(2, P, 5).transpose(1, 0, 2)
    o["l6_dtb"], o["l6_alog"] = all_rows(a["L2_attn_dt_bias"]), all_rows(a["L2_attn_A_log"])
    o["l2_rw"] = kn(a["L0_ffn_router_w"].T)
    wv = np.stack([a["L0_ffn_w1"], a["L0_ffn_v1"]], 1).reshape(NS, 4, 2, F2, 2, P)
    o["moe_w1v1"] = wv.transpose(0, 5, 1, 2, 4, 3).reshape(NS, P, 1536)
    o["moe_w2"] = a["L0_ffn_w2"].reshape(NS, 4, F2, D).transpose(0, 2, 1, 3).reshape(NS, F2, 1024)
    o["l11_wg"], o["l11_sw1"], o["l11_sw3"] = kn(a["L3_ffn_Wg"]), kn(a["L3_ffn_sw1"]), kn(a["L3_ffn_sw3"])
    o["l11_sw2a"], o["l11_sw2b"] = kn(a["L3_ffn_sw2"][0:256]), a["L3_ffn_sw2"][256:]
    for n in ("w1", "w3"):
        o["moe8_" + n] = a["L3_ffn_" + n.upper()].reshape(E11, 2, P, F11).transpose(0, 2, 1, 3).reshape(E11, P, 704)
    o["moe8_w2a"] = a["L3_ffn_W2"][:, 0:256].reshape(E11, 2, P, D).transpose(0, 2, 1, 3).reshape(E11, P, 512)
    o["moe8_w2b"] = a["L3_ffn_W2"][:, 256:]
    t = a["ctx_512"].reshape(TOK, 8, 1, 8)
    o["ctxT32"] = np.broadcast_to(t, (TOK, 8, 4, 8)).reshape(TOK, 2, P).transpose(2, 1, 0)
    o["l9_wo"], o["l9_bo"] = h2_major(a["L3_attn_wo"].T), a["L3_attn_bo"].reshape(1, D)
    return {n: np.ascontiguousarray(v) for n, v in o.items()}


def kernel(**inputs):
    import concourse.bacc as bacc
    from concourse.bass_utils import run_bass_kernel_spmd

    arrays = {**constants(), **layout({n: np.asarray(v) for n, v in inputs.items()})}
    keep = ["l%d_" % n for n in LAYERS]
    arrays = {n: v for n, v in arrays.items() if layer_of(n) is None or any(n.startswith(k) for k in keep)}
    nc = bacc.Bacc("TRN2", target_bir_lowering=False, num_devices=1)
    dram = {n: nc.dram_tensor("in_" + n, v.shape, F32, kind="ExternalInput").ap() for n, v in arrays.items()}
    out = nc.dram_tensor("out_x", (TOK, D), F32, kind="ExternalOutput").ap()
    scratch = {n: nc.dram_tensor(n, shape, F32, kind="Internal").ap() for n, shape in SCRATCH.items()}
    build(nc, dram, out, scratch)
    r = run_bass_kernel_spmd(nc, [{"in_" + n: v for n, v in arrays.items()}], core_ids=[0])
    return np.asarray(r.results[0]["out_x"]).reshape(B, S, D)
```

```python
from contextlib import ExitStack

import numpy as np

import concourse.bass as bass
from concourse import mybir

LAYERS = (0, 1, 2, 3, 4, 5, 6, 7, 8, 9, 10, 11)

F32 = mybir.dt.float32
ALU = mybir.AluOpType
ACT = mybir.ActivationFunctionType
AX = mybir.AxisListType

B, S, D, DC = 32, 64, 256, 64
TOK = B * S
P = 128
NT = TOK // P
H, HD = 16, 16
LN_EPS = 1e-5
NEG = -1e30
FOUR_CHAINS = (0, 1, 4, 9, 10)


class Layer:

    def __init__(self, sems, base):
        self.sems, self.base, self.used = sems, base, set()

    def s(self, name):
        assert name in self.base, name
        self.used.add(name)
        return self.sems[name]

    def after(self, name, n):
        return self.sems[name], self.base[name] + n


OWN_DMA = ("gathered", "scattered", "fetched", "slot_y_out0", "slot_y_out1", "ctx_loaded0", "ctx_loaded1")


def stage_semaphores(nc, ctx, layers):
    slots, of = [], {}
    for names in layers:
        free = [slot for slot in slots if not any(n in names or n in OWN_DMA for n in slot)]
        for name in names:
            if name not in of:
                slot = next((slot for slot in free if name not in OWN_DMA and not any(name in other and any(n in other for n in slot)
                                                              for other in layers)), None)
                if slot is None:
                    slots.append([name])
                    of[name] = slots[-1]
                else:
                    slot.append(name)
                    free.remove(slot)
                    of[name] = slot
    sem = {id(slot): ctx.enter_context(nc.semaphore("_or_".join(slot))) for slot in slots}
    value = {id(slot): 0 for slot in slots}
    made = []
    for names in layers:
        made.append(Layer({n: sem[id(of[n])] for n in names}, {n: value[id(of[n])] for n in names}))
        for n, count in names.items():
            value[id(of[n])] += count
    return made


class Mem:
    pass


class Arena:

    def __init__(self, tensor):
        self.tensor, self.at = tensor, 0

    def take(self, dims, rows=P):
        n = int(np.prod(dims))
        assert self.at + n <= self.tensor.shape[1], (self.at, n, self.tensor.shape)
        ap = self.tensor[0:rows, self.at:self.at + n]
        self.at += n
        if len(dims) > 1:
            names = "abcdef"[:len(dims)]
            ap = ap.rearrange("p (" + " ".join(names) + ") -> p " + " ".join(names),
                              **{k: v for k, v in zip(names[1:], dims[1:])})
        return ap



TILE = ("x_written", "x_copied", "r_kept", "stats_ready", "aggr_ready", "var_ready", "rstd_ready")
CORE = TILE + ("masked_ready", "plain_kept", "scores_ready", "pT_ready", "pT_kept0", "pT_kept1", "v_kept", "o_ready",
               "o_kept", "oT_ready", "oT_kept", "y_ready")
SOFTMAX = ("max_ready", "shift_ready", "exp_ready", "sum_ready", "rinv_ready")


def per_tile(*names):
    return {n: NT for n in names}


def attn_places(m, ar):
    m.xc, m.xT, m.r = ar.take([m.chains, D]), ar.take([m.chains, 2, P]), ar.take([m.chains, D])
    m.bn, m.stat = ar.take([m.chains, 6]), ar.take([m.chains, 16])
    m.km, m.qT, m.kT = ar.take([m.chains, 2, 2, 4, S]), ar.take([m.chains, 2, P]), ar.take([m.chains, 2, P])
    m.pr, m.pT = ar.take([m.chains, 1024]), ar.take([m.chains, 1024])
    m.o, m.oT = ar.take([m.chains, D]), ar.take([m.chains, D])
    m.mx, m.sums, m.rinv = ar.take([m.chains, 16]), ar.take([m.chains, 16]), ar.take([m.chains, 16])
    m.cb = ar.take([m.chains, DC])


def full_places(m, ar, twice=2 * 2 * P):
    attn_places(m, ar)
    m.vd, place = ar.take([m.chains, 2, 8, 2, HD]), ar.take([m.chains, twice])
    if twice == 2 * DC:
        m.cb2 = place
    elif twice == 3 * P:
        m.ctxT = place[0:DC]
    else:
        m.xTd = place.rearrange("p j (h b t) -> p j h b t", h=2, b=2)


def l0_places(m, ar):
    full_places(m, ar)
    m.o2 = m.r
    m.s1, m.lng, m.decay = ar.take([m.chains, 16]), ar.take([H]), ar.take([H * S])
    m.gT, m.gE = ar.take([m.chains, 2, P]), ar.take([m.chains, 2, P])


def l1_places(m, ar):
    full_places(m, ar, 2 * DC)
    m.vd_ctx = m.vd
    m.qn, m.qk = ar.take([m.chains, D + DC]), ar.take([m.chains, 2 * D])
    m.qt1, m.qt2 = m.pr[:, :, 0:D + DC], m.pr[:, :, 512:512 + D + DC]


def l3_places(m, ar):
    full_places(m, ar)
    m.kf, m.pr2 = ar.take([m.chains, 2, 2, 4, S]), ar.take([m.chains, 1024])
    m.rt1, m.rt2, m.ft = ar.take([m.chains, 2 * D]), ar.take([m.chains, 2 * D]), ar.take([m.chains, 2 * D])
    m.lsum, m.linv, m.gsig, m.grest = ar.take([m.chains, 16]), ar.take([m.chains, 16]), ar.take([16]), ar.take([16])


def l4_places(m, ar):
    full_places(m, ar, 3 * P)


def l5_places(m, ar):
    attn_places(m, ar)
    m.ta, m.tb, m.tern, m.ternT, m.tstat = (ar.take([m.chains, D]), ar.take([m.chains, D]), ar.take([m.chains, D]), ar.take([m.chains, D]),
                                            ar.take([m.chains, 4]))


def l9_places(m, ar):
    full_places(m, ar)
    m.rt1, m.rt2 = m.pr[:, :, 0:2 * D], m.pr[:, :, 2 * D:4 * D]


def l10_places(m, ar):
    full_places(m, ar, 2 * DC)
    m.vd_ctx = m.vd.rearrange("p j b u e d -> p j (b u e d)").rearrange("p j (b u e d) -> p j b u e d", b=2, u=16, e=2)
    m.km8 = [m.km.rearrange("p j a b c s -> p j a (b c) s"), ar.take([m.chains, 2, 8, S])]


def pool_copy_x(pool, m, L, T, j):
    pool.wait_ge(*L.after("x_written", T + 1 - m.chains))
    pool.tensor_copy(m.xc[:, j, :], m.x[:, T, :]).then_inc(L.s("x_copied"), 1)


def act_copy_x(act, m, L, i):
    for j in range(m.chains):
        act.wait_ge(*L.after(m.chain_free, i + j + 1 - m.chains))
        act.copy(m.xc[:, j, :], m.x[:, bass.ds(i + j, 1), :].rearrange("p a d -> p (a d)")).then_inc(L.s("x_copied"), 1)


def pool_rstd(pool, m, L, T, j):
    pool.wait_ge(*L.after("var_ready", T + 1))
    pool.tensor_tensor(m.stat[:, j, 3:4], m.stat[:, j, 2:3], m.mhalf[:, 0:1], ALU.pow).then_inc(L.s("rstd_ready"), 1)


def dve_residual_norm(dve, m, L, i, y_name, y_of, scale_of=None):
    for j in range(m.chains):
        T = i + j
        dve.wait_ge(*L.after(y_name, T + 1))
        dve.wait_ge(*L.after("x_written", T + 1 - m.chains))
        dve.tensor_tensor(m.r[:, j, :], y_of(j), m.xc[:, j, :], ALU.add).then_inc(L.s("r_kept"), 1)
    dve_norm_tail(dve, m, L, i)


def dve_norm_tail(dve, m, L, i):
    for j in range(m.chains):
        T = i + j
        dve.wait_ge(*L.after("r_kept", T + 1))
        dve.bn_stats(m.bn[:, j, :], m.r[:, j, :]).then_inc(L.s("stats_ready"), 1)
    dve.wait_ge(*L.after("stats_ready", i + m.chains))
    dve.memset(m.pause[:, :], 0.0)
    for j in range(m.chains):
        dve.bn_aggr(m.stat[:, j, 0:2], m.bn[:, j, :]).then_inc(L.s("aggr_ready"), 1)
    for j in range(m.chains):
        T = i + j
        dve.wait_ge(*L.after("aggr_ready", T + 1))
        dve.tensor_scalar(m.stat[:, j, 2:3], m.stat[:, j, 1:2], LN_EPS, None, ALU.add).then_inc(L.s("var_ready"), 1)
    for j in range(m.chains):
        T = i + j
        dve.wait_ge(*L.after("rstd_ready", T + 1))
        dve.tensor_scalar(m.x[:, T, :], m.r[:, j, :], m.stat[:, j, 0:1], m.stat[:, j, 3:4],
                          ALU.subtract, ALU.mult).then_inc(L.s("x_written"), 1)


def pe_xT(pe, m, L, i):
    for j in range(m.chains):
        pe.wait_ge(*L.after("x_copied", i + j + 1))
        for h in range(2):
            ins = pe.transpose(m.work(j)[:, h * P:(h + 1) * P], m.xc[:, j, h * P:(h + 1) * P], m.ident[:])
        ins.then_inc(L.s("xT_ready"), 1)


def act_xT(act, m, L, i):
    for j in range(m.chains):
        act.wait_ge(*L.after("xT_ready", i + j + 1))
        act.copy(m.xT[:, j], m.work(j)[:, 0:D].rearrange("p (h t) -> p h t", h=2)).then_inc(L.s("xT_kept"), 1)


def pe_projT(pe, m, out, w, j):
    for h in range(2):
        for k in range(2):
            ins = pe.matmul(out[:, h * P:(h + 1) * P], w[:, k, h * P:(h + 1) * P], m.xT[:, j, k, :],
                            start=(k == 0), stop=(k == 1))
    return ins


def act_xT_twice(act, m, L, i):
    for j in range(m.chains):
        act.wait_ge(*L.after("xT_ready", i + j + 1))
        act.copy(m.xT[:, j], m.work(j)[:, 0:D].rearrange("p (h t) -> p h t", h=2))
        act.copy(m.xTd[:, j].rearrange("p h b (e s) -> p (h b) e s", e=2),
                 m.work(j)[:, 0:D].rearrange("p (a s) -> p a s", s=S).unsqueeze(2).to_broadcast([P, 4, 2, S]))\
           .then_inc(L.s("xT_kept"), 1)


def pe_v_twice(pe, m, j, w, bias=None):
    for b in range(2):
        out = m.work(j)[:, b * D:(b + 1) * D]
        for k in range(2):
            ins = pe.matmul(out, m.xTd[:, j, k, b, :], w[:, k, :], start=(k == 0), stop=(k == 1 and bias is None))
        if bias is not None:
            ins = pe.matmul(out, m.ones_row[0:1, :], bias, start=False, stop=True)
    return ins


def act_v_blocks(act, m, L, i):
    for j in range(m.chains):
        act.wait_ge(*L.after("v_ready", i + j + 1))
        for h2 in range(2):
            rows = slice(64 * h2, 64 * h2 + 64)
            ins = act.copy(m.vd[rows, j, :, :, h2, :],
                           m.work(j)[rows, :].rearrange("p (b u e d) -> p b u e d", b=2, u=8, e=2)[:, :, :, h2, :])
        ins.then_inc(L.s("v_kept"), 1)


def act_context_blocks(act, m, L, i, loaded):
    for j in range(m.chains):
        act.wait_ge(*loaded(i, j))
        for h2 in range(2):
            rows = slice(64 * h2, 64 * h2 + 64)
            for b in range(2):
                dst = m.vd_ctx[rows, j, b].rearrange("p (v c) e d -> p v c e d", c=2)[:, :, :, h2, :]
                kv, d = dst.shape[1], dst.shape[3]
                ins = act.copy(dst, m.cb2[rows, j, b * DC:(b + 1) * DC].rearrange("p (v d) -> p v d", d=d).unsqueeze(2)
                               .to_broadcast([64, kv, 2, d]))
        ins.then_inc(L.s("v_kept"), 1)


def pe_scores_full(pe, m, L, i):
    for j in range(m.chains):
        T = i + j
        pe.wait_ge(*L.after("masked_ready", T + 1))
        pe.wait_ge(*L.after("plain_kept", T + 1))
        pe.wait_ge(*L.after("v_kept", T + 1))
        pe_pause(pe, m, j, 1)
        pe_products(pe, m, j, 0, m.qT[:, j].rearrange("p h t -> p (h t)"), m.km).then_inc(L.s("scores_ready"), 1)


def pe_pause(pe, m, j, n):
    pe.matmul(m.bank(j, n)[0:32, 511:512], m.ident[:, 0:32], m.ident[:, 0:1], start=True, stop=True)


def pe_products(pe, m, j, bank, q, km):
    for g in range(2):
        rows = slice(64 * g, 64 * g + 64)
        for half in range(2):
            for b in range(2):
                ins = pe.matmul(m.bank(j, bank + g)[64 * b:64 * b + 64, half * 256:(half + 1) * 256],
                                q[rows, half * P + b * S:half * P + (b + 1) * S],
                                km[rows, j, half, b].rearrange("p e s -> p (e s)"), start=True, stop=True)
    return ins


def pe_pv_full(pe, m, L, i):
    for j in range(m.chains):
        T = i + j
        pe.wait_ge(*L.after("pT_kept0", T + 1))
        pe.wait_ge(*L.after("pT_kept1", T + 1))
        pe.wait_ge(*L.after("v_kept", T + 1))
        for u in range(8):
            for b in range(2):
                ins = pe.matmul(m.work(j)[64 * b:64 * b + 64, u * 32:(u + 1) * 32], m.pT[:, j, u * P + 64 * b:u * P + 64 * b + 64],
                                m.vd[:, j, b, u].rearrange("p e d -> p (e d)"), start=True, stop=True)
        ins.then_inc(L.s("o_ready"), 1)


def dve_o_full(dve, m, L, i, scaled=True):
    for j in range(m.chains):
        T = i + j
        dve.wait_ge(*L.after("o_ready", T + 1))
        if scaled:
            dve.wait_ge(*L.after("rinv_ready", T + 1))
            ins = dve.tensor_tensor(m.o[:, j, :].rearrange("p (h d) -> p h d", d=HD),
                                    m.work(j)[:, 0:D].rearrange("p (h d) -> p h d", d=HD),
                                    m.rinv[:, j, :].unsqueeze(2).to_broadcast([P, H, HD]), ALU.mult)
        else:
            ins = dve.tensor_copy(m.o[:, j, :], m.work(j)[:, 0:D])
        ins.then_inc(L.s("o_kept"), 1)


def pe_out_full(pe, m, L, i, wo, bias=None):
    for j in range(m.chains):
        pe.wait_ge(*L.after("oT_kept", i + j + 1))
        for half in range(2):
            ins = pe.matmul(m.work(j)[:, 0:D], m.oT[:, j, half * P:(half + 1) * P], wo[:, half, :],
                            start=(half == 0), stop=(half == 1 and bias is None))
        if bias is not None:
            ins = pe.matmul(m.work(j)[:, 0:D], m.ones_row[0:1, :], bias, start=False, stop=True)
        ins.then_inc(L.s("y_ready"), 1)


def pe_proj(pe, m, out, w, j, bias=None):
    for k in range(2):
        ins = pe.matmul(out, m.xT[:, j, k, :], w[:, k, :], start=(k == 0), stop=(k == 1 and bias is None))
    if bias is not None:
        ins = pe.matmul(out, m.ones_row[0:1, :], bias, start=False, stop=True)
    return ins


def dve_mask_heads(dve, m, L, j, src, mask, out=None, name="masked_ready", heads=4):
    out = m.km if out is None else out
    for half in range(2):
        ins = dve.tensor_tensor(out[:, j, half],
                                src[:, half * P:(half + 1) * P].rearrange("p (b s) -> p b s", b=2).unsqueeze(2)
                                .to_broadcast([P, 2, heads, S]),
                                mask[:, 0:heads].unsqueeze(1).unsqueeze(3).to_broadcast([P, 2, heads, S]), ALU.mult)
    ins.then_inc(L.s(name), 1)


def pe_pT(pe, m, L, i, name="exp_ready"):
    for j in range(m.chains):
        pe.wait_ge(*L.after(name, i + j + 1))
        for u in range(8):
            ins = pe.transpose(m.bank(j, u // 4)[:, (u % 4) * P:(u % 4 + 1) * P], m.pr[:, j, u * P:(u + 1) * P], m.ident[:])
        ins.then_inc(L.s("pT_ready"), 1)


def act_pT(act, m, L, i):
    for j in range(m.chains):
        act.wait_ge(*L.after("pT_ready", i + j + 1))
        act.copy(m.pT[:, j, 0:512], m.bank(j, 0)).then_inc(L.s("pT_kept0"), 1)


def dve_pT(dve, m, L, i):
    for j in range(m.chains):
        dve.wait_ge(*L.after("pT_ready", i + j + 1))
        dve.tensor_copy(m.pT[:, j, 512:1024], m.bank(j, 1)).then_inc(L.s("pT_kept1"), 1)


def pe_oT(pe, m, L, i, name="o_kept"):
    for j in range(m.chains):
        pe.wait_ge(*L.after(name, i + j + 1))
        for b in range(2):
            ins = pe.transpose(m.bank(j, 1)[:, b * P:(b + 1) * P], m.o[:, j, b * P:(b + 1) * P], m.ident[:])
        ins.then_inc(L.s("oT_ready"), 1)


def act_oT(act, m, L, i):
    for j in range(m.chains):
        act.wait_ge(*L.after("oT_ready", i + j + 1))
        act.copy(m.oT[:, j, :], m.bank(j, 1)[:, 0:D]).then_inc(L.s("oT_kept"), 1)


def dve_softmax(dve, m, L, i, causal):
    for j in range(m.chains):
        T = i + j
        dve.wait_ge(*L.after("scores_ready", T + 1))
        for g in range(2):
            sc = m.bank(j, g)[:, :].rearrange("p (f r k) -> p f r k", f=2, r=4)
            pr = m.pr[:, j, :].rearrange("p (f g r k) -> p f g r k", f=2, g=2, r=4)[:, :, g]
            mx = m.mx[:, j, :].rearrange("p (f g r) -> p f g r", f=2, g=2)[:, :, g]
            if causal:
                ins = dve.tensor_tensor(pr, sc, m.causal[:, :].unsqueeze(1).unsqueeze(1).to_broadcast([P, 2, 4, S]), ALU.add)
            else:
                ins = dve.tensor_reduce(mx, sc, AX.X, ALU.max)
        ins.then_inc(L.s("scores_kept" if causal else "max_ready"), 1)
    if causal:
        for j in range(m.chains):
            dve.wait_ge(*L.after("scores_kept", i + j + 1))
            dve.tensor_reduce(m.mx[:, j, :], m.pr[:, j, :].rearrange("p (r k) -> p r k", k=S), AX.X, ALU.max)\
               .then_inc(L.s("max_ready"), 1)
    for j in range(m.chains):
        T = i + j
        dve.wait_ge(*L.after("max_ready", T + 1))
        if causal:
            pr = m.pr[:, j, :].rearrange("p (r k) -> p r k", k=S)
            ins = dve.tensor_tensor(pr, pr, m.mx[:, j, :].unsqueeze(2).to_broadcast([P, 16, S]), ALU.subtract)
        else:
            for g in range(2):
                sc = m.bank(j, g)[:, :].rearrange("p (f r k) -> p f r k", f=2, r=4)
                pr = m.pr[:, j, :].rearrange("p (f g r k) -> p f g r k", f=2, g=2, r=4)[:, :, g]
                mx = m.mx[:, j, :].rearrange("p (f g r) -> p f g r", f=2, g=2)[:, :, g]
                ins = dve.tensor_tensor(pr, sc, mx.unsqueeze(3).to_broadcast([P, 2, 4, S]), ALU.subtract)
        ins.then_inc(L.s("shift_ready"), 1)


def act_exp(act, m, L, i):
    for j in range(m.chains):
        act.wait_ge(*L.after("shift_ready", i + j + 1))
        ins = act.activation(m.pr[:, j, :], m.pr[:, j, :], ACT.Exp)
        ins.then_inc(L.s("exp_ready"), 1)


def dve_sums(dve, m, L, i):
    for j in range(m.chains):
        dve.wait_ge(*L.after("exp_ready", i + j + 1))
        dve.tensor_reduce(m.sums[:, j, :], m.pr[:, j, :].rearrange("p (r k) -> p r k", k=S), AX.X, ALU.add)\
           .then_inc(L.s("sum_ready"), 1)
    for j in range(m.chains):
        dve.wait_ge(*L.after("sum_ready", i + j + 1))
        dve.reciprocal(m.rinv[:, j, :], m.sums[:, j, :]).then_inc(L.s("rinv_ready"), 1)



def l0_names():
    n = per_tile(*CORE, "xT_ready", "xT_kept", "q_ready", "v_ready", "p_ready", "s1_ready", "mean_ready", "centred",
                 "sq_ready", "s2_ready", "gvar_ready", "gvar_kept", "grstd_ready", "normed", "g_ready", "g_kept",
                 "g_exp", "gate_ready", "affine_ready")
    n.update({"lng_ready": 1, "v_zeroed": 1, "dist_ready": H, "decay_exp": 1, "decay_ready": 1})
    return n


def l0_pe(pe, m, L):
    pe.wait_ge(m.s_w[0], 16 * m.n_w[0])
    w = m.w
    with pe.Fori(0, NT // m.chains) as r:
        i = m.chains * r
        pe_xT(pe, m, L, i)
        for j in range(m.chains):
            pe.wait_ge(*L.after("xT_kept", i + j + 1))
            pe_projT(pe, m, m.proj(j)[:, 0:D], w["l0_wq"], j)
            pe_projT(pe, m, m.proj(j)[:, D:2 * D], w["l0_wk"], j).then_inc(L.s("q_ready"), 1)
            pe_v_twice(pe, m, j, w["l0_wv"], w["l0_bv"][0:1, :]).then_inc(L.s("v_ready"), 1)
        for j in range(m.chains):
            pe.wait_ge(*L.after("plain_kept", i + j + 1))
            pe_projT(pe, m, m.proj(j)[:, 0:D], w["l0_wg"], j).then_inc(L.s("g_ready"), 1)
        for j in range(m.chains):
            pe.wait_ge(*L.after("g_kept", i + j + 1))
        pe_scores_full(pe, m, L, i)
        pe_pT(pe, m, L, i, "p_ready")
        pe_pv_full(pe, m, L, i)
        for j in range(m.chains):
            pe.wait_ge(*L.after("s1_ready", i + j + 1))
            pe.matmul(m.bank(j, 0)[:, 0:16], m.blk[:, :], m.s1[:, j, :], start=True, stop=True).then_inc(L.s("mean_ready"), 1)
        for j in range(m.chains):
            pe.wait_ge(*L.after("s2_ready", i + j + 1))
            pe.matmul(m.bank(j, 0)[:, 32:48], m.blk[:, :], m.s1[:, j, :], start=True, stop=True).then_inc(L.s("gvar_ready"), 1)
        pe_oT(pe, m, L, i, "normed")
        pe_out_full(pe, m, L, i, w["l0_wo"], w["l0_bo"][0:1, :])


def l0_act(act, m, L):
    w = m.w
    act.wait_ge(m.s_w[0], 16 * m.n_w[0])
    act.wait_ge(*L.after("v_zeroed", 1))
    act.activation(m.lng[:, :], m.gam[:, :], ACT.Ln).then_inc(L.s("lng_ready"), 1)
    act.wait_ge(*L.after("dist_ready", H))
    act.activation(m.decay[:, :], m.decay[:, :], ACT.Exp).then_inc(L.s("decay_exp"), 1)
    with act.Fori(0, NT // m.chains) as r:
        i = m.chains * r
        act_copy_x(act, m, L, i)
        act_xT_twice(act, m, L, i)
        for j in range(m.chains):
            act.wait_ge(*L.after("q_ready", i + j + 1))
            for h in range(2):
                act.activation(m.qT[:, j, h, :], m.proj(j)[:, h * P:(h + 1) * P], ACT.Identity,
                               bias=m.w["l0_bq"][:, h:h + 1])
            for h in range(2):
                ins = act.activation(m.kT[:, j, h, :], m.proj(j)[:, D + h * P:D + (h + 1) * P], ACT.Identity,
                                     bias=m.w["l0_bk"][:, h:h + 1])
            ins.then_inc(L.s("plain_kept"), 1)
        act_v_blocks(act, m, L, i)
        for j in range(m.chains):
            act.wait_ge(*L.after("g_ready", i + j + 1))
            for h in range(2):
                ins = act.activation(m.gT[:, j, h, :], m.proj(j)[:, h * P:(h + 1) * P], ACT.Identity,
                                     bias=m.w["l0_bg"][:, h:h + 1])
            ins.then_inc(L.s("g_kept"), 1)
        for j in range(m.chains):
            act.wait_ge(*L.after("g_kept", i + j + 1))
            act.activation(m.gE[:, j], m.gT[:, j], ACT.Tanh, scale=0.5).then_inc(L.s("g_exp"), 1)
        act_pT(act, m, L, i)


def l0_dve(dve, m, L):
    w = m.w
    dve.memset(m.vd, 0.0).then_inc(L.s("v_zeroed"), 1)
    dve.wait_ge(*L.after("lng_ready", 1))
    for u in range(H):
        dve.tensor_scalar(m.decay[:, u * S:(u + 1) * S], m.dist[:, :], m.lng[:, u:u + 1], None, ALU.mult)\
           .then_inc(L.s("dist_ready"), 1)
    dve.wait_ge(*L.after("decay_exp", 1))
    dec = m.decay[:, :].rearrange("p (u k) -> p u k", k=S)
    dve.tensor_tensor(dec, dec, m.tril[:, :].unsqueeze(1).to_broadcast([P, H, S]), ALU.mult).then_inc(L.s("decay_ready"), 1)
    dve.wait_ge(*L.after("decay_ready", 1))
    with dve.Fori(0, NT // m.chains) as r:
        i = m.chains * r
        for j in range(m.chains):
            dve.wait_ge(*L.after("plain_kept", i + j + 1))
            dve_mask_heads(dve, m, L, j, m.kT[:, j].rearrange("p h t -> p (h t)"), m.w["hmask_one"])
        for j in range(m.chains):
            dve.wait_ge(*L.after("scores_ready", i + j + 1))
            for g in range(2):
                pr, dec = (t.rearrange("p (f g r k) -> p f g r k", f=2, g=2, r=4)[:, :, g] for t in (m.pr[:, j, :], m.decay))
                ins = dve.tensor_tensor(pr, m.bank(j, g).rearrange("p (f r k) -> p f r k", f=2, r=4), dec, ALU.mult)
            ins.then_inc(L.s("p_ready"), 1)
        for j in range(m.chains):
            dve.wait_ge(*L.after("g_exp", i + j + 1))
            dve.scalar_tensor_tensor(m.gE[:, j], m.gE[:, j], 1.0, m.gT[:, j], ALU.add, ALU.mult).then_inc(L.s("gate_ready"), 1)
        dve_pT(dve, m, L, i)
        dve_o_full(dve, m, L, i, scaled=False)
        for j in range(m.chains):
            dve.wait_ge(*L.after("o_kept", i + j + 1))
            o3 = m.o[:, j, :].rearrange("p (r d) -> p r d", d=HD)
            dve.tensor_reduce(m.s1[:, j, :], o3, AX.X, ALU.add).then_inc(L.s("s1_ready"), 1)
        for j in range(m.chains):
            dve.wait_ge(*L.after("mean_ready", i + j + 1))
            o3 = m.o[:, j, :].rearrange("p (r d) -> p r d", d=HD)
            dve.tensor_tensor(o3, o3, m.bank(j, 0)[:, 0:16].unsqueeze(2).to_broadcast([P, 16, HD]), ALU.subtract)\
               .then_inc(L.s("centred"), 1)
        for j in range(m.chains):
            dve.wait_ge(*L.after("centred", i + j + 1))
            dve.tensor_tensor(m.o2[:, j, :], m.o[:, j, :], m.o[:, j, :], ALU.mult).then_inc(L.s("sq_ready"), 1)
        for j in range(m.chains):
            dve.wait_ge(*L.after("sq_ready", i + j + 1))
            dve.tensor_reduce(m.s1[:, j, :], m.o2[:, j, :].rearrange("p (r d) -> p r d", d=HD), AX.X, ALU.add)\
               .then_inc(L.s("s2_ready"), 1)
        for j in range(m.chains):
            dve.wait_ge(*L.after("gvar_ready", i + j + 1))
            dve.tensor_scalar(m.sums[:, j, :], m.bank(j, 0)[:, 32:48], LN_EPS, None, ALU.add).then_inc(L.s("gvar_kept"), 1)
        for j in range(m.chains):
            dve.wait_ge(*L.after("grstd_ready", i + j + 1))
            o3 = m.o[:, j, :].rearrange("p (r d) -> p r d", d=HD)
            dve.tensor_tensor(o3, o3, m.rinv[:, j, :].unsqueeze(2).to_broadcast([P, 16, HD]), ALU.mult)\
               .then_inc(L.s("normed"), 1)
        for j in range(m.chains):
            dve.wait_ge(*L.after("oT_ready", i + j + 1))
            for e in range(2):
                ins = dve.tensor_scalar(m.o2[:, j, e * P:(e + 1) * P], m.bank(j, 1)[:, e * P:(e + 1) * P], w["l0_gnw"][:, e:e + 1], w["l0_gnb"][:, e:e + 1],
                                        ALU.mult, ALU.add)
            ins.then_inc(L.s("affine_ready"), 1)
        for j in range(m.chains):
            dve.wait_ge(*L.after("affine_ready", i + j + 1))
            dve.wait_ge(*L.after("gate_ready", i + j + 1))
            dve.scalar_tensor_tensor(m.oT[:, j, :], m.o2[:, j, :], 0.5, m.gE[:, j].rearrange("p e t -> p (e t)"),
                                     ALU.mult, ALU.mult).then_inc(L.s("oT_kept"), 1)
        dve_residual_norm(dve, m, L, i, "y_ready", lambda j: m.work(j)[:, 0:D])


def l0_pool(pool, m, L):
    with pool.Fori(0, NT // m.chains) as r:
        i = m.chains * r
        for j in range(m.chains):
            pool.wait_ge(*L.after("gvar_kept", i + j + 1))
            pool.tensor_tensor(m.rinv[:, j, :], m.sums[:, j, :], m.mhalf[:, 0:16], ALU.pow).then_inc(L.s("grstd_ready"), 1)
        for j in range(m.chains):
            pool_rstd(pool, m, L, i + j, j)




def l1_names():
    n = per_tile(*CORE, *SOFTMAX, "scores_kept", "xss_ready", "ms_ready", "rms_ready", "qn_ready", "sin_part",
                 "qk_roped", "qkT_ready", "css_ready")
    n.update({"ctx_loaded%d" % j: 32 * NT // 4 for j in range(4)})
    n["v_zeroed"] = 1
    return n


def ctx_after(m, L, i, j):
    return L.after("ctx_loaded%d" % j, 16 // m.chains * i + 16)


def ctx_twice_after(m, L, i, j):
    return L.after("ctx_loaded%d" % j, 32 // m.chains * i + 32)


def l1_sync(sp, m, L):
    with sp.Fori(0, NT // m.chains) as r:
        i = m.chains * r
        for j in range(m.chains):
            T = i + j
            sp.wait_ge(*L.after(m.chain_free, T + 1 - m.chains))
            sp.dma_start(m.cb[:, j, :], m.ctx_tiles[T]).then_inc(L.s("ctx_loaded%d" % j), 16)
            sp.dma_start(m.cb2[:, j, :], m.ctx_twice[T]).then_inc(L.s("ctx_loaded%d" % j), 16)


def l1_pe(pe, m, L):
    pe.wait_ge(m.s_w[1], 16 * m.n_w[1])
    with pe.Fori(0, NT // m.chains) as r:
        i = m.chains * r
        for j in range(m.chains):
            pe.wait_ge(*L.after("qk_roped", i + j + 1))
            for c in range(4):
                ins = pe.transpose(m.proj(j)[:, c * P:(c + 1) * P], m.qk[:, j, c * P:(c + 1) * P], m.ident[:])
            ins.then_inc(L.s("qkT_ready"), 1)
        pe_scores_full(pe, m, L, i)
        pe_pT(pe, m, L, i)
        pe_pv_full(pe, m, L, i)
        pe_oT(pe, m, L, i)
        pe_out_full(pe, m, L, i, m.w["l1_wo"])


def l1_act(act, m, L):
    act.wait_ge(*L.after("v_zeroed", 1))
    with act.Fori(0, NT // m.chains) as r:
        i = m.chains * r
        act_copy_x(act, m, L, i)
        for j in range(m.chains):
            T = i + j
            act.wait_ge(*L.after("x_copied", T + 1))
            act.activation(m.oT[:, j, :], m.xc[:, j, :], ACT.Square, accum_out=m.stat[:, j, 4:5]).then_inc(L.s("xss_ready"), 1)
            act.wait_ge(*ctx_twice_after(m, L, i, j))
            act.activation(m.pT[:, j, 0:DC], m.cb[:, j, :], ACT.Square, accum_out=m.stat[:, j, 5:6]).then_inc(L.s("css_ready"), 1)
        act_context_blocks(act, m, L, i, lambda i, j: ctx_twice_after(m, L, i, j))
        for j in range(m.chains):
            act.wait_ge(*L.after("qkT_ready", i + j + 1))
            act.copy(m.qT[:, j], m.proj(j)[:, 0:D].rearrange("p (h t) -> p h t", h=2)).then_inc(L.s("plain_kept"), 1)
        act_exp(act, m, L, i)
        act_pT(act, m, L, i)
        act_oT(act, m, L, i)


def l1_dve(dve, m, L):
    w = m.w
    dve.memset(m.vd, 0.0).then_inc(L.s("v_zeroed"), 1)
    dve.wait_ge(m.s_w[1], 16 * m.n_w[1])
    with dve.Fori(0, NT // m.chains) as r:
        i = m.chains * r
        for j in range(m.chains):
            dve.wait_ge(*L.after("xss_ready", i + j + 1))
            dve.wait_ge(*L.after("css_ready", i + j + 1))
            dve.tensor_scalar(m.stat[:, j, 6:7], m.stat[:, j, 4:5], 1.0 / D, 1e-5, ALU.mult, ALU.add)
            dve.tensor_scalar(m.stat[:, j, 7:8], m.stat[:, j, 5:6], 1.0 / DC, 1e-5, ALU.mult, ALU.add).then_inc(L.s("ms_ready"), 1)
        for j in range(m.chains):
            dve.wait_ge(*L.after("rms_ready", i + j + 1))
            dve.scalar_tensor_tensor(m.qn[:, j, 0:D], m.xc[:, j, :], m.stat[:, j, 8:9], w["l1_qw"][:, :], ALU.mult, ALU.mult)
            dve.scalar_tensor_tensor(m.qn[:, j, D:D + DC], m.cb[:, j, :], m.stat[:, j, 9:10], w["l1_kw"][:, :],
                                     ALU.mult, ALU.mult).then_inc(L.s("qn_ready"), 1)
        for j in range(m.chains):
            dve.wait_ge(*L.after("qn_ready", i + j + 1))
            q3 = m.qn[:, j, :].rearrange("p (h d) -> p h d", d=HD)
            t1 = m.qt1[:, j, :].rearrange("p (h d) -> p h d", d=HD)
            t2 = m.qt2[:, j, :].rearrange("p (h d) -> p h d", d=HD)
            dve.tensor_tensor(t1, q3, w["l1_cos"][:, :].unsqueeze(1).to_broadcast([P, 20, HD]), ALU.mult)
            for half in range(2):
                ins = dve.tensor_tensor(t2[:, :, 8 * half:8 * half + 8], q3[:, :, 8 - 8 * half:16 - 8 * half],
                                        w["l1_sin"][:, 8 * half:8 * half + 8].unsqueeze(1).to_broadcast([P, 20, 8]), ALU.mult)
            ins.then_inc(L.s("sin_part"), 1)
        for j in range(m.chains):
            dve.wait_ge(*L.after("sin_part", i + j + 1))
            dve.tensor_tensor(m.qk[:, j, 0:D], m.qt1[:, j, 0:D], m.qt2[:, j, 0:D], ALU.add)
            a, c = (t[:, j, D:D + DC].rearrange("p (v d) -> p v d", d=HD).unsqueeze(2).to_broadcast([P, 4, 4, HD])
                    for t in (m.qt1, m.qt2))
            dve.tensor_tensor(m.qk[:, j, D:2 * D].rearrange("p (v g d) -> p v g d", v=4, g=4), a, c, ALU.add)\
               .then_inc(L.s("qk_roped"), 1)
        for j in range(m.chains):
            dve.wait_ge(*L.after("plain_kept", i + j + 1))
            dve_mask_heads(dve, m, L, j, m.proj(j)[:, D:2 * D], w["hmask_q"])
        dve_softmax(dve, m, L, i, True)
        dve_sums(dve, m, L, i)
        dve_pT(dve, m, L, i)
        dve_o_full(dve, m, L, i)
        dve_residual_norm(dve, m, L, i, "y_ready", lambda j: m.work(j)[:, 0:D])


def l1_pool(pool, m, L):
    with pool.Fori(0, NT // m.chains) as r:
        i = m.chains * r
        for j in range(m.chains):
            pool.wait_ge(*L.after("ms_ready", i + j + 1))
            pool.tensor_tensor(m.stat[:, j, 8:10], m.stat[:, j, 6:8], m.mhalf[:, 0:2], ALU.pow).then_inc(L.s("rms_ready"), 1)
        for j in range(m.chains):
            pool_rstd(pool, m, L, i + j, j)



def l3_names():
    n = per_tile(*CORE, *SOFTMAX, "xT_ready", "xT_kept", "q_ready", "v_ready", "p_ready", "rope_parts", "qT_kept",
                 "neg_ready", "negexp_ready", "feat_ready", "kf_ready", "lin_ready", "lsum_ready", "linv_ready",
                 "coef_ready", "soft_part", "lin_part")
    n.update({"v_zeroed": 1, "gate_exp": 1, "gate_one": 1, "gate_sig": 1, "gate_rest": 1})
    return n


def l3_pe(pe, m, L):
    w = m.w
    pe.wait_ge(m.s_w[3], 16 * m.n_w[3])
    with pe.Fori(0, NT // m.chains) as r:
        i = m.chains * r
        pe_xT(pe, m, L, i)
        for j in range(m.chains):
            pe.wait_ge(*L.after("xT_kept", i + j + 1))
            pe_projT(pe, m, m.proj(j)[:, 0:D], w["l3_wq"], j)
            pe_projT(pe, m, m.proj(j)[:, D:2 * D], w["l3_wk"], j).then_inc(L.s("q_ready"), 1)
            pe_v_twice(pe, m, j, w["l3_wv"]).then_inc(L.s("v_ready"), 1)
        pe_scores_full(pe, m, L, i)
        for j in range(m.chains):
            T = i + j
            pe.wait_ge(*L.after("kf_ready", T + 1))
            pe.wait_ge(*L.after("v_kept", T + 1))
            pe_pause(pe, m, j, 3)
            ins = pe_products(pe, m, j, 2, m.ft[:, j], m.kf)
            ins.then_inc(L.s("lin_ready"), 1)
        pe_pT(pe, m, L, i, "p_ready")
        pe_pv_full(pe, m, L, i)
        pe_oT(pe, m, L, i)
        pe_out_full(pe, m, L, i, w["l3_wo"])


def l3_act(act, m, L):
    act.wait_ge(m.s_w[3], 16 * m.n_w[3])
    act.activation(m.gsig[:, :], m.w["l3_gate"][:, :], ACT.Exp, scale=-1.0).then_inc(L.s("gate_exp"), 1)
    act.wait_ge(*L.after("v_zeroed", 1))
    with act.Fori(0, NT // m.chains) as r:
        i = m.chains * r
        act_copy_x(act, m, L, i)
        act_xT_twice(act, m, L, i)
        act_v_blocks(act, m, L, i)
        for j in range(m.chains):
            act.wait_ge(*L.after("neg_ready", i + j + 1))
            act.activation(m.ft[:, j, :], m.ft[:, j, :], ACT.Exp).then_inc(L.s("negexp_ready"), 1)
        act_exp(act, m, L, i)
        act_pT(act, m, L, i)
        act_oT(act, m, L, i)


def l3_dve(dve, m, L):
    w = m.w
    dve.memset(m.vd, 0.0).then_inc(L.s("v_zeroed"), 1)
    dve.wait_ge(m.s_w[3], 16 * m.n_w[3])
    dve.wait_ge(*L.after("gate_exp", 1))
    dve.tensor_scalar(m.gsig[:, :], m.gsig[:, :], 1.0, None, ALU.add).then_inc(L.s("gate_one"), 1)
    dve.wait_ge(*L.after("gate_one", 1))
    dve.reciprocal(m.gsig[:, :], m.gsig[:, :]).then_inc(L.s("gate_sig"), 1)
    dve.wait_ge(*L.after("gate_sig", 1))
    dve.tensor_scalar(m.grest[:, :], m.gsig[:, :], -1.0, 1.0, ALU.mult, ALU.add).then_inc(L.s("gate_rest"), 1)
    dve.wait_ge(*L.after("gate_rest", 1))
    with dve.Fori(0, NT // m.chains) as r:
        i = m.chains * r
        for j in range(m.chains):
            dve.wait_ge(*L.after("q_ready", i + j + 1))
            src = m.proj(j)[:, :].rearrange("p (x h b s) -> p x h b s", x=2, h=2, b=2)
            dve.tensor_tensor(m.rt1[:, j, :].rearrange("p (a s) -> p a s", s=S), m.proj(j)[:, :].rearrange("p (a s) -> p a s", s=S),
                              w["l3_cos"][:, :].unsqueeze(1).to_broadcast([P, 8, S]), ALU.mult)
            dst = m.rt2[:, j, :].rearrange("p (x h b s) -> p x h b s", x=2, h=2, b=2)
            for half in range(2):
                for x in range(2):
                    ins = dve.tensor_tensor(dst[:, x, half], src[:, x, 1 - half],
                                            w["l3_sin"][:, half * S:(half + 1) * S].unsqueeze(1).to_broadcast([P, 2, S]), ALU.mult)
            ins.then_inc(L.s("rope_parts"), 1)
        for j in range(m.chains):
            dve.wait_ge(*L.after("rope_parts", i + j + 1))
            dve.tensor_tensor(m.qT[:, j].rearrange("p h t -> p (h t)"), m.rt1[:, j, 0:D], m.rt2[:, j, 0:D], ALU.add)\
               .then_inc(L.s("qT_kept"), 1)
            dve.tensor_tensor(m.kT[:, j].rearrange("p h t -> p (h t)"), m.rt1[:, j, D:2 * D], m.rt2[:, j, D:2 * D], ALU.add)\
               .then_inc(L.s("plain_kept"), 1)
        for j in range(m.chains):
            dve.wait_ge(*L.after("plain_kept", i + j + 1))
            dve.tensor_scalar(m.ft[:, j, 0:D], m.qT[:, j].rearrange("p h t -> p (h t)"), 0.0, None, ALU.min)
            dve.tensor_scalar(m.ft[:, j, D:2 * D], m.kT[:, j].rearrange("p h t -> p (h t)"), 0.0, None, ALU.min)\
               .then_inc(L.s("neg_ready"), 1)
            dve_mask_heads(dve, m, L, j, m.kT[:, j].rearrange("p h t -> p (h t)"), w["hmask_q"])
        for j in range(m.chains):
            dve.wait_ge(*L.after("negexp_ready", i + j + 1))
            dve.scalar_tensor_tensor(m.ft[:, j, 0:D], m.qT[:, j].rearrange("p h t -> p (h t)"), 0.0, m.ft[:, j, 0:D], ALU.max, ALU.add)
            dve.scalar_tensor_tensor(m.ft[:, j, D:2 * D], m.kT[:, j].rearrange("p h t -> p (h t)"), 0.0, m.ft[:, j, D:2 * D],
                                     ALU.max, ALU.add).then_inc(L.s("feat_ready"), 1)
        for j in range(m.chains):
            dve.wait_ge(*L.after("feat_ready", i + j + 1))
            dve_mask_heads(dve, m, L, j, m.ft[:, j, D:2 * D], w["hmask_one"], m.kf, "kf_ready")
        dve_softmax(dve, m, L, i, False)
        for j in range(m.chains):
            dve.wait_ge(*L.after("lin_ready", i + j + 1))
            for g in range(2):
                ins = dve.tensor_reduce(m.lsum[:, j, :].rearrange("p (f g r) -> p f g r", f=2, g=2)[:, :, g],
                                        m.bank(j, 2 + g)[:, :].rearrange("p (f r k) -> p f r k", f=2, r=4), AX.X, ALU.add)
            ins.then_inc(L.s("lsum_ready"), 1)
        for j in range(m.chains):
            dve.wait_ge(*L.after("lsum_ready", i + j + 1))
            dve.reciprocal(m.linv[:, j, :], m.lsum[:, j, :]).then_inc(L.s("linv_ready"), 1)
        dve_sums(dve, m, L, i)
        for j in range(m.chains):
            dve.wait_ge(*L.after("linv_ready", i + j + 1))
            dve.wait_ge(*L.after("rinv_ready", i + j + 1))
            dve.tensor_tensor(m.linv[:, j, :], m.linv[:, j, :], m.gsig[:, :], ALU.mult)
            dve.tensor_tensor(m.rinv[:, j, :], m.rinv[:, j, :], m.grest[:, :], ALU.mult).then_inc(L.s("coef_ready"), 1)
        for j in range(m.chains):
            dve.wait_ge(*L.after("coef_ready", i + j + 1))
            pr = m.pr[:, j, :].rearrange("p (r k) -> p r k", k=S)
            dve.tensor_tensor(pr, pr, m.rinv[:, j, :].unsqueeze(2).to_broadcast([P, 16, S]), ALU.mult).then_inc(L.s("soft_part"), 1)
            for g in range(2):
                ins = dve.tensor_tensor(m.pr2[:, j, :].rearrange("p (f g r k) -> p f g r k", f=2, g=2, r=4)[:, :, g],
                                        m.bank(j, 2 + g)[:, :].rearrange("p (f r k) -> p f r k", f=2, r=4),
                                        m.linv[:, j, :].rearrange("p (f g r) -> p f g r", f=2, g=2)[:, :, g].unsqueeze(3)
                                        .to_broadcast([P, 2, 4, S]), ALU.mult)
            ins.then_inc(L.s("lin_part"), 1)
        for j in range(m.chains):
            dve.wait_ge(*L.after("lin_part", i + j + 1))
            dve.wait_ge(*L.after("soft_part", i + j + 1))
            dve.tensor_tensor(m.pr[:, j, :], m.pr[:, j, :], m.pr2[:, j, :], ALU.add).then_inc(L.s("p_ready"), 1)
        dve_pT(dve, m, L, i)
        dve_o_full(dve, m, L, i, scaled=False)
        dve_residual_norm(dve, m, L, i, "y_ready", lambda j: m.work(j)[:, 0:D])


def plain_pool(pool, m, L):
    with pool.Fori(0, NT // m.chains) as r:
        i = m.chains * r
        for j in range(m.chains):
            pool_rstd(pool, m, L, i + j, j)



def l4_names():
    n = per_tile(*CORE, *SOFTMAX, "scores_kept", "xT_ready", "xT_kept", "q_ready", "v_ready")
    n.update({"ctx_loaded%d" % j: 16 * NT // 4 for j in range(4)})
    n["v_zeroed"] = 1
    return n


def l4_sync(sp, m, L):
    with sp.Fori(0, NT // m.chains) as r:
        i = m.chains * r
        for j in range(m.chains):
            T = i + j
            sp.wait_ge(*L.after(m.chain_free, T + 1 - m.chains))
            sp.dma_start(m.ctxT[:, j, :], m.ctxT_d[:, bass.ds(T * 3 * P, 3 * P)]).then_inc(L.s("ctx_loaded%d" % j), 16)


def l4_pe(pe, m, L):
    w = m.w
    pe.wait_ge(m.s_w[4], 16 * m.n_w[4])
    with pe.Fori(0, NT // m.chains) as r:
        i = m.chains * r
        pe_xT(pe, m, L, i)
        for j in range(m.chains):
            pe.wait_ge(*L.after("xT_kept", i + j + 1))
            pe_projT(pe, m, m.proj(j)[:, 0:D], w["l4_wq"], j)
            pe.wait_ge(*ctx_after(m, L, i, j))
            for h in range(2):
                ins = pe.matmul(m.proj(j)[:, D + h * P:D + (h + 1) * P], w["l4_wkv"][:, h * P:(h + 1) * P],
                                m.ctxT[:, j, 2 * P:3 * P],
                                start=True, stop=True)
            ins.then_inc(L.s("q_ready"), 1)
            for b in range(2):
                ins = pe.matmul(m.work(j)[:, b * D:(b + 1) * D], m.ctxT[:, j, b * P:(b + 1) * P], w["l4_wkv"][:, D:2 * D],
                                start=True, stop=True)
            ins.then_inc(L.s("v_ready"), 1)
        pe_scores_full(pe, m, L, i)
        pe_pT(pe, m, L, i)
        pe_pv_full(pe, m, L, i)
        pe_oT(pe, m, L, i)
        pe_out_full(pe, m, L, i, w["l4_wo"])


def l4_act(act, m, L):
    act.wait_ge(*L.after("v_zeroed", 1))
    with act.Fori(0, NT // m.chains) as r:
        i = m.chains * r
        act_copy_x(act, m, L, i)
        act_xT(act, m, L, i)
        for j in range(m.chains):
            act.wait_ge(*L.after("q_ready", i + j + 1))
            act.copy(m.qT[:, j], m.proj(j)[:, 0:D].rearrange("p (h t) -> p h t", h=2)).then_inc(L.s("plain_kept"), 1)
        act_v_blocks(act, m, L, i)
        act_exp(act, m, L, i)
        act_pT(act, m, L, i)
        act_oT(act, m, L, i)


def l4_dve(dve, m, L):
    dve.memset(m.vd, 0.0).then_inc(L.s("v_zeroed"), 1)
    with dve.Fori(0, NT // m.chains) as r:
        i = m.chains * r
        for j in range(m.chains):
            dve.wait_ge(*L.after("plain_kept", i + j + 1))
            dve_mask_heads(dve, m, L, j, m.proj(j)[:, D:2 * D], m.w["hmask_q"])
        dve_softmax(dve, m, L, i, True)
        dve_sums(dve, m, L, i)
        dve_pT(dve, m, L, i)
        dve_o_full(dve, m, L, i)
        dve_residual_norm(dve, m, L, i, "y_ready", lambda j: m.work(j)[:, 0:D])



def l5_names():
    n = per_tile(*TILE, "xT_ready", "xT_kept", "y_ready")
    n.update({"abs_ready": 2, "abs_sum": 2, "thr_ready": 2, "nthr_ready": 2, "above_ready": 2, "below_ready": 2,
              "tern_ready": 2, "off_ready": 2, "ternw_ready": 2, "ternT_ready": 1, "ternT_kept": 1})
    return n


def l5_pe(pe, m, L):
    pe.wait_ge(*L.after("ternw_ready", 2))
    pe.wait_ge(*L.after("x_written", 0))
    for k in range(2):
        for h in range(2):
            ins = pe.transpose(m.bank(0, 0)[:, (k * 2 + h) * P:(k * 2 + h + 1) * P], m.tern[:, h, k * P:(k + 1) * P], m.ident[:])
    ins.then_inc(L.s("ternT_ready"), 1)
    pe.wait_ge(*L.after("ternT_kept", 1))
    with pe.Fori(0, NT // m.chains) as r:
        i = m.chains * r
        pe_xT(pe, m, L, i)
        for j in range(m.chains):
            pe.wait_ge(*L.after("xT_kept", i + j + 1))
            pe_proj(pe, m, m.proj(j)[:, 0:D], m.ternT, j, m.w["l5_b"][0:1, :]).then_inc(L.s("y_ready"), 1)


def l5_act(act, m, L):
    act.wait_ge(*L.after("ternT_ready", 1))
    act.copy(m.ternT[:, :, :], m.bank(0, 0)[:, :].rearrange("p (k o) -> p k o", k=2)).then_inc(L.s("ternT_kept"), 1)
    with act.Fori(0, NT // m.chains) as r:
        i = m.chains * r
        act_copy_x(act, m, L, i)
        act_xT(act, m, L, i)


def l5_dve(dve, m, L):
    w = m.w["l5_w"]
    dve.wait_ge(m.s_w[5], 16 * m.n_w[5])
    for h in range(2):
        dve.scalar_tensor_tensor(m.ta[:, h, :], w[:, h, :], -1.0, w[:, h, :], ALU.mult, ALU.max).then_inc(L.s("abs_ready"), 1)
    for h in range(2):
        dve.wait_ge(*L.after("abs_ready", h + 1))
        dve.tensor_reduce(m.tstat[:, h, 0:1], m.ta[:, h, :], AX.X, ALU.add).then_inc(L.s("abs_sum"), 1)
    for h in range(2):
        dve.wait_ge(*L.after("abs_sum", h + 1))
        dve.tensor_scalar(m.tstat[:, h, 1:2], m.tstat[:, h, 0:1], 1.0 / D, 0.7, ALU.mult, ALU.mult).then_inc(L.s("thr_ready"), 1)
    for h in range(2):
        dve.wait_ge(*L.after("thr_ready", h + 1))
        dve.tensor_scalar(m.tstat[:, h, 2:3], m.tstat[:, h, 1:2], -1.0, None, ALU.mult).then_inc(L.s("nthr_ready"), 1)
        dve.tensor_scalar(m.ta[:, h, :], w[:, h, :], m.tstat[:, h, 1:2], None, ALU.is_gt).then_inc(L.s("above_ready"), 1)
    for h in range(2):
        dve.wait_ge(*L.after("nthr_ready", h + 1))
        dve.tensor_scalar(m.tb[:, h, :], w[:, h, :], m.tstat[:, h, 2:3], None, ALU.is_lt).then_inc(L.s("below_ready"), 1)
    for h in range(2):
        dve.wait_ge(*L.after("below_ready", h + 1))
        dve.wait_ge(*L.after("above_ready", h + 1))
        dve.tensor_tensor(m.ta[:, h, :], m.ta[:, h, :], m.tb[:, h, :], ALU.subtract).then_inc(L.s("tern_ready"), 1)
    for h in range(2):
        dve.wait_ge(*L.after("tern_ready", h + 1))
        dve.tensor_tensor(m.ta[:, h, :], m.ta[:, h, :], w[:, h, :], ALU.subtract).then_inc(L.s("off_ready"), 1)
    for h in range(2):
        dve.wait_ge(*L.after("off_ready", h + 1))
        dve.tensor_tensor(m.tern[:, h, :], m.ta[:, h, :], w[:, h, :], ALU.add).then_inc(L.s("ternw_ready"), 1)
    with dve.Fori(0, NT // m.chains) as r:
        i = m.chains * r
        dve_residual_norm(dve, m, L, i, "y_ready", lambda j: m.proj(j)[:, 0:D])



def l9_names():
    n = per_tile(*CORE, *SOFTMAX, "xT_ready", "xT_kept", "q_ready", "k_ready", "v_ready", "rope_parts", "krope_parts",
                 "qT_kept")
    n["v_zeroed"] = 1
    return n


def l9_pe(pe, m, L):
    w = m.w
    pe.wait_ge(m.s_w[9], 16 * m.n_w[9])
    with pe.Fori(0, NT // m.chains) as r:
        i = m.chains * r
        pe_xT(pe, m, L, i)
        for j in range(m.chains):
            pe.wait_ge(*L.after("xT_kept", i + j + 1))
            pe_projT(pe, m, m.proj(j)[:, 0:D], w["l9_wq"], j)
            pe_projT(pe, m, m.proj(j)[:, D:2 * D], w["l9_wqp"], j).then_inc(L.s("q_ready"), 1)
            pe_projT(pe, m, m.bank(j, 0)[:, 0:D], w["l9_wk"], j)
            pe_projT(pe, m, m.bank(j, 0)[:, D:2 * D], w["l9_wkp"], j).then_inc(L.s("k_ready"), 1)
        for j in range(m.chains):
            pe.wait_ge(*L.after("krope_parts", i + j + 1))
            pe_v_twice(pe, m, j, w["l9_wv"], w["l9_bv"][0:1, :]).then_inc(L.s("v_ready"), 1)
        pe_scores_full(pe, m, L, i)
        pe_pT(pe, m, L, i)
        pe_pv_full(pe, m, L, i)
        pe_oT(pe, m, L, i)
        pe_out_full(pe, m, L, i, w["l9_wo"], w["l9_bo"][0:1, :])


def l9_act(act, m, L):
    act.wait_ge(*L.after("v_zeroed", 1))
    with act.Fori(0, NT // m.chains) as r:
        i = m.chains * r
        act_copy_x(act, m, L, i)
        act_xT_twice(act, m, L, i)
        act_v_blocks(act, m, L, i)
        act_exp(act, m, L, i)
        act_pT(act, m, L, i)
        act_oT(act, m, L, i)


def l9_dve(dve, m, L):
    w = m.w
    dve.memset(m.vd, 0.0).then_inc(L.s("v_zeroed"), 1)
    dve.wait_ge(m.s_w[9], 16 * m.n_w[9])
    with dve.Fori(0, NT // m.chains) as r:
        i = m.chains * r
        for name, ready, bias, bank, t in (("rope_parts", "q_ready", "l9_bq", lambda j: m.proj(j), m.rt1),
                                           ("krope_parts", "k_ready", "l9_bk", lambda j: m.bank(j, 0), m.rt2)):
            for j in range(m.chains):
                dve.wait_ge(*L.after(ready, i + j + 1))
                for c in range(4):
                    tab = w["l9_cos"] if c < 2 else w["l9_sin"]
                    ins = dve.scalar_tensor_tensor(
                        t[:, j, c * P:(c + 1) * P].rearrange("p (b s) -> p b s", b=2),
                        bank(j)[:, c * P:(c + 1) * P].rearrange("p (b s) -> p b s", b=2), w[bias][:, c:c + 1],
                        tab[:, :].unsqueeze(1).to_broadcast([P, 2, S]), ALU.add, ALU.mult)
                ins.then_inc(L.s(name), 1)
        for j in range(m.chains):
            dve.wait_ge(*L.after("rope_parts", i + j + 1))
            dve.tensor_tensor(m.qT[:, j].rearrange("p h t -> p (h t)"), m.rt1[:, j, 0:D], m.rt1[:, j, D:2 * D], ALU.add)\
               .then_inc(L.s("qT_kept"), 1)
            dve.wait_ge(*L.after("krope_parts", i + j + 1))
            dve.tensor_tensor(m.kT[:, j].rearrange("p h t -> p (h t)"), m.rt2[:, j, 0:D], m.rt2[:, j, D:2 * D], ALU.add)\
               .then_inc(L.s("plain_kept"), 1)
        for j in range(m.chains):
            dve.wait_ge(*L.after("plain_kept", i + j + 1))
            dve_mask_heads(dve, m, L, j, m.kT[:, j].rearrange("p h t -> p (h t)"), w["hmask_q"])
        dve_softmax(dve, m, L, i, False)
        dve_sums(dve, m, L, i)
        dve_pT(dve, m, L, i)
        dve_o_full(dve, m, L, i)
        dve_residual_norm(dve, m, L, i, "y_ready", lambda j: m.work(j)[:, 0:D])



E2, K2, F2, C2 = 64, 8, 96, 32
SLOTS = E2 * C2
NS = SLOTS // P


def l2_names():
    n = per_tile(*TILE)
    n.update({k: GROUPS for k in ("xs_copied", "xsT_ready", "xsT_kept", "logits_ready", "logits_kept")})
    n.update({k: NT for k in ("place_matrix", "slot_sums", "slot_x_kept", "slot_x_T", "slot_xT_kept", "hidden_ready",
                              "tanh_ready", "silu_ready", "h_kept", "slot_y_ready", "slot_y_kept", "back_matrix", "y_ready")})
    n.update({"expert_w0": 16 * NT, "expert_w1": 16 * NT, "x_in_dram": 16, "gathered": 16 * NS})
    n.update({"route_step": 20, "shifted": 1, "route_exp": 1, "prefix_ready": 1, "places_ready": 1,
              "slots_known": 1})
    return n


def l2_places(m, ar):
    group_places(m, ar)
    m.xc, m.r, m.bn, m.stat = ar.take([2, D]), ar.take([2, D]), ar.take([2, 6]), ar.take([2, 16])
    m.lg, m.sel, m.wt, m.top = ar.take([NT, E2]), ar.take([NT, E2]), ar.take([NT, E2]), ar.take([NT, 8])
    m.pre, m.pre2 = ar.take([NT + 1, E2]), ar.take([NT + 1, E2])
    m.tmp, m.posm = ar.take([NT, E2]), ar.take([NT, E2])
    m.rsum, m.rrec = ar.take([NT]), ar.take([NT])
    m.big = ar.take([2, SLOTS])
    m.rh = ar.take([NT, NS, 5])
    m.info, m.wsl4, m.wsl = ar.take([NS, 5]), ar.take([NS, 4]), ar.take([NS])
    m.tid, m.tidT = ar.take([NS]), ar.take([NT, NS])
    m.xg, m.yw = ar.take([NS, D]), ar.take([NS, D])
    m.sgT, m.th2, m.sg2, m.hT2 = ar.take([2, 2, P]), ar.take([2, P]), ar.take([2, P]), ar.take([2, P])


def l2_sync(sp, m, L):
    sp.dma_start(m.scratch["x_rows"].rearrange("(t p) d -> p t d", p=P), m.x[:, :, :]).then_inc(L.s("x_in_dram"), 16)
    for j in range(2):
        sp.dma_start(m.w["l2_ring"][:, j, 0:1536], m.dram["moe_w1v1"][j]).then_inc(L.s("expert_w%d" % j), 16)
        sp.dma_start(m.w["l2_ring"][0:F2, j, 1536:2560], m.dram["moe_w2"][j]).then_inc(L.s("expert_w%d" % j), 16)
    with sp.Fori(1, NS // 2) as i:
        for j in range(2):
            s = 2 * i + j
            sp.wait_ge(*L.after("slot_y_ready", s - 1))
            sp.dma_start(m.w["l2_ring"][:, j, 0:1536], m.dram["moe_w1v1"][bass.ds(s, 1)].rearrange("a p n -> (a p) n")).then_inc(L.s("expert_w%d" % j), 16)
            sp.dma_start(m.w["l2_ring"][0:F2, j, 1536:2560], m.dram["moe_w2"][bass.ds(s, 1)].rearrange("a p n -> (a p) n")).then_inc(L.s("expert_w%d" % j), 16)


def l2_pe(pe, m, L):
    w = m.w
    pe.wait_ge(m.s_w[2], 16 * m.n_w[2])
    with pe.Fori(0, GROUPS) as g:
        pe_group_T(pe, m, L, g, [m.flat(0), m.flat(1)])
        pe.wait_ge(*L.after("xsT_kept", g + 1))
        for q in range(4):
            for k in range(2):
                ins = pe.matmul(m.flat(2)[:, q * E2:(q + 1) * E2], m.xsT[:, k, q * P:(q + 1) * P], w["l2_rw"][:, k, :],
                                start=(k == 0), stop=(k == 1))
        ins.then_inc(L.s("logits_ready"), 1)
    pe.wait_ge(*L.after("prefix_ready", 1))
    for c in range(2):
        out = m.flat(3 + c)
        pe.matmul(out, w["l2_before"][:, :], m.pre2[:, NT:NT + 1, :].to_broadcast([P, 8, E2]), start=True, stop=False)
        pe.matmul(out, w["l2_same"][:, :], m.pre2[:, 8 * c:8 * c + 8, :], start=False, stop=False)
        ins = pe.matmul(out, w["l2_first_half"][:, :], m.sel[:, 8 * c:8 * c + 8, :], start=False, stop=True)
    ins.then_inc(L.s("places_ready"), 1)
    for T in range(NT):
        pe.wait_ge(*L.after("place_matrix", T + 1))
        for s in range(NS):
            ins = pe.matmul(m.flat(5)[:, s * 5:(s + 1) * 5], m.big[:, T % 2, s * P:(s + 1) * P], m.rh[:, T, s, :],
                            start=(T == 0 and s == 0), stop=(T == NT - 1), skip_group_check=True)
        ins.then_inc(L.s("slot_sums"), 1)
    with pe.Fori(0, NS // 2) as i:
        for j in range(2):
            pe.wait_ge(*L.after("slot_x_kept", 2 * i + j + 1))
            for h in range(2):
                ins = pe.transpose(m.bank(j, 0)[:, h * P:(h + 1) * P], m.xc[:, j, h * P:(h + 1) * P], m.ident[:])
            ins.then_inc(L.s("slot_x_T"), 1)
        for j in range(2):
            ring = m.w["l2_ring"][:, j, 0:1536].rearrange("p (e v k f) -> p e v k f", e=4, v=2, k=2)
            pe.wait_ge(*L.after("slot_xT_kept", 2 * i + j + 1))
            pe.wait_ge(*L.after("expert_w%d" % j, 32 * (i + 1)))
            for v in range(2):
                for e in range(4):
                    for k in range(2):
                        ins = pe.matmul(m.bank(j, 1)[0:F2, v * P + e * C2:v * P + (e + 1) * C2], ring[:, e, v, k, :],
                                        m.sgT[:, j, k, e * C2:(e + 1) * C2], start=(k == 0), stop=(k == 1))
            ins.then_inc(L.s("hidden_ready"), 1)
        for j in range(2):
            pe.wait_ge(*L.after("h_kept", 2 * i + j + 1))
            for e in range(4):
                ins = pe.matmul(m.bank(j, 2)[e * C2:(e + 1) * C2, 0:D], m.hT2[0:F2, j, e * C2:(e + 1) * C2],
                                m.w["l2_ring"][0:F2, j, 1536 + e * D:1536 + (e + 1) * D], start=True, stop=True)
            ins.then_inc(L.s("slot_y_ready"), 1)
    pe.wait_ge(*L.after("slot_y_kept", NS))
    with pe.Fori(0, NT // 2) as i:
        for j in range(2):
            pe.wait_ge(*L.after("back_matrix", 2 * i + j + 1))
            for s in range(NS):
                ins = pe.matmul(m.bank(j, 3)[:, 0:D], m.big[:, j, s * P:(s + 1) * P], m.yw[:, s, :],
                                start=(s == 0), stop=(s == NS - 1))
            ins.then_inc(L.s("y_ready"), 1)


def l2_act(act, m, L):
    with act.Fori(0, GROUPS) as g:
        act.copy(m.xs[:, :, :], m.x[:, bass.ds(4 * g, 4), :]).then_inc(L.s("xs_copied"), 1)
        act_group_T(act, m, L, g, [m.flat(0), m.flat(1)])
        act.wait_ge(*L.after("logits_ready", g + 1))
        act.copy(m.lg[:, bass.ds(4 * g, 4), :], m.flat(2)[:, 0:4 * E2].rearrange("p (q e) -> p q e", q=4))\
           .then_inc(L.s("logits_kept"), 1)
    act.wait_ge(*L.after("shifted", 1))
    act.activation(m.wt[:, :, :], m.wt[:, :, :], ACT.Exp).then_inc(L.s("route_exp"), 1)
    with act.Fori(0, NS // 2) as i:
        for j in range(2):
            s = 2 * i + j
            act.wait_ge(*L.after("gathered", 16 * NS))
            act.copy(m.xc[:, j, :], m.xg[:, s, :]).then_inc(L.s("slot_x_kept"), 1)
        for j in range(2):
            act.wait_ge(*L.after("slot_x_T", 2 * i + j + 1))
            act.copy(m.sgT[:, j], m.bank(j, 0)[:, 0:D].rearrange("p (h t) -> p h t", h=2)).then_inc(L.s("slot_xT_kept"), 1)
        for j in range(2):
            act.wait_ge(*L.after("hidden_ready", 2 * i + j + 1))
            act.activation(m.th2[0:F2, j, :], m.bank(j, 1)[0:F2, 0:P], ACT.Tanh, scale=0.5).then_inc(L.s("tanh_ready"), 1)


def l2_dve(dve, m, L):
    w = m.w
    done = [0]

    def then(ins):
        done[0] += 1
        ins.then_inc(L.s("route_step"), 1)
        dve.wait_ge(*L.after("route_step", done[0]))

    dve.wait_ge(m.s_w[2], 16 * m.n_w[2])
    dve.wait_ge(*L.after("logits_kept", GROUPS))
    for T in range(NT):
        ins = dve.max(m.top[:, T, :], m.lg[:, T, :])
    then(ins)
    for T in range(NT):
        ins = dve.match_replace(out=m.tmp[:, T, :], in_to_replace=m.top[:, T, :], in_values=m.lg[:, T, :], imm_value=-3e38)
    dve.tensor_tensor(m.wt[:, :, :], m.lg[:, :, :], m.top[:, :, 0:1].to_broadcast([P, NT, E2]), ALU.subtract)\
       .then_inc(L.s("shifted"), 1)
    then(dve.memset(m.pre[:, 0, :], 0.0))
    then(dve.tensor_tensor(m.sel[:, :, :], m.tmp[:, :, :], m.lg[:, :, :], ALU.not_equal))
    then(dve.tensor_copy(m.pre[:, 1:NT + 1, :], m.sel[:, :, :]))
    a, b = m.pre, m.pre2
    for shift in (1, 2, 4, 8):
        dve.tensor_copy(b[:, 0:shift, :], a[:, 0:shift, :])
        then(dve.tensor_tensor(b[:, shift:NT + 1, :], a[:, shift:NT + 1, :], a[:, 0:NT + 1 - shift, :], ALU.add))
        a, b = b, a
    then(dve.tensor_copy(m.pre2[:, :, :], m.pre[:, :, :]))
    dve.memset(m.pause[:, :], 0.0).then_inc(L.s("prefix_ready"), 1)
    dve.wait_ge(*L.after("route_exp", 1))
    then(dve.tensor_tensor(m.wt[:, :, :], m.wt[:, :, :], m.sel[:, :, :], ALU.mult))
    then(dve.tensor_reduce(m.rsum[:, :], m.wt[:, :, :], AX.X, ALU.add))
    then(dve.reciprocal(m.rrec[:, :], m.rsum[:, :]))
    then(dve.tensor_tensor(m.wt[:, :, :], m.wt[:, :, :], m.rrec[:, :].unsqueeze(2).to_broadcast([P, NT, E2]), ALU.mult))
    dve.tensor_copy(m.rh[:, :, :, 0], w["l2_token"][:, :].unsqueeze(2).to_broadcast([P, NT, NS]))
    then(dve.tensor_copy(m.rh[:, :, :, 1:5], m.wt[:, :, :].rearrange("p t (s e) -> p t s e", e=4)))
    dve.wait_ge(*L.after("places_ready", 1))
    for c in range(2):
        ins = dve.scalar_tensor_tensor(m.tmp[:, 8 * c:8 * c + 8, :].rearrange("p t e -> p (t e)"), m.flat(3 + c), 1.0,
                                       m.sel[:, 8 * c:8 * c + 8, :].rearrange("p t e -> p (t e)"), ALU.add, ALU.mult)
    then(ins)
    then(dve.tensor_scalar(m.posm[:, :, :], m.tmp[:, :, :], -1.0, None, ALU.add))
    for T in range(NT):
        if T >= 2:
            dve.wait_ge(*L.after("slot_sums", T - 1))
        dve.tensor_tensor(m.big[:, T % 2, :].rearrange("p (e c) -> p e c", c=C2),
                          m.posm[:, T, :].unsqueeze(2).to_broadcast([P, E2, C2]),
                          w["l2_iota"][:, 0:C2].unsqueeze(1).to_broadcast([P, E2, C2]), ALU.is_equal)\
           .then_inc(L.s("place_matrix"), 1)
    dve.wait_ge(*L.after("slot_sums", NT))
    then(dve.tensor_copy(m.info[:, :, :], m.flat(5)[:, 0:NS * 5].rearrange("p (s c) -> p s c", c=5)))
    then(dve.tensor_tensor(m.wsl4[:, :, :], m.info[:, :, 1:5], w["l2_own"][:, :].unsqueeze(1).to_broadcast([P, NS, 4]), ALU.mult))
    then(dve.tensor_reduce(m.wsl[:, :], m.wsl4[:, :, :], AX.X, ALU.add))
    then(dve.tensor_copy(m.tid[:, :].bitcast(mybir.dt.uint32), m.info[:, :, 0]))
    dve.tensor_tensor(m.tidT[:, :, :], m.info[:, :, 0].unsqueeze(1).to_broadcast([P, NT, NS]),
                      w["l2_tile_start"][:, :].unsqueeze(2).to_broadcast([P, NT, NS]), ALU.subtract).then_inc(L.s("slots_known"), 1)
    dve.wait_ge(*L.after("slots_known", 1))
    assert done[0] == 20, done
    with dve.Fori(0, NS // 2) as i:
        for j in range(2):
            dve.wait_ge(*L.after("tanh_ready", 2 * i + j + 1))
            dve.scalar_tensor_tensor(m.sg2[0:F2, j, :], m.th2[0:F2, j, :], 1.0, m.bank(j, 1)[0:F2, 0:P], ALU.add, ALU.mult)\
               .then_inc(L.s("silu_ready"), 1)
        for j in range(2):
            dve.wait_ge(*L.after("silu_ready", 2 * i + j + 1))
            dve.scalar_tensor_tensor(m.hT2[0:F2, j, :], m.sg2[0:F2, j, :], 0.5, m.bank(j, 1)[0:F2, P:2 * P], ALU.mult, ALU.mult)\
               .then_inc(L.s("h_kept"), 1)
        for j in range(2):
            s = 2 * i + j
            dve.wait_ge(*L.after("slot_y_ready", s + 1))
            dve.tensor_scalar(m.yw[:, s, :], m.bank(j, 2)[:, 0:D], m.wsl[:, bass.ds(s, 1)], None, ALU.mult)\
               .then_inc(L.s("slot_y_kept"), 1)
    with dve.Fori(0, NT // 2) as i:
        for j in range(2):
            T = 2 * i + j
            dve.wait_ge(*L.after("x_written", T - 1))
            dve.tensor_tensor(m.big[:, j, :].rearrange("p (s t) -> p s t", t=P),
                              m.tidT[:, T, :].unsqueeze(2).to_broadcast([P, NS, P]),
                              w["l2_iota"][:, :].unsqueeze(1).to_broadcast([P, NS, P]), ALU.is_equal)\
               .then_inc(L.s("back_matrix"), 1)
        dve.wait_ge(*L.after("x_copied", 2 * i + 2))
        dve_residual_norm(dve, m, L, 2 * i, "y_ready", lambda j: m.bank(j, 3)[:, 0:D])


def l2_pool(pool, m, L):
    pool.wait_ge(*L.after("slots_known", 1))
    pool.wait_ge(*L.after("x_in_dram", 16))
    for s in range(NS):
        pool.indirect_dma_start(m.xg[:, s, :], None, m.scratch["x_rows"],
                                bass.IndirectOffsetOnAxis(ap=m.tid[:, s:s + 1].bitcast(mybir.dt.uint32), axis=0))\
            .then_inc(L.s("gathered"), 16)
    with pool.Fori(0, NT // 2) as i:
        for j in range(2):
            T = 2 * i + j
            pool.wait_ge(*L.after("slot_y_kept", NS))
            pool_copy_x(pool, m, L, T, j)
        for j in range(2):
            pool_rstd(pool, m, L, 2 * i + j, j)



E11, F11 = 8, 352
C11 = TOK // E11
CHUNKS = ((0, 128), (128, 128), (256, 96))
NC = len(CHUNKS)


def l11_names():
    n = {k: NT for k in ("x_written", "r_kept", "stats_ready", "aggr_ready", "var_ready", "rstd_ready")}
    n.update({k: GROUPS for k in ("xs_copied", "xsT_ready", "xsT_kept", "logits_ready", "logits_kept", "shared_ready",
                                  "shared_kept")})
    n.update({k: GROUPS * NC + E11 * NC for k in ("gu_ready", "tanh_ready", "silu_ready", "h_kept")})
    n.update({k: E11 for k in ("slot_x_T", "slot_xT_kept", "slot_y_ready", "slot_y_kept")})
    for j in range(2):
        n.update({"slot_x%d" % j: 16 * E11 // 2, "slot_y_out%d" % j: 16 * E11 // 2, "expert_w%d" % j: 64 * E11 // 2})
    n.update({"zeros_ready": 1, "slots_zeroed": 16, "scattered": 16 * NT, "fetched": 16 * NT, "route_step": 17,
              "shifted": 1, "route_exp": 1, "prefix_ready": 1, "places_ready": 1, "slots_known": 1})
    return n


def l11_places(m, ar):
    group_places(m, ar)
    m.r, m.bn, m.stat = ar.take([2, D]), ar.take([2, 6]), ar.take([2, 16])
    m.th, m.sg, m.hT = ar.take([2, 512]), ar.take([2, 512]), ar.take([NC, 512])
    m.sh = ar.take([NT, D])
    m.og = ar.take([NT, D])
    m.lg, m.cand, m.oh, m.tmp = (ar.take([NT, E11]) for _ in range(4))
    m.pre, m.pre2 = ar.take([NT + 1, E11]), ar.take([NT + 1, E11])
    (m.mx, m.eidx, m.rsum, m.gate, m.place, m.keep, m.slot, m.a1, m.a2, m.idx_put, m.idx_get) = (
        ar.take([NT]) for _ in range(11))
    m.xd, m.xdT, m.ys = ar.take([2, 2, D]), ar.take([2, 2 * P]), ar.take([2, 2, D])
    m.zeros = ar.take([D])


def l11_sync(sp, m, L):
    sp.wait_ge(*L.after("zeros_ready", 1))
    xd = m.scratch["slot_x"]
    sp.dma_start(xd[0:TOK, :].rearrange("(t p) d -> p t d", p=P), m.zeros.unsqueeze(1).to_broadcast([P, NT, D]))\
      .then_inc(L.s("slots_zeroed"), 16)
    ring = m.w["l11_ring"]
    slots = xd[0:TOK, :].rearrange("(e h p) d -> e p h d", h=2, p=P)
    w1, w3, w2a, w2b = (m.dram["moe8_" + n] for n in ("w1", "w3", "w2a", "w2b"))

    def expert(ap, e):
        return ap[bass.ds(e, 1)].rearrange("a p n -> (a p) n")

    def weights(j, e):
        done = L.s("expert_w%d" % j)
        sp.dma_start(ring[:, j, 0:704], expert(w1, e)).then_inc(done, 16)
        sp.dma_start(ring[:, j, 704:1408], expert(w3, e)).then_inc(done, 16)
        sp.dma_start(ring[:, j, 1408:1920], expert(w2a, e)).then_inc(done, 16)
        sp.dma_start(ring[0:96, j, 1920:2176], expert(w2b, e)).then_inc(done, 16)

    def rows(j, e):
        sp.dma_start(m.xd[:, j], slots[bass.ds(e, 1)].rearrange("a p h d -> (a p) h d")).then_inc(L.s("slot_x%d" % j), 16)

    for j in range(2):
        weights(j, j)
    sp.wait_ge(*L.after("scattered", 16 * NT))
    for j in range(2):
        rows(j, j)
    with sp.Fori(1, E11 // 2) as i:
        for j in range(2):
            sp.wait_ge(*L.after("slot_y_ready", 2 * i + j - 1))
            weights(j, 2 * i + j)
            rows(j, 2 * i + j)


def l11_gate_up(pe, m, L, n, c, w1, w3, moving, width):
    at, rows = CHUNKS[c]
    for side, w in enumerate((w1, w3)):
        for k in range(2):
            ins = pe.matmul(m.flat(2 * side + c % 2)[0:rows, 0:width], w[:, k, at:at + rows], moving[:, k, :],
                            start=(k == 0), stop=(k == 1))
    ins.then_inc(L.s("gu_ready"), 1)


def l11_pe(pe, m, L):
    w = m.w
    pe.wait_ge(m.s_w[11], 16 * m.n_w[11])
    with pe.Fori(0, GROUPS) as g:
        pe_group_T(pe, m, L, g, [m.flat(6), m.flat(7)])
        pe.wait_ge(*L.after("xsT_kept", g + 1))
        for q in range(4):
            for k in range(2):
                ins = pe.matmul(m.flat(6)[:, q * E11:(q + 1) * E11], m.xsT[:, k, q * P:(q + 1) * P], w["l11_wg"][:, k, :],
                                start=(k == 0), stop=(k == 1))
        ins.then_inc(L.s("logits_ready"), 1)
        for c in range(NC):
            if c == 2:
                pe.wait_ge(*L.after("h_kept", NC * g + 1))
            l11_gate_up(pe, m, L, NC * g + c, c, w["l11_sw1"], w["l11_sw3"], m.xsT, 512)
        for c in range(NC):
            at, rows = CHUNKS[c]
            w2 = w["l11_sw2a"][:, c, :] if c < 2 else w["l11_sw2b"]
            pe.wait_ge(*L.after("h_kept", NC * g + c + 1))
            for q in range(4):
                ins = pe.matmul(m.flat(4 + q // 2)[:, (q % 2) * D:(q % 2 + 1) * D], m.hT[0:rows, c, q * P:(q + 1) * P],
                                w2, start=(c == 0 and q % 2 == 0), stop=(c == NC - 1), skip_group_check=True)
        ins.then_inc(L.s("shared_ready"), 1)
    pe.wait_ge(*L.after("prefix_ready", 1))
    pe.matmul(m.flat(0)[:, 0:P], w["l11_before"], m.oh.rearrange("p t e -> p (t e)"), start=True, stop=False)
    pe.matmul(m.flat(0)[:, 0:P], w["l11_ones"], m.pre2[:, 0:NT, :].rearrange("p t e -> p (t e)"), start=False, stop=True)\
      .then_inc(L.s("places_ready"), 1)
    with pe.Fori(0, E11 // 2) as i:
        for j in range(2):
            e = 2 * i + j
            ring = m.w["l11_ring"][:, j, :]
            w1, w3 = (ring[:, v * 704:(v + 1) * 704].rearrange("p (k f) -> p k f", k=2) for v in range(2))
            pe.wait_ge(*L.after("slot_x%d" % j, 16 * (i + 1)))
            for k in range(2):
                for h in range(2):
                    ins = pe.transpose(m.flat(6)[:, (2 * k + h) * P:(2 * k + h + 1) * P], m.xd[:, j, h, k * P:(k + 1) * P], m.ident[:])
            ins.then_inc(L.s("slot_x_T"), 1)
            pe.wait_ge(*L.after("slot_xT_kept", e + 1))
            pe.wait_ge(*L.after("expert_w%d" % j, 64 * (i + 1)))
            n0 = GROUPS * NC + NC * e
            for c in range(NC):
                if c == 2:
                    pe.wait_ge(*L.after("h_kept", n0 + 1))
                l11_gate_up(pe, m, L, n0 + c, c, w1, w3, m.xdT, 2 * P)
            for c in range(NC):
                at, rows = CHUNKS[c]
                pe.wait_ge(*L.after("h_kept", n0 + c + 1))
                for h in range(2):
                    ins = pe.matmul(m.flat(4)[:, h * D:(h + 1) * D], m.hT[0:rows, c, h * P:(h + 1) * P],
                                    ring[0:rows, 1408 + c * D:1408 + (c + 1) * D], start=(c == 0 and h == 0),
                                    stop=(c == NC - 1), skip_group_check=True)
            ins.then_inc(L.s("slot_y_ready"), 1)


def l11_act(act, m, L):
    with act.Fori(0, GROUPS) as g:
        act.copy(m.xs[:, :, :], m.x[:, bass.ds(4 * g, 4), :]).then_inc(L.s("xs_copied"), 1)
        act_group_T(act, m, L, g, [m.flat(6), m.flat(7)])
        act.wait_ge(*L.after("logits_ready", g + 1))
        act.copy(m.lg[:, bass.ds(4 * g, 4), :], m.flat(6)[:, 0:4 * E11].rearrange("p (q e) -> p q e", q=4))\
           .then_inc(L.s("logits_kept"), 1)
        for c in range(NC):
            rows = CHUNKS[c][1]
            act.wait_ge(*L.after("gu_ready", NC * g + c + 1))
            act.activation(m.th[0:rows, c % 2, :], m.flat(c % 2)[0:rows, :], ACT.Tanh, scale=0.5).then_inc(L.s("tanh_ready"), 1)
        act.wait_ge(*L.after("shared_kept", g + 1))
    act.wait_ge(*L.after("shifted", 1))
    act.activation(m.tmp, m.tmp, ACT.Exp).then_inc(L.s("route_exp"), 1)
    with act.Fori(0, E11 // 2) as i:
        for j in range(2):
            e = 2 * i + j
            act.wait_ge(*L.after("slot_x_T", e + 1))
            act.copy(m.xdT[:, :, :].rearrange("p k t -> p (k t)"), m.flat(6)).then_inc(L.s("slot_xT_kept"), 1)
            n0 = GROUPS * NC + NC * e
            for c in range(NC):
                rows = CHUNKS[c][1]
                act.wait_ge(*L.after("gu_ready", n0 + c + 1))
                act.activation(m.th[0:rows, c % 2, 0:2 * P], m.flat(c % 2)[0:rows, 0:2 * P], ACT.Tanh, scale=0.5)\
                   .then_inc(L.s("tanh_ready"), 1)


def l11_hidden(dve, m, L, n, c, width):
    rows = CHUNKS[c][1]
    dve.wait_ge(*L.after("tanh_ready", n + 1))
    dve.scalar_tensor_tensor(m.sg[0:rows, c % 2, 0:width], m.th[0:rows, c % 2, 0:width], 1.0,
                             m.flat(c % 2)[0:rows, 0:width], ALU.add, ALU.mult).then_inc(L.s("silu_ready"), 1)
    dve.wait_ge(*L.after("silu_ready", n + 1))
    dve.scalar_tensor_tensor(m.hT[0:rows, c, 0:width], m.sg[0:rows, c % 2, 0:width], 0.5,
                             m.flat(2 + c % 2)[0:rows, 0:width], ALU.mult, ALU.mult).then_inc(L.s("h_kept"), 1)


def l11_dve(dve, m, L):
    w = m.w
    done = [0]

    def then(ins):
        done[0] += 1
        ins.then_inc(L.s("route_step"), 1)
        dve.wait_ge(*L.after("route_step", done[0]))

    dve.memset(m.zeros, 0.0).then_inc(L.s("zeros_ready"), 1)
    with dve.Fori(0, GROUPS) as g:
        for c in range(NC):
            l11_hidden(dve, m, L, NC * g + c, c, 512)
        dve.wait_ge(*L.after("shared_ready", g + 1))
        for q in range(4):
            ins = dve.tensor_tensor(m.sh[:, 4 * g + q, :], m.flat(4 + q // 2)[:, (q % 2) * D:(q % 2 + 1) * D], m.xs[:, q, :], ALU.add)
        ins.then_inc(L.s("shared_kept"), 1)
    dve.wait_ge(m.s_w[11], 16 * m.n_w[11])
    dve.wait_ge(*L.after("logits_kept", GROUPS))
    then(dve.tensor_reduce(m.mx, m.lg, AX.X, ALU.max))
    mx = m.mx.unsqueeze(2).to_broadcast([P, NT, E11])
    dve.tensor_tensor(m.tmp, m.lg, mx, ALU.subtract).then_inc(L.s("shifted"), 1)
    then(dve.tensor_tensor(m.cand, m.lg, mx, ALU.not_equal))
    then(dve.scalar_tensor_tensor(m.cand, m.cand, 1000.0, w["l11_iota"].unsqueeze(1).to_broadcast([P, NT, E11]), ALU.mult, ALU.add))
    then(dve.tensor_reduce(m.eidx, m.cand, AX.X, ALU.min))
    then(dve.tensor_tensor(m.oh, m.cand, m.eidx.unsqueeze(2).to_broadcast([P, NT, E11]), ALU.is_equal))
    dve.memset(m.pre[:, 0, :], 0.0)
    then(dve.tensor_copy(m.pre[:, 1:NT + 1, :], m.oh))
    a, b = m.pre, m.pre2
    for shift in (1, 2, 4, 8):
        dve.tensor_copy(b[:, 0:shift, :], a[:, 0:shift, :])
        then(dve.tensor_tensor(b[:, shift:NT + 1, :], a[:, shift:NT + 1, :], a[:, 0:NT + 1 - shift, :], ALU.add))
        a, b = b, a
    dve.tensor_copy(m.pre2, m.pre).then_inc(L.s("prefix_ready"), 1)
    dve.wait_ge(*L.after("route_exp", 1))
    then(dve.tensor_reduce(m.rsum, m.tmp, AX.X, ALU.add))
    then(dve.reciprocal(m.gate, m.rsum))
    dve.wait_ge(*L.after("places_ready", 1))
    then(dve.tensor_tensor(m.cand, m.flat(0)[:, 0:P].rearrange("p (t e) -> p t e", e=E11), m.oh, ALU.mult))
    then(dve.tensor_reduce(m.place, m.cand, AX.X, ALU.add))
    dve.tensor_scalar(m.keep, m.place, float(C11), None, ALU.is_lt)
    then(dve.scalar_tensor_tensor(m.slot, m.eidx, float(C11), m.place, ALU.mult, ALU.add))
    dve.tensor_tensor(m.a1, m.slot, w["l11_overflow"], ALU.subtract)
    then(dve.tensor_scalar(m.a2, m.slot, 1.0 - TOK, None, ALU.add))
    dve.tensor_tensor(m.a1, m.a1, m.keep, ALU.mult)
    dve.tensor_tensor(m.gate, m.gate, m.keep, ALU.mult)
    then(dve.tensor_tensor(m.a2, m.a2, m.keep, ALU.mult))
    dve.tensor_tensor(m.idx_put.bitcast(mybir.dt.uint32), m.a1, w["l11_overflow"], ALU.add)
    dve.tensor_scalar(m.idx_get.bitcast(mybir.dt.uint32), m.a2, TOK - 1.0, None, ALU.add).then_inc(L.s("slots_known"), 1)
    assert done[0] == 17, done
    with dve.Fori(0, E11 // 2) as i:
        for j in range(2):
            e = 2 * i + j
            for c in range(NC):
                l11_hidden(dve, m, L, GROUPS * NC + NC * e + c, c, 2 * P)
            dve.wait_ge(*L.after("slot_y_ready", e + 1))
            dve.tensor_copy(m.ys[:, j].rearrange("p h d -> p (h d)"), m.flat(4)).then_inc(L.s("slot_y_kept"), 1)
        for j in range(2):
            dve.wait_ge(*L.after("slot_y_out%d" % j, 16 * (i + 1)))
    dve.wait_ge(*L.after("fetched", 16 * NT))
    with dve.Fori(0, NT // 2) as i:
        for j in range(2):
            T = 2 * i + j
            dve.wait_ge(*L.after("x_written", T - 1))
            dve.scalar_tensor_tensor(m.r[:, j, :], m.og[:, T, :], m.gate[:, bass.ds(T, 1)], m.sh[:, T, :], ALU.mult, ALU.add)\
               .then_inc(L.s("r_kept"), 1)
        dve_norm_tail(dve, m, L, 2 * i)


def l11_pool(pool, m, L):
    x_rows, y_rows = m.scratch["slot_x"], m.scratch["slot_y"]
    u32 = mybir.dt.uint32
    pool.wait_ge(*L.after("slots_known", 1))
    pool.wait_ge(*L.after("slots_zeroed", 16))
    for T in range(NT):
        pool.indirect_dma_start(x_rows, bass.IndirectOffsetOnAxis(ap=m.idx_put[:, T:T + 1].bitcast(u32), axis=0),
                                m.x[:, T, :], None).then_inc(L.s("scattered"), 16)
    y_out = y_rows.rearrange("(e h p) d -> e p h d", h=2, p=P)
    with pool.Fori(0, E11 // 2) as i:
        for j in range(2):
            pool.wait_ge(*L.after("slot_y_kept", 2 * i + j + 1))
            pool.dma_start(y_out[bass.ds(2 * i + j, 1)].rearrange("a p h d -> (a p) h d"), m.ys[:, j])\
                .then_inc(L.s("slot_y_out%d" % j), 16)
    for j in range(2):
        pool.wait_ge(*L.after("slot_y_out%d" % j, 16 * E11 // 2))
    for T in range(NT):
        pool.indirect_dma_start(m.og[:, T, :], None, y_rows,
                                bass.IndirectOffsetOnAxis(ap=m.idx_get[:, T:T + 1].bitcast(u32), axis=0))\
            .then_inc(L.s("fetched"), 16)
    with pool.Fori(0, NT // 2) as i:
        for j in range(2):
            pool_rstd(pool, m, L, 2 * i + j, j)



DI = 4096
CT = DI // P
MH = 64
W_IN, W_OUT = 2 * 2 * P + 5, D + 2


def l6_names():
    n = per_tile(*TILE4)
    n.update({k: GROUPS for k in ("var_ready", "rstd_ready", "xs_copied", "xsT_ready", "xsT_kept", "dt_ready", "dt_biased",
                                  "dt_abs", "dt_exp", "dt_ln", "dt_kept", "dA_kept", "bc_ready", "bc_conv1", "bc_conv2",
                                  "bc_conv3", "bc_conv0", "bc_tanh", "bc_kept", "cb_ready", "cb_kept", "ss_ready",
                                  "ms_kept", "scale_ready")})
    n.update({k: GROUPS * CT for k in ("x_ready6", "g_ready6", "x2T_ready", "diff_ready", "yT_ready", "out_added",
                                       "conv0", "x_tanh", "g_tanh", "decay_kept", "hid_sq", "conv1", "conv2", "conv3",
                                       "x2_kept", "g2_kept", "xdt_kept", "hid2_kept", "hid4_kept", "spread", "weighted",
                                       "wo_scaled", "sq_summed")})
    for u in range(4):
        n["in_loaded%d" % u] = n["out_loaded%d" % u] = 16 * GROUPS * CT // 4
    n["a_exp"] = n["cb_zeroed"] = 1
    return n


def l6_places(m, ar):
    group_places(m, ar)
    m.dtv, m.dta, m.dt, m.dA = (ar.take([4, MH]) for _ in range(4))
    m.aexp = ar.take([MH])
    m.bcy, m.bct, m.bc2, m.cbm = ar.take([2, 512]), ar.take([2, 512]), ar.take([2, 512]), ar.take([4, 2, S])
    m.y, m.th, m.x2 = ar.take([2, 512]), ar.take([2, 512]), ar.take([4, 512])
    m.tg, m.g2 = ar.take([2, 512]), ar.take([4, 512])
    m.xdt, m.da_i, m.ed = ar.take([2, 512]), ar.take([2, 512]), ar.take([2, 512])
    m.sx = ar.take([2, 4, 2, 2, S])
    m.h2, m.h4, m.sq, m.acc = ar.take([2, 512]), ar.take([4, 512]), ar.take([2, 512]), ar.take([2, 512])
    m.wos = ar.take([2, D])
    m.ms, m.rv, m.ones_col = ar.take([4]), ar.take([4]), ar.take([1])


def channel_steps(eng, body):
    for s in range(4):
        body(s, 0, s, lambda k, s=s: s >= k)
    with eng.Fori(1, CT // 4) as q:
        for u in range(4):
            body(4 * q + u, q, u, lambda k: True)
    for s in range(CT, CT + 3):
        body(s, s // 4, s % 4, lambda k, s=s: s - k < CT)


def l6_sync(sp, m, L):
    def quad(g, q, wait):
        for u in range(4):
            n = CT * g + 4 * q + u
            c = 4 * q + u
            if wait:
                sp.wait_ge(*L.after("g2_kept", n - 3))
            sp.dma_start(m.w["l6_in"][:, u, :], m.dram["mamba_in"][bass.ds(c, 1)].rearrange("a p n -> (a p) n"))\
              .then_inc(L.s("in_loaded%d" % u), 16)
            if wait:
                sp.wait_ge(*L.after("out_added", n - 3))
            sp.dma_start(m.w["l6_out"][:, u, :], m.dram["mamba_out"][bass.ds(c, 1)].rearrange("a p n -> (a p) n"))\
              .then_inc(L.s("out_loaded%d" % u), 16)

    quad(0, 0, False)
    with sp.Fori(1, CT // 4) as q:
        quad(0, q, True)
    with sp.Fori(1, GROUPS) as g:
        with sp.Fori(0, CT // 4) as q:
            quad(g, q, True)


def l6_pe(pe, m, L):
    w = m.w
    X, G, XT, DF, OUT = m.flat(0), m.flat(1), m.flat(2), m.flat(3), 6
    pe.wait_ge(m.s_w[6], 16 * m.n_w[6])
    with pe.Fori(0, GROUPS) as g:
        pe_group_T(pe, m, L, g, [m.flat(6), m.flat(7)])
        pe.wait_ge(*L.after("xsT_kept", g + 1))
        for q in range(4):
            for k in range(2):
                ins = pe.matmul(XT[:, q * MH:(q + 1) * MH], m.xsT[:, k, q * P:(q + 1) * P], w["l6_wdt"][:, k, :],
                                start=(k == 0), stop=(k == 1))
        ins.then_inc(L.s("dt_ready"), 1)
        for side, bank in enumerate((X, G)):
            for k in range(2):
                ins = pe.matmul(bank, w["l6_wbc"][:, k, side * P:(side + 1) * P], m.xsT[:, k, :], start=(k == 0), stop=(k == 1))
        ins.then_inc(L.s("bc_ready"), 1)
        pe.wait_ge(*L.after("bc_kept", g + 1))
        for b in range(8):
            ins = pe.matmul(DF[64 * (b % 2):64 * (b % 2) + 64, (b // 2) * S:(b // 2 + 1) * S], m.bc2[:, 0, b * S:(b + 1) * S],
                            m.bc2[:, 1, b * S:(b + 1) * S], start=True, stop=True)
        ins.then_inc(L.s("cb_ready"), 1)
        pe.wait_ge(*L.after("cb_kept", g + 1))

        def step(s, q, u, on):
            n = CT * g + s
            if on(0):
                ring = w["l6_in"][:, u, 0:512].rearrange("p (v k c) -> p v k c", v=2, k=2)
                pe.wait_ge(*L.after("in_loaded%d" % u, (q + 1 + 8 * g) * 16))
                if not (isinstance(s, int) and s == 0):
                    pe.wait_ge(*L.after("conv3", n))
                for k in range(2):
                    ins = pe.matmul(X, ring[:, 0, k, :], m.xsT[:, k, :], start=(k == 0), stop=(k == 1))
                ins.then_inc(L.s("x_ready6"), 1)
                if not (isinstance(s, int) and s == 0):
                    pe.wait_ge(*L.after("g2_kept", n))
                for k in range(2):
                    ins = pe.matmul(G, ring[:, 1, k, :], m.xsT[:, k, :], start=(k == 0), stop=(k == 1))
                ins.then_inc(L.s("g_ready6"), 1)
            if on(1):
                v = (u - 1) % 4
                pe.wait_ge(*L.after("spread", n))
                if on(2):
                    pe.wait_ge(*L.after("decay_kept", n - 1))
                pe.matmul(DF, w["l6_after"], m.da_i[:, v % 2, :], start=True, stop=True).then_inc(L.s("diff_ready"), 1)
                pe.wait_ge(*L.after("x2_kept", n))
                if on(2):
                    pe.wait_ge(*L.after("xdt_kept", n - 1))
                for t in range(4):
                    ins = pe.transpose(XT[:, t * P:(t + 1) * P], m.x2[:, v, t * P:(t + 1) * P], m.ident[:])
                ins.then_inc(L.s("x2T_ready"), 1)
            if on(2):
                v = (u - 2) % 4
                pe.wait_ge(*L.after("xdt_kept", n - 1))
                pe.wait_ge(*L.after("weighted", n - 1))
                if on(3):
                    pe.wait_ge(*L.after("hid2_kept", n - 2))
                for t in range(4):
                    for e in range(2):
                        at = (2 * t + e) * S
                        ins = pe.matmul(m.flat(4)[64 * e:64 * e + 64, t * P:(t + 1) * P], m.xdt[:, v % 2, at:at + S],
                                        m.sx[:, v % 2, t, e].rearrange("p b i -> p (b i)"), start=True, stop=True)
                ins.then_inc(L.s("yT_ready"), 1)
            if on(3):
                v = (u - 3) % 4
                c0 = isinstance(s, int) and s == 3
                c31 = isinstance(s, int) and s == CT + 2
                pe.wait_ge(*L.after("wo_scaled", n - 2))
                pe.wait_ge(*L.after("hid4_kept", n - 2))
                for t in range(4):
                    ins = pe.matmul(m.flat(OUT + t // 2)[:, (t % 2) * D:(t % 2 + 1) * D], m.h4[:, v, t * P:(t + 1) * P],
                                    m.wos[:, v % 2, :], start=(c0 and t % 2 == 0), stop=c31, skip_group_check=True)
                ins.then_inc(L.s("out_added"), 1)

        channel_steps(pe, step)
        pe.wait_ge(*L.after("sq_summed", CT * (g + 1)))
        for t in range(4):
            ins = pe.matmul(X[:, t:t + 1], m.acc[:, (CT - 1) % 2, t * P:(t + 1) * P], m.ones_col, start=True, stop=True)
        ins.then_inc(L.s("ss_ready"), 1)


def l6_act(act, m, L):
    X, G, DF = m.flat(0), m.flat(1), m.flat(3)
    act.wait_ge(m.s_w[6], 16 * m.n_w[6])
    act.activation(m.aexp, m.w["l6_alog"], ACT.Exp).then_inc(L.s("a_exp"), 1)
    with act.Fori(0, GROUPS) as g:
        act_group_copy(act, m, L, g)
        act_group_T(act, m, L, g, [m.flat(6), m.flat(7)])
        act.wait_ge(*L.after("dt_abs", g + 1))
        act.activation(m.dta, m.dta, ACT.Exp, scale=-1.0).then_inc(L.s("dt_exp"), 1)
        act.wait_ge(*L.after("dt_exp", g + 1))
        act.activation(m.dta, m.dta, ACT.Ln, bias=1.0).then_inc(L.s("dt_ln"), 1)
        act.wait_ge(*L.after("bc_ready", g + 1))
        for side, bank in enumerate((X, G)):
            ins = act.activation(m.bcy[:, side, :], bank, ACT.Identity, bias=m.w["l6_cbc"][:, side, 4:5],
                                 scale=m.w["l6_cbc"][:, side, 3:4])
        ins.then_inc(L.s("bc_conv0"), 1)
        act.wait_ge(*L.after("bc_conv3", g + 1))
        act.activation(m.bct, m.bcy, ACT.Tanh, scale=0.5).then_inc(L.s("bc_tanh"), 1)

        def step(s, q, u, on):
            n = CT * g + s
            if on(0):
                conv = m.w["l6_in"][:, u, 512:517]
                act.wait_ge(*L.after("x_ready6", n + 1))
                act.activation(m.y[:, u % 2, :], X, ACT.Identity, bias=conv[:, 4:5], scale=conv[:, 3:4]).then_inc(L.s("conv0"), 1)
            if on(1):
                v = (u - 1) % 4
                act.wait_ge(*L.after("diff_ready", n))
                if on(3):
                    act.wait_ge(*L.after("weighted", n - 2))
                act.activation(m.ed[:, v % 2, :], DF, ACT.Exp).then_inc(L.s("decay_kept"), 1)
            if on(0):
                act.wait_ge(*L.after("g_ready6", n + 1))
                act.activation(m.tg[:, u % 2, :], G, ACT.Tanh, scale=0.5).then_inc(L.s("g_tanh"), 1)
                act.wait_ge(*L.after("conv3", n + 1))
                act.activation(m.th[:, u % 2, :], m.y[:, u % 2, :], ACT.Tanh, scale=0.5).then_inc(L.s("x_tanh"), 1)
            if on(2):
                v = (u - 2) % 4
                act.wait_ge(*L.after("hid4_kept", n - 1))
                if not (isinstance(s, int) and s < 4):
                    act.wait_ge(*L.after("sq_summed", n - 3))
                act.activation(m.sq[:, v % 2, :], m.h4[:, v, :], ACT.Square).then_inc(L.s("hid_sq"), 1)

        channel_steps(act, step)


def l6_conv(dve, m, L, name, n, taps, y, x):
    for shift in range(1, 4):
        dve.wait_ge(*L.after(name + str(shift - 1), n + 1))
        for a, (tap, yy, xx) in enumerate(zip(taps, y, x)):
            y3, x3 = yy.rearrange("p (b s) -> p b s", b=8), xx.rearrange("p (b s) -> p b s", b=8)
            ins = dve.scalar_tensor_tensor(y3[:, :, shift:S], x3[:, :, 0:S - shift], tap[:, 3 - shift:4 - shift],
                                           y3[:, :, shift:S], ALU.mult, ALU.add)
        ins.then_inc(L.s(name + str(shift)), 1)


def l6_dve(dve, m, L):
    w = m.w
    X, G, XT, DF = m.flat(0), m.flat(1), m.flat(2), m.flat(3)
    dve.memset(m.ones_col, 1.0)
    dve.memset(m.cbm, 0.0).then_inc(L.s("cb_zeroed"), 1)
    dve.wait_ge(*L.after("cb_zeroed", 1))
    dve.wait_ge(m.s_w[6], 16 * m.n_w[6])
    dve.wait_ge(*L.after("a_exp", 1))
    with dve.Fori(0, GROUPS) as g:
        dve.wait_ge(*L.after("dt_ready", g + 1))
        dve.tensor_tensor(m.dtv, XT[:, 0:4 * MH].rearrange("p (t h) -> p t h", t=4), w["l6_dtb"].unsqueeze(1).to_broadcast([P, 4, MH]),
                          ALU.add).then_inc(L.s("dt_biased"), 1)
        dve.wait_ge(*L.after("dt_biased", g + 1))
        dve.scalar_tensor_tensor(m.dta, m.dtv, -1.0, m.dtv, ALU.mult, ALU.max).then_inc(L.s("dt_abs"), 1)
        dve.wait_ge(*L.after("dt_ln", g + 1))
        dve.scalar_tensor_tensor(m.dt, m.dtv, 0.0, m.dta, ALU.max, ALU.add).then_inc(L.s("dt_kept"), 1)
        dve.wait_ge(*L.after("dt_kept", g + 1))
        dve.scalar_tensor_tensor(m.dA, m.dt, -1.0, m.aexp.unsqueeze(1).to_broadcast([P, 4, MH]), ALU.mult, ALU.mult)\
           .then_inc(L.s("dA_kept"), 1)
        l6_conv(dve, m, L, "bc_conv", g, [w["l6_cbc"][:, a, :] for a in range(2)], [m.bcy[:, a, :] for a in range(2)], [X, G])
        dve.wait_ge(*L.after("bc_tanh", g + 1))
        dve.scalar_tensor_tensor(m.bc2, m.bct, 1.0, m.bcy, ALU.add, ALU.mult).then_inc(L.s("bc_kept"), 1)
        dve.wait_ge(*L.after("cb_ready", g + 1))
        for b in range(2):
            rows = slice(64 * b, 64 * b + 64)
            ins = dve.tensor_tensor(m.cbm[rows, :, b, :], DF[rows, 0:4 * S].rearrange("p (t i) -> p t i", t=4),
                                    w["l6_mask"][rows].unsqueeze(1).to_broadcast([64, 4, S]), ALU.mult)
        ins.then_inc(L.s("cb_kept"), 1)

        def step(s, q, u, on):
            n = CT * g + s
            if on(0):
                l6_conv(dve, m, L, "conv", n, [w["l6_in"][:, u, 512:517]], [m.y[:, u % 2, :]], [X])
            if on(1):
                v = (u - 1) % 4
                dve.wait_ge(*L.after("x2T_ready", n))
                if on(3):
                    dve.wait_ge(*L.after("yT_ready", n - 2))
                c = s - 1
                dts = m.dt[:, :, bass.ds(2 * c, 2)].unsqueeze(3).to_broadcast([P, 4, 2, 64])
                dve.tensor_tensor(m.xdt[:, v % 2, :].rearrange("p (t e c) -> p t e c", t=4, e=2),
                                  XT.rearrange("p (t e c) -> p t e c", t=4, e=2), dts, ALU.mult).then_inc(L.s("xdt_kept"), 1)
            if on(0):
                dve.wait_ge(*L.after("g_tanh", n + 1))
                dve.scalar_tensor_tensor(m.g2[:, u, :], m.tg[:, u % 2, :], 1.0, G, ALU.add, ALU.mult).then_inc(L.s("g2_kept"), 1)
                dve.wait_ge(*L.after("x_tanh", n + 1))
                dve.scalar_tensor_tensor(m.x2[:, u, :], m.th[:, u % 2, :], 1.0, m.y[:, u % 2, :], ALU.add, ALU.mult)\
                   .then_inc(L.s("x2_kept"), 1)
            if on(2):
                v = (u - 2) % 4
                qq = q if u >= 2 else q - 1
                dve.wait_ge(*L.after("out_loaded%d" % v, (qq + 1 + 8 * g) * 16))
                dve.wait_ge(*L.after("yT_ready", n - 1))
                ins = dve.scalar_tensor_tensor(m.h2[:, v % 2, :], m.x2[:, v, :], w["l6_out"][:, v, D:D + 1], m.flat(4),
                                               ALU.mult, ALU.add)
                ins.then_inc(L.s("hid2_kept"), 1)
                dve.wait_ge(*L.after("hid2_kept", n - 1))
                dve.tensor_tensor(m.h4[:, v, :], m.h2[:, v % 2, :], m.g2[:, v, :], ALU.mult).then_inc(L.s("hid4_kept"), 1)

        channel_steps(dve, step)
        dve.wait_ge(*L.after("ss_ready", g + 1))
        dve.tensor_scalar(m.ms, X[:, 0:4], 1.0 / DI, 16e-5, ALU.mult, ALU.add).then_inc(L.s("ms_kept"), 1)
        dve.wait_ge(*L.after("scale_ready", g + 1))
        for t in range(4):
            dve.scalar_tensor_tensor(m.r4[:, t, :], m.flat(6 + t // 2)[:, (t % 2) * D:(t % 2 + 1) * D], m.rv[:, t:t + 1],
                                     m.xs[:, t, :], ALU.mult, ALU.add).then_inc(L.s("r_kept"), 1)
        dve_norm4_tail(dve, m, L, g)


def l6_pool(pool, m, L):
    w = m.w
    pool.wait_ge(m.s_w[6], 16 * m.n_w[6])
    with pool.Fori(0, GROUPS) as g:
        pool.wait_ge(*L.after("dA_kept", g + 1))
        pool.wait_ge(*L.after("cb_kept", g + 1))

        def step(s, q, u, on):
            n = CT * g + s
            if on(0):
                if not (isinstance(s, int) and s < 2):
                    pool.wait_ge(*L.after("diff_ready", n - 1))
                das = m.dA[:, :, bass.ds(2 * s, 2)].unsqueeze(3).to_broadcast([P, 4, 2, S])
                pool.tensor_tensor(m.da_i[:, u % 2, :].rearrange("p (t e i) -> p t e i", t=4, e=2), das,
                                   w["l6_upto"].unsqueeze(1).unsqueeze(1).to_broadcast([P, 4, 2, S]), ALU.mult).then_inc(L.s("spread"), 1)
            if on(1):
                v = (u - 1) % 4
                pool.wait_ge(*L.after("decay_kept", n))
                if on(3):
                    pool.wait_ge(*L.after("yT_ready", n - 2))
                for e in range(2):
                    ins = pool.tensor_tensor(m.sx[:, v % 2, :, e],
                                             m.ed[:, v % 2, :].rearrange("p (t e i) -> p t e i", t=4, e=2)[:, :, e].unsqueeze(2)
                                             .to_broadcast([P, 4, 2, S]), m.cbm, ALU.mult)
                ins.then_inc(L.s("weighted"), 1)
            if on(2):
                v = (u - 2) % 4
                qq = q if u >= 2 else q - 1
                pool.wait_ge(*L.after("out_loaded%d" % v, (qq + 1 + 8 * g) * 16))
                if not (isinstance(s, int) and s < 4):
                    pool.wait_ge(*L.after("out_added", n - 3))
                pool.tensor_tensor(m.wos[:, v % 2, :], w["l6_out"][:, v, 0:D], w["l6_out"][:, v, D + 1:D + 2].to_broadcast([P, D]),
                                   ALU.mult).then_inc(L.s("wo_scaled"), 1)
                pool.wait_ge(*L.after("hid_sq", n - 1))
                if isinstance(s, int) and s == 2:
                    pool.tensor_tensor(m.acc[:, 0, :], m.sq[:, 0, :], m.ones_col.to_broadcast([P, 512]), ALU.mult).then_inc(L.s("sq_summed"), 1)
                else:
                    pool.wait_ge(*L.after("sq_summed", n - 2))
                    pool.tensor_tensor(m.acc[:, v % 2, :], m.acc[:, (v - 1) % 2, :], m.sq[:, v % 2, :], ALU.add)\
                        .then_inc(L.s("sq_summed"), 1)

        channel_steps(pool, step)
        pool.wait_ge(*L.after("ms_kept", g + 1))
        pool.tensor_tensor(m.rv, m.ms, m.mhalf[:, 0:4], ALU.pow).then_inc(L.s("scale_ready"), 1)
        pool.wait_ge(*L.after("var_ready", g + 1))
        pool.tensor_tensor(m.rs4[:, :], m.va4[:, :], m.mhalf[:, 0:4], ALU.pow).then_inc(L.s("rstd_ready"), 1)



QD, QH, RD = 192, 96, 64


def l7_names():
    n = per_tile(*TILE, "scores_ready", "max_ready", "shift_ready", "exp_ready", "sum_ready", "rinv_ready", "p_ready",
                 "pT_ready", "pT_kept0", "pT_kept1", "o_ready", "oT_kept", "y_ready")
    n.pop("x_copied")
    n.update({k: GROUPS for k in ("xs_copied", "xsT_ready", "xsT_kept", "kv_parts", "kv_roped", "kvT_ready", "kvT_kept")})
    n.update({k: GROUPS * H for k in ("big_ready", "rope_parts", "roped", "qc_ready", "qc_kept")})
    n.update({"weff_ready": H, "weff_kept": H, "wqk_ready": 4, "wqk_kept": 4, "wvo_ready": 4, "wvo_kept": 4})
    n.update({"raw_loaded": 16 * 3, "ctx_group": 16 * GROUPS})
    return n


def l7_places(m, ar):
    m.weff, m.wqk, m.wvo = ar.take([2, H * QD]), ar.take([H, 2, RD], QH), ar.take([8, D])
    start = ar.at
    m.kcq, m.qrT, m.woT = ar.take([H, QD]), ar.take([H, QD], RD), ar.take([H, D])
    ar.at = start
    m.xs, m.xsT = ar.take([4, D]), ar.take([2, 512])
    m.cbg, m.kt1, m.kt2, m.kvr, m.kvT = ar.take([4, DC]), ar.take([4, DC]), ar.take([4, DC]), ar.take([4, 2, DC]), ar.take([4, P])
    m.qp = ar.take([4, 8, 2, S])
    m.r, m.bn, m.stat = ar.take([2, D]), ar.take([2, 6]), ar.take([2, 16])
    m.mx, m.sums, m.rinv = ar.take([2, 16]), ar.take([2, 16]), ar.take([2, 16])
    start = ar.at
    m.rp, m.qr = ar.take([2, 4, 512], QH), ar.take([2, 2, 512], QH)
    ar.at = start
    m.pr, m.pT, m.oc = ar.take([2, 1024]), ar.take([2, 1024]), ar.take([2, 8, P])


def l7_sync(sp, m, L):
    for place, name in ((m.kcq, "raw_kcq"), (m.qrT, "raw_qrT"), (m.woT, "raw_woT")):
        sp.dma_start(place, m.dram[name]).then_inc(L.s("raw_loaded"), 16)
    l7_folded(sp, L)
    with sp.Fori(0, GROUPS) as g:
        sp.wait_ge(*L.after("x_written", 4 * g))
        sp.dma_start(m.cbg, m.dram["ctx"][bass.ds(g * 4 * P, 4 * P), :].rearrange("(t p) d -> p t d", p=P))\
          .then_inc(L.s("ctx_group"), 16)


def l7_folded(eng, L):
    eng.wait_ge(*L.after("weff_kept", H))
    eng.wait_ge(*L.after("wqk_kept", 4))
    eng.wait_ge(*L.after("wvo_kept", 4))


def l7_pe(pe, m, L):
    w = m.w
    pe.wait_ge(m.s_w[7], 16 * m.n_w[7])
    pe.wait_ge(*L.after("raw_loaded", 16 * 3))
    for h in range(H):
        if h >= 2:
            pe.wait_ge(*L.after("weff_kept", h - 1))
        for k in range(2):
            ins = pe.matmul(m.flat(h % 2)[:, k * QD:(k + 1) * QD], w["l7_wq"][:, h, k * P:(k + 1) * P], m.kcq[:, h, :],
                            start=True, stop=True)
        ins.then_inc(L.s("weff_ready"), 1)
        if h % 4 == 3:
            n = h // 4
            if n >= 2:
                pe.wait_ge(*L.after("wqk_kept", n - 1))
                pe.wait_ge(*L.after("wvo_kept", n - 1))
            for q in range(4):
                for side in range(2):
                    ins = pe.matmul(m.flat(2 + n % 2)[0:QH, (2 * q + side) * RD:(2 * q + side + 1) * RD],
                                    m.qrT[:, 4 * n + q, side * QH:(side + 1) * QH], w["l7_krT"][:, 4 * n + q, :],
                                    start=True, stop=True)
            ins.then_inc(L.s("wqk_ready"), 1)
            for q in range(4):
                hh = 4 * n + q
                ins = pe.matmul(m.flat(4 + n % 2)[64 * (q % 2):64 * (q % 2) + 64, (q // 2) * D:(q // 2 + 1) * D],
                                w["l7_kv"][:, hh, :], m.woT[:, hh, :], start=True, stop=True)
            ins.then_inc(L.s("wvo_ready"), 1)
    l7_folded(pe, L)
    with pe.Fori(0, GROUPS) as g:
        pe_group_T(pe, m, L, g, [m.flat(6), m.flat(7)])
        pe.wait_ge(*L.after("xsT_kept", g + 1))

        def big(h):
            if h >= 2:
                pe.wait_ge(*L.after("rope_parts", H * g + h - 1))
            for side in range(2):
                for k in range(2):
                    ins = pe.matmul(m.flat(2 * side + h % 2)[0:QH, :], m.weff[:, k, h * QD + side * QH:h * QD + (side + 1) * QH],
                                    m.xsT[:, k, :], start=(k == 0), stop=(k == 1))
            ins.then_inc(L.s("big_ready"), 1)

        def to_latent(h):
            pe.wait_ge(*L.after("roped", H * g + h + 1))
            if h >= 2:
                pe.wait_ge(*L.after("qc_kept", H * g + h - 1))
            for side in range(2):
                ins = pe.matmul(m.flat(4 + h % 2)[RD * (h // 8):RD * (h // 8) + RD, :], m.wqk[:, h, side, :], m.qr[:, h % 2, side, :],
                                start=(side == 0), stop=(side == 1))
            ins.then_inc(L.s("qc_ready"), 1)

        big(0)
        pe.wait_ge(*L.after("kv_roped", g + 1))
        for t in range(4):
            ins = pe.transpose(m.flat(6)[:, t * P:(t + 1) * P], m.kvr[:, t].rearrange("p a c -> p (a c)"), m.ident[:])
        ins.then_inc(L.s("kvT_ready"), 1)
        for h in range(1, H):
            big(h)
            to_latent(h - 1)
        to_latent(H - 1)
        pe.wait_ge(*L.after("qc_kept", H * g + H))
        pe.wait_ge(*L.after("kvT_kept", g + 1))
        for u in range(2):
            for j in range(2):
                t = 2 * u + j
                T = 4 * g + t
                if u:
                    pe.wait_ge(*L.after("pT_kept0", T - 1))
                    pe.wait_ge(*L.after("pT_kept1", T - 1))
                for hp in range(8):
                    for b in range(2):
                        at = (hp * 2 + b) * S
                        rows = slice(64 * (hp // 4), 64 * (hp // 4) + 64)
                        ins = pe.matmul(m.bank(j, at // 512)[:, at % 512:at % 512 + S],
                                        m.qp[rows, hp % 4, 2 * t + b].rearrange("p e s -> p (e s)"),
                                        m.kvT[rows, t, b * S:(b + 1) * S], start=True, stop=True)
                ins.then_inc(L.s("scores_ready"), 1)
            for j in range(2):
                T = 4 * g + 2 * u + j
                pe.wait_ge(*L.after("p_ready", T + 1))
                for hp in range(8):
                    ins = pe.transpose(m.bank(j, hp // 4)[:, (hp % 4) * P:(hp % 4 + 1) * P], m.pr[:, j, hp * P:(hp + 1) * P], m.ident[:])
                ins.then_inc(L.s("pT_ready"), 1)
            for j in range(2):
                t = 2 * u + j
                T = 4 * g + t
                pe.wait_ge(*L.after("pT_kept0", T + 1))
                pe.wait_ge(*L.after("pT_kept1", T + 1))
                if u:
                    pe.wait_ge(*L.after("r_kept", T - 1))
                pe.matmul(m.bank(j, 2)[:, 0:1], m.ident[:, :], m.ident[:, 0:1], start=True, stop=True)
                for b in range(2):
                    rows = slice(b * S, (b + 1) * S)
                    for h2 in range(2):
                        ins = pe.matmul(m.bank(j, 2 + b)[h2 * 64:(h2 + 1) * 64, :], m.kvr[rows, t, 0, :],
                                        m.pT[rows, j, :].rearrange("p (u e q) -> p u e q", u=8, e=2)[:, :, h2, :],
                                        start=True, stop=True)
                ins.then_inc(L.s("o_ready"), 1)
            for j in range(2):
                T = 4 * g + 2 * u + j
                pe.wait_ge(*L.after("oT_kept", T + 1))
                for hp in range(8):
                    ins = pe.matmul(m.bank(j, 2)[:, 0:D], m.oc[:, j, hp, :], m.wvo[:, hp, :], start=(hp == 0), stop=(hp == 7))
                ins.then_inc(L.s("y_ready"), 1)


def l7_act(act, m, L):
    for h in range(H):
        act.wait_ge(*L.after("weff_ready", h + 1))
        act.copy(m.weff[:, :, h * QD:(h + 1) * QD], m.flat(h % 2)[:, 0:2 * QD].rearrange("p (k q) -> p k q", k=2))\
           .then_inc(L.s("weff_kept"), 1)
    l7_folded(act, L)
    with act.Fori(0, GROUPS) as g:
        act_group_copy(act, m, L, g)
        act_group_T(act, m, L, g, [m.flat(6), m.flat(7)])
        act.wait_ge(*L.after("kvT_ready", g + 1))
        act.copy(m.kvT.rearrange("p t q -> p (t q)"), m.flat(6)).then_inc(L.s("kvT_kept"), 1)
        for h in range(H):
            act.wait_ge(*L.after("qc_ready", H * g + h + 1))
            rows = slice(RD * (h // 8), RD * (h // 8) + RD)
            act.copy(m.qp[rows, h // 2 % 4, :, h % 2, :], m.flat(4 + h % 2)[rows, :].rearrange("p (b s) -> p b s", b=8))\
               .then_inc(L.s("qc_kept"), 1)
        for u in range(2):
            for j in range(2):
                T = 4 * g + 2 * u + j
                act.wait_ge(*L.after("shift_ready", T + 1))
                act.activation(m.pr[:, j, :], m.pr[:, j, :], ACT.Exp).then_inc(L.s("exp_ready"), 1)
            for j in range(2):
                T = 4 * g + 2 * u + j
                act.wait_ge(*L.after("pT_ready", T + 1))
                act.copy(m.pT[:, j, 0:512], m.bank(j, 0)).then_inc(L.s("pT_kept0"), 1)
            for j in range(2):
                T = 4 * g + 2 * u + j
                act.wait_ge(*L.after("o_ready", T + 1))
                for b in range(2):
                    ins = act.copy(m.oc[:, j, :, b * S:(b + 1) * S], m.bank(j, 2 + b).rearrange("p (u q) -> p u q", u=8))
                ins.then_inc(L.s("oT_kept"), 1)


def l7_dve(dve, m, L):
    w = m.w
    for n in range(4):
        dve.wait_ge(*L.after("wqk_ready", n + 1))
        dve.tensor_copy(m.wqk[:, 4 * n:4 * n + 4].rearrange("p h a r -> p (h a r)"), m.flat(2 + n % 2)[0:QH, :])\
           .then_inc(L.s("wqk_kept"), 1)
        dve.wait_ge(*L.after("wvo_ready", n + 1))
        dve.tensor_copy(m.wvo[:, 2 * n:2 * n + 2].rearrange("p u o -> p (u o)"), m.flat(4 + n % 2)).then_inc(L.s("wvo_kept"), 1)
    l7_folded(dve, L)
    dve.wait_ge(m.s_w[7], 16 * m.n_w[7])
    with dve.Fori(0, GROUPS) as g:
        dve.wait_ge(*L.after("ctx_group", 16 * (g + 1)))
        dve.tensor_tensor(m.kt1, m.cbg, w["l7_kcos"].unsqueeze(1).to_broadcast([P, 4, DC]), ALU.mult)
        for half in range(2):
            ins = dve.tensor_tensor(m.kt2[:, :, 32 * half:32 * half + 32], m.cbg[:, :, 32 - 32 * half:64 - 32 * half],
                                    w["l7_ksin"][:, 32 * half:32 * half + 32].unsqueeze(1).to_broadcast([P, 4, 32]), ALU.mult)
        ins.then_inc(L.s("kv_parts"), 1)
        dve.wait_ge(*L.after("kv_parts", g + 1))
        dve.tensor_tensor(m.kvr, m.kt1.unsqueeze(2).to_broadcast([P, 4, 2, DC]), m.kt2.unsqueeze(2).to_broadcast([P, 4, 2, DC]), ALU.add).then_inc(L.s("kv_roped"), 1)
        for h in range(H):
            n = H * g + h
            dve.wait_ge(*L.after("big_ready", n + 1))
            if h >= 2:
                dve.wait_ge(*L.after("roped", n - 1))
            a, b = m.flat(h % 2)[0:QH, :], m.flat(2 + h % 2)[0:QH, :]
            for k, (src, tab) in enumerate(((a, 0), (b, 1), (b, 2), (a, 3))):
                ins = dve.tensor_tensor(m.rp[:, h % 2, k, :].rearrange("p (b s) -> p b s", b=8),
                                        src.rearrange("p (b s) -> p b s", b=8),
                                        w["l7_qtab"][:, tab, :].unsqueeze(1).to_broadcast([QH, 8, S]), ALU.mult)
            ins.then_inc(L.s("rope_parts"), 1)
            dve.wait_ge(*L.after("rope_parts", n + 1))
            if h >= 2:
                dve.wait_ge(*L.after("qc_ready", n - 1))
            dve.tensor_tensor(m.qr[:, h % 2], m.rp[:, h % 2, 0:4:2, :], m.rp[:, h % 2, 1:4:2, :], ALU.add)\
               .then_inc(L.s("roped"), 1)
        for u in range(2):
            for j in range(2):
                T = 4 * g + 2 * u + j
                dve.wait_ge(*L.after("scores_ready", T + 1))
                for f in range(2):
                    ins = dve.tensor_reduce(m.mx[:, j, 8 * f:8 * f + 8], m.bank(j, f).rearrange("p (r k) -> p r k", k=S), AX.X, ALU.max)
                ins.then_inc(L.s("max_ready"), 1)
            for j in range(2):
                T = 4 * g + 2 * u + j
                dve.wait_ge(*L.after("max_ready", T + 1))
                for f in range(2):
                    ins = dve.tensor_tensor(m.pr[:, j, 512 * f:512 * f + 512].rearrange("p (r k) -> p r k", k=S),
                                            m.bank(j, f).rearrange("p (r k) -> p r k", k=S),
                                            m.mx[:, j, 8 * f:8 * f + 8].unsqueeze(2).to_broadcast([P, 8, S]), ALU.subtract)
                ins.then_inc(L.s("shift_ready"), 1)
            for j in range(2):
                T = 4 * g + 2 * u + j
                dve.wait_ge(*L.after("exp_ready", T + 1))
                dve.tensor_reduce(m.sums[:, j, :], m.pr[:, j, :].rearrange("p (r k) -> p r k", k=S), AX.X, ALU.add)\
                   .then_inc(L.s("sum_ready"), 1)
            for j in range(2):
                T = 4 * g + 2 * u + j
                dve.wait_ge(*L.after("sum_ready", T + 1))
                dve.reciprocal(m.rinv[:, j, :], m.sums[:, j, :]).then_inc(L.s("rinv_ready"), 1)
            for j in range(2):
                T = 4 * g + 2 * u + j
                dve.wait_ge(*L.after("rinv_ready", T + 1))
                pr = m.pr[:, j, :].rearrange("p (r k) -> p r k", k=S)
                dve.tensor_tensor(pr, pr, m.rinv[:, j, :].unsqueeze(2).to_broadcast([P, 16, S]), ALU.mult).then_inc(L.s("p_ready"), 1)
            for j in range(2):
                T = 4 * g + 2 * u + j
                dve.wait_ge(*L.after("pT_ready", T + 1))
                dve.tensor_copy(m.pT[:, j, 512:1024], m.bank(j, 1)).then_inc(L.s("pT_kept1"), 1)
            for j in range(2):
                T = 4 * g + 2 * u + j
                dve.wait_ge(*L.after("y_ready", T + 1))
                dve.wait_ge(*L.after("x_written", T - 1))
                dve.tensor_tensor(m.r[:, j, :], m.bank(j, 2)[:, 0:D], m.xs[:, 2 * u + j, :], ALU.add).then_inc(L.s("r_kept"), 1)
            dve_norm_tail(dve, m, L, 4 * g + 2 * u)


def l7_pool(pool, m, L):
    with pool.Fori(0, NT // 2) as i:
        for j in range(2):
            pool_rstd(pool, m, L, 2 * i + j, j)



GROUPS = NT // 4
TILE4 = ("x_written", "r_kept", "stats_ready", "aggr_ready")


def act_group_copy(act, m, L, g):
    act.wait_ge(*L.after("x_written", 4 * g))
    act.copy(m.xs[:, :, :], m.x[:, bass.ds(4 * g, 4), :]).then_inc(L.s("xs_copied"), 1)


def pe_group_T(pe, m, L, g, banks):
    pe.wait_ge(*L.after("xs_copied", g + 1))
    for h in range(2):
        for q in range(4):
            ins = pe.transpose(banks[h][:, q * P:(q + 1) * P], m.xs[:, q, h * P:(h + 1) * P], m.ident[:])
    ins.then_inc(L.s("xsT_ready"), 1)


def act_group_T(act, m, L, g, banks):
    act.wait_ge(*L.after("xsT_ready", g + 1))
    for h in range(2):
        ins = act.copy(m.xsT[:, h, :], banks[h])
    ins.then_inc(L.s("xsT_kept"), 1)


def dve_norm4(dve, m, L, g, y_of):
    for q in range(4):
        dve.tensor_tensor(m.r4[:, q, :], y_of(q), m.xs[:, q, :], ALU.add).then_inc(L.s("r_kept"), 1)
    dve_norm4_tail(dve, m, L, g)


def dve_norm4_tail(dve, m, L, g):
    for q in range(4):
        dve.wait_ge(*L.after("r_kept", 4 * g + q + 1))
        dve.bn_stats(m.bn4[:, q, :], m.r4[:, q, :]).then_inc(L.s("stats_ready"), 1)
    dve.wait_ge(*L.after("stats_ready", 4 * g + 4))
    dve.memset(m.pause[:, :], 0.0)
    for q in range(4):
        dve.bn_aggr(m.mv4[:, q, :], m.bn4[:, q, :]).then_inc(L.s("aggr_ready"), 1)
    dve.wait_ge(*L.after("aggr_ready", 4 * g + 4))
    dve.tensor_scalar(m.va4[:, :], m.mv4[:, :, 1], LN_EPS, None, ALU.add).then_inc(L.s("var_ready"), 1)
    dve.wait_ge(*L.after("rstd_ready", g + 1))
    for q in range(4):
        dve.tensor_scalar(m.x[:, 4 * g + q, :], m.r4[:, q, :], m.mv4[:, q, 0:1], m.rs4[:, q:q + 1],
                          ALU.subtract, ALU.mult).then_inc(L.s("x_written"), 1)


def group_pool(pool, m, L):
    with pool.Fori(0, GROUPS) as g:
        pool.wait_ge(*L.after("var_ready", g + 1))
        pool.tensor_tensor(m.rs4[:, :], m.va4[:, :], m.mhalf[:, 0:4], ALU.pow).then_inc(L.s("rstd_ready"), 1)


def group_places(m, ar):
    m.xs, m.xsT, m.r4 = ar.take([4, D]), ar.take([2, 512]), ar.take([4, D])
    m.bn4, m.mv4, m.va4, m.rs4 = ar.take([4, 6]), ar.take([4, 2]), ar.take([4]), ar.take([4])



FI = 1024 // P


def l8_names():
    n = per_tile(*TILE4)
    n.update({k: GROUPS for k in ("var_ready", "rstd_ready", "xs_copied", "xsT_ready", "xsT_kept", "y_ready")})
    n.update({k: GROUPS * FI for k in ("gu_ready", "tanh_ready", "silu_ready", "h_kept")})
    return n


def l8_places(m, ar):
    group_places(m, ar)
    m.th, m.sg, m.hT = ar.take([2, 512]), ar.take([2, 512]), ar.take([FI, 512])


def l8_pe(pe, m, L):
    w = m.w
    pe.wait_ge(m.s_w[8], 16 * m.n_w[8])
    with pe.Fori(0, GROUPS) as g:
        pe_group_T(pe, m, L, g, [m.flat(6), m.flat(7)])
        pe.wait_ge(*L.after("xsT_kept", g + 1))

        def gate_up(c):
            if c >= 2:
                pe.wait_ge(*L.after("h_kept", FI * g + c - 1))
            for side in range(2):
                for k in range(2):
                    ins = pe.matmul(m.flat(2 * side + c % 2), w["l8_gu"][:, k, side * 1024 + c * P:side * 1024 + (c + 1) * P],
                                    m.xsT[:, k, :], start=(k == 0), stop=(k == 1))
            ins.then_inc(L.s("gu_ready"), 1)

        def down(c):
            pe.wait_ge(*L.after("h_kept", FI * g + c + 1))
            for q in range(4):
                ins = pe.matmul(m.flat(4 + q // 2)[:, (q % 2) * D:(q % 2 + 1) * D], m.hT[:, c, q * P:(q + 1) * P],
                                w["l8_down"][:, c, :], start=(c == 0 and q % 2 == 0), stop=(c == FI - 1), skip_group_check=True)
            return ins

        for c in range(FI):
            gate_up(c)
            if c >= 1:
                down(c - 1)
        down(FI - 1).then_inc(L.s("y_ready"), 1)


def l8_act(act, m, L):
    with act.Fori(0, GROUPS) as g:
        act_group_copy(act, m, L, g)
        act_group_T(act, m, L, g, [m.flat(6), m.flat(7)])
        for c in range(FI):
            act.wait_ge(*L.after("gu_ready", FI * g + c + 1))
            act.activation(m.th[:, c % 2, :], m.flat(c % 2), ACT.Tanh, scale=0.5).then_inc(L.s("tanh_ready"), 1)


def l8_dve(dve, m, L):
    with dve.Fori(0, GROUPS) as g:
        for c in range(FI):
            dve.wait_ge(*L.after("tanh_ready", FI * g + c + 1))
            dve.scalar_tensor_tensor(m.sg[:, c % 2, :], m.th[:, c % 2, :], 1.0, m.flat(c % 2), ALU.add, ALU.mult)\
               .then_inc(L.s("silu_ready"), 1)
            dve.wait_ge(*L.after("silu_ready", FI * g + c + 1))
            dve.scalar_tensor_tensor(m.hT[:, c, :], m.sg[:, c % 2, :], 0.5, m.flat(2 + c % 2), ALU.mult, ALU.mult)\
               .then_inc(L.s("h_kept"), 1)
        dve.wait_ge(*L.after("y_ready", g + 1))
        dve_norm4(dve, m, L, g, lambda q: m.flat(4 + q // 2)[:, (q % 2) * D:(q % 2 + 1) * D])



ROUNDS = 2


def l10_names():
    n = per_tile(*TILE, "xT_ready", "xT_kept", "v_kept")
    n.update({k: ROUNDS * NT for k in ("km_ready", "scores_ready", "max_ready", "shift_ready", "exp_ready", "sum_ready",
                                       "rinv_ready", "pT_ready", "pT_kept0", "pT_kept1", "o_ready", "o_kept")})
    n.update({"ctx_loaded%d" % j: 32 * NT // 4 for j in range(4)})
    n["v_zeroed"] = 1
    return n


def l10_sync(sp, m, L):
    with sp.Fori(0, NT // m.chains) as r:
        i = m.chains * r
        for j in range(m.chains):
            T = i + j
            sp.wait_ge(*L.after(m.chain_free, T + 1 - m.chains))
            sp.dma_start(m.cb2[:, j, :], m.ctx_twice[T]).then_inc(L.s("ctx_loaded%d" % j), 16)
            sp.dma_start(m.kT[:, j], m.dram["ctxT32"][:, :, bass.ds(T * P, P)]).then_inc(L.s("ctx_loaded%d" % j), 16)


def l10_pe(pe, m, L):
    pe.wait_ge(m.s_w[10], 16 * m.n_w[10])
    with pe.Fori(0, NT // m.chains) as r:
        i = m.chains * r
        pe_xT(pe, m, L, i)
        for f in range(ROUNDS):
            for j in range(m.chains):
                n = ROUNDS * i + m.chains * f + j
                pe.wait_ge(*L.after("km_ready", n + 1))
                if f:
                    pe.wait_ge(*L.after("o_kept", n + 1 - m.chains))
                else:
                    pe.wait_ge(*L.after("xT_kept", i + j + 1))
                pe_pause(pe, m, j, 1)
                for g in range(2):
                    rows = slice(64 * g, 64 * g + 64)
                    for b in range(2):
                        ins = pe.matmul(m.bank(j, g)[64 * b:64 * b + 64, :], m.xT[rows, j, f, b * S:(b + 1) * S],
                                        m.km8[f][rows, j, b].rearrange("p h s -> p (h s)"), start=True, stop=True)
                ins.then_inc(L.s("scores_ready"), 1)
            for j in range(m.chains):
                n = ROUNDS * i + m.chains * f + j
                pe.wait_ge(*L.after("exp_ready", n + 1))
                for u in range(8):
                    ins = pe.transpose(m.bank(j, u // 4)[:, (u % 4) * P:(u % 4 + 1) * P], m.pr[:, j, u * P:(u + 1) * P], m.ident[:])
                ins.then_inc(L.s("pT_ready"), 1)
            for j in range(m.chains):
                n = ROUNDS * i + m.chains * f + j
                pe.wait_ge(*L.after("pT_kept0", n + 1))
                pe.wait_ge(*L.after("pT_kept1", n + 1))
                pe.wait_ge(*L.after("v_kept", i + j + 1))
                for u in range(8):
                    for b in range(2):
                        ins = pe.matmul(m.work(j)[64 * b:64 * b + 64, u * 16:(u + 1) * 16],
                                        m.pT[:, j, u * P + 64 * b:u * P + 64 * b + 64],
                                        m.vd_ctx[:, j, b, f * 8 + u].rearrange("p e d -> p (e d)"), start=True, stop=True)
                ins.then_inc(L.s("o_ready"), 1)


def l10_act(act, m, L):
    act.wait_ge(*L.after("v_zeroed", 1))
    with act.Fori(0, NT // m.chains) as r:
        i = m.chains * r
        act_copy_x(act, m, L, i)
        act_xT(act, m, L, i)
        act_context_blocks(act, m, L, i, lambda i, j: ctx_twice_after(m, L, i, j))
        for f in range(ROUNDS):
            for j in range(m.chains):
                n = ROUNDS * i + m.chains * f + j
                act.wait_ge(*L.after("shift_ready", n + 1))
                act.activation(m.pr[:, j, :], m.pr[:, j, :], ACT.Exp).then_inc(L.s("exp_ready"), 1)
            for j in range(m.chains):
                n = ROUNDS * i + m.chains * f + j
                act.wait_ge(*L.after("pT_ready", n + 1))
                act.copy(m.pT[:, j, 0:512], m.bank(j, 0)).then_inc(L.s("pT_kept0"), 1)


def l10_dve(dve, m, L):
    w = m.w
    dve.memset(m.vd, 0.0).then_inc(L.s("v_zeroed"), 1)
    dve.wait_ge(m.s_w[10], 16 * m.n_w[10])
    with dve.Fori(0, NT // m.chains) as r:
        i = m.chains * r
        for f in range(ROUNDS):
            for j in range(m.chains):
                dve.wait_ge(*ctx_twice_after(m, L, i, j))
                dve.tensor_tensor(m.km8[f][:, j], m.kT[:, j, f].rearrange("p (b s) -> p b s", b=2).unsqueeze(2)
                                  .to_broadcast([P, 2, 8, S]),
                                  w["l10_hmask"][:, :].unsqueeze(1).unsqueeze(3).to_broadcast([P, 2, 8, S]), ALU.mult)\
                   .then_inc(L.s("km_ready"), 1)
        for f in range(ROUNDS):
            for j in range(m.chains):
                n = ROUNDS * i + m.chains * f + j
                dve.wait_ge(*L.after("scores_ready", n + 1))
                for g in range(2):
                    ins = dve.tensor_reduce(m.mx[:, j, g * 8:(g + 1) * 8], m.bank(j, g).rearrange("p (r k) -> p r k", k=S),
                                            AX.X, ALU.max)
                ins.then_inc(L.s("max_ready"), 1)
            for j in range(m.chains):
                n = ROUNDS * i + m.chains * f + j
                dve.wait_ge(*L.after("max_ready", n + 1))
                for g in range(2):
                    ins = dve.tensor_tensor(m.pr[:, j, g * 512:(g + 1) * 512].rearrange("p (r k) -> p r k", k=S),
                                            m.bank(j, g).rearrange("p (r k) -> p r k", k=S),
                                            m.mx[:, j, g * 8:(g + 1) * 8].unsqueeze(2).to_broadcast([P, 8, S]), ALU.subtract)
                ins.then_inc(L.s("shift_ready"), 1)
            for j in range(m.chains):
                n = ROUNDS * i + m.chains * f + j
                dve.wait_ge(*L.after("exp_ready", n + 1))
                dve.tensor_reduce(m.sums[:, j, :], m.pr[:, j, :].rearrange("p (r k) -> p r k", k=S), AX.X, ALU.add)\
                   .then_inc(L.s("sum_ready"), 1)
            for j in range(m.chains):
                n = ROUNDS * i + m.chains * f + j
                dve.wait_ge(*L.after("sum_ready", n + 1))
                dve.reciprocal(m.rinv[:, j, :], m.sums[:, j, :]).then_inc(L.s("rinv_ready"), 1)
            for j in range(m.chains):
                n = ROUNDS * i + m.chains * f + j
                dve.wait_ge(*L.after("pT_ready", n + 1))
                dve.tensor_copy(m.pT[:, j, 512:1024], m.bank(j, 1)).then_inc(L.s("pT_kept1"), 1)
            for j in range(m.chains):
                n = ROUNDS * i + m.chains * f + j
                dve.wait_ge(*L.after("o_ready", n + 1))
                dve.wait_ge(*L.after("rinv_ready", n + 1))
                dve.tensor_tensor(m.o[:, j, f * P:(f + 1) * P].rearrange("p (h d) -> p h d", d=8),
                                  m.work(j)[:, 0:P].rearrange("p (h d) -> p h d", d=8),
                                  m.rinv[:, j, :].unsqueeze(2).to_broadcast([P, 16, 8]), ALU.mult)\
                   .then_inc(L.s("o_kept"), 1)
        for j in range(m.chains):
            dve.wait_ge(*L.after("o_kept", ROUNDS * i + m.chains + j + 1))
            dve.wait_ge(*L.after("x_written", i + j + 1 - m.chains))
            dve.tensor_tensor(m.r[:, j, :], m.o[:, j, :], m.xc[:, j, :], ALU.add).then_inc(L.s("r_kept"), 1)
        dve_norm_tail(dve, m, L, i)



LAYER_PARTS = {
    0: (l0_names, l0_places, {"tensor": l0_pe, "scalar": l0_act, "vector": l0_dve, "gpsimd": l0_pool}),
    1: (l1_names, l1_places, {"sync": l1_sync, "tensor": l1_pe, "scalar": l1_act, "vector": l1_dve, "gpsimd": l1_pool}),
    3: (l3_names, l3_places, {"tensor": l3_pe, "scalar": l3_act, "vector": l3_dve, "gpsimd": plain_pool}),
    4: (l4_names, l4_places, {"sync": l4_sync, "tensor": l4_pe, "scalar": l4_act, "vector": l4_dve, "gpsimd": plain_pool}),
    5: (l5_names, l5_places, {"tensor": l5_pe, "scalar": l5_act, "vector": l5_dve, "gpsimd": plain_pool}),
    8: (l8_names, l8_places, {"tensor": l8_pe, "scalar": l8_act, "vector": l8_dve, "gpsimd": group_pool}),
    9: (l9_names, l9_places, {"tensor": l9_pe, "scalar": l9_act, "vector": l9_dve, "gpsimd": plain_pool}),
    10: (l10_names, l10_places, {"sync": l10_sync, "tensor": l10_pe, "scalar": l10_act, "vector": l10_dve, "gpsimd": plain_pool}),
    2: (l2_names, l2_places, {"sync": l2_sync, "tensor": l2_pe, "scalar": l2_act, "vector": l2_dve, "gpsimd": l2_pool}),
    11: (l11_names, l11_places, {"sync": l11_sync, "tensor": l11_pe, "scalar": l11_act, "vector": l11_dve, "gpsimd": l11_pool}),
    7: (l7_names, l7_places, {"sync": l7_sync, "tensor": l7_pe, "scalar": l7_act, "vector": l7_dve, "gpsimd": l7_pool}),
    6: (l6_names, l6_places, {"sync": l6_sync, "tensor": l6_pe, "scalar": l6_act, "vector": l6_dve, "gpsimd": l6_pool}),
}
SCRATCH = {"x_rows": (TOK, D), "slot_x": (2 * TOK, D), "slot_y": (TOK, D)}
WORK_WORDS = 27500
WEIGHT_WORDS = 6900


def layer_of(name):
    head = name[1:name.find("_")]
    return int(head) if name[0] == "l" and head.isdigit() else None


def build(nc, dram, out, scratch):
    with ExitStack() as ctx:
        def sb(name, shape, dt=F32):
            return ctx.enter_context(nc.sbuf_tensor(name, shape, dt))

        x_sb, ident, mhalf, ones_row, pause = (sb("x", [P, NT, D]), sb("ident", [P, P]), sb("mhalf", [P, 16]),
                                               sb("ones_row", [1, P]), sb("pause", [P, 1]))
        work_sb = sb("work", [P, WORK_WORDS])
        weight_sb = [sb("weights%d" % n, [P, WEIGHT_WORDS]) for n in range(2)]
        const_sb = {n[2:]: sb("sb_" + n, list(ap.shape)) for n, ap in dram.items() if n.startswith("c_")}
        psum = ctx.enter_context(nc.psum_tensor("banks", [P, 8, 512], F32))
        s_const = ctx.enter_context(nc.semaphore("constants_loaded"))
        s_out = ctx.enter_context(nc.semaphore("out_stored"))
        s_wt = [ctx.enter_context(nc.semaphore("weights_loaded%d" % n)) for n in range(2)]

        first, *stages = stage_semaphores(nc, ctx, [{"x_written": 16}] + [LAYER_PARTS[n][0]() for n in LAYERS])
        plan = []
        n_loaded = [0, 0]
        for at, layer in enumerate(LAYERS):
            _, places, parts = LAYER_PARTS[layer]
            m = Mem()
            m.x, m.ident, m.mhalf, m.ones_row, m.pause = x_sb, ident, mhalf, ones_row, pause
            if layer in FOUR_CHAINS:
                m.chains = 4
                m.bank = m.obank = lambda j, n: psum[:, 2 * j + n]
                m.work = lambda j: psum[:, 2 * j]
                m.proj = lambda j: psum[:, 2 * j + 1]
            else:
                m.chains = 2
                m.bank = lambda j, n: psum[:, 4 * j + n]
                m.work = lambda j: psum[:, 4 * j + 2]
                m.proj = lambda j: psum[:, 4 * j + 3]
                m.obank = lambda j, b: psum[:, 4 * j + (2 if b == 0 else 0)]
            m.flat = lambda n: psum[:, n]
            m.psum = psum
            m.chain_free = "x_written" if at == 0 else "r_kept"
            places(m, Arena(work_sb))
            m.dram, m.scratch = dram, scratch
            m.ctx_twice = Tiles(dram["ctx2"])
            m.ctx_tiles, m.ctxT_d = Tiles(dram["ctx"]), dram["ctxT"]
            m.s_const = s_const
            m.w = dict(const_sb)
            m.blk, m.tril, m.dist, m.causal = (m.w[k] for k in ("blk", "tril", "dist", "causal"))
            weights = Arena(weight_sb[at % 2])
            m.loads = []
            for name, ap in dram.items():
                if layer_of(name) == layer:
                    m.w[name] = weights.take(list(ap.shape[1:]), ap.shape[0])
                    m.loads.append(name)
            m.gam = m.w.get("l0_gam")
            if layer == 2:
                m.w["l2_ring"] = weights.take([2, 2560])
            if layer == 6:
                m.w["l6_in"], m.w["l6_out"] = weights.take([4, W_IN]), weights.take([4, W_OUT])
            if layer == 11:
                m.w["l11_ring"] = weights.take([2, 2176])
            n_loaded[at % 2] += len(m.loads)
            m.s_w, m.n_w = {layer: s_wt[at % 2]}, {layer: n_loaded[at % 2]}
            plan.append((parts, stages[at], m))
        n_const = len(const_sb) + 1
        block = ctx.enter_context(nc.Block())

        def load_weights(sp, at):
            m = plan[at][2]
            for name in m.loads:
                sp.dma_start(m.w[name], dram[name]).then_inc(s_wt[at % 2], 16)

        def run(eng, which):
            eng.wait_ge(*first.after("x_written", 16))
            eng.wait_ge(s_const, 16 * n_const + 2)
            for at, (parts, L, m) in enumerate(plan):
                eng.wait_ge(*L.after("x_written", 0))
                if which == "sync" and at + 1 < len(plan):
                    load_weights(eng, at + 1)
                if which in parts:
                    parts[which](eng, m, L)

        @block.sync
        def _(sp):
            sp.dma_start(x_sb[:, :, :], dram["x"].rearrange("(t p) d -> p t d", p=P)).then_inc(first.s("x_written"), 16)
            sp.dma_start(ident[:, :], dram["identity"]).then_inc(s_const, 16)
            for name in const_sb:
                sp.dma_start(const_sb[name][:], dram["c_" + name]).then_inc(s_const, 16)
            load_weights(sp, 0)
            run(sp, "sync")
            sp.wait_ge(*plan[-1][1].after("x_written", NT))
            sp.dma_start(out.rearrange("(t p) d -> p t d", p=P), x_sb[:, :, :]).then_inc(s_out, 16)
            sp.wait_ge(s_out, 16)
            for n in range(2):
                if n_loaded[n]:
                    sp.wait_ge(s_wt[n], 16 * n_loaded[n])

        @block.gpsimd
        def _(pool):
            pool.memset(mhalf[:, :], -0.5).then_inc(s_const, 1)
            pool.memset(ones_row[:, :], 1.0).then_inc(s_const, 1)
            run(pool, "gpsimd")

        @block.tensor
        def _(pe):
            run(pe, "tensor")

        @block.scalar
        def _(act):
            run(act, "scalar")

        @block.vector
        def _(dve):
            run(dve, "vector")

        for parts, L, m in plan:
            assert L.used == set(L.base), (sorted(set(L.base) - L.used), sorted(L.used - set(L.base)))


class Tiles:

    def __init__(self, ap):
        self.ap = ap

    def __getitem__(self, t):
        return self.ap[bass.ds(t * P, P), :]


def rope_angles(length, dim):
    inv = (1.0 / 10000.0 ** (np.arange(0, dim, 2, dtype=np.float32) / np.float32(dim))).astype(np.float32)
    return (np.arange(length, dtype=np.float32)[:, None] * inv[None, :]).astype(np.float32)


def constants():
    c = {"identity": np.eye(P, dtype=np.float32)}
    d = np.arange(P)
    one = ((d[:, None] // HD) % 4 == np.arange(4)[None, :]).astype(np.float32)
    c["c_hmask_one"] = one
    c["c_hmask_q"] = one * np.float32(1.0 / np.sqrt(HD))
    q = (d % S)[:, None]
    k = np.arange(S)[None, :]
    c["c_tril"] = (q >= k).astype(np.float32)
    c["c_causal"] = np.where(q >= k, 0.0, NEG).astype(np.float32)
    c["c_dist"] = np.maximum(q - k, 0).astype(np.float32)
    c["c_blk"] = ((d[:, None] // S) == (d[None, :] // S)).astype(np.float32) / np.float32(S * HD)
    a = rope_angles(S, HD)
    pos = d % S
    c["l1_cos"] = np.concatenate([np.cos(a), np.cos(a)], 1)[pos]
    c["l1_sin"] = np.concatenate([-np.sin(a), np.sin(a)], 1)[pos]
    a = rope_angles(S, D).T
    c["l3_cos"] = np.cos(a)
    c["l3_sin"] = np.concatenate([-np.sin(a), np.sin(a)], 1)
    theta = (10000.0 ** (-np.arange(0, HD, 2, dtype=np.float32) / np.float32(HD))).astype(np.float32)
    f = (np.arange(S, dtype=np.float32)[:, None] * theta[None, :]).T
    e = d % HD
    c["l9_cos"] = np.where((e < 8)[:, None], np.cos(f)[e % 8], 1.0)
    c["l9_sin"] = np.where((e < 8)[:, None], -np.sin(f)[e % 8], 0.0)
    c["l10_hmask"] = ((d[:, None] // 8) % 8 == np.arange(8)[None, :]) * np.float32(1.0 / np.sqrt(np.float32(8)))
    s = d % S
    a = np.repeat(rope_angles(S, QD), 2, axis=1).T
    c["l7_qtab"] = np.stack([np.cos(a[:QH]), -np.sin(a[:QH]), np.cos(a[QH:]), np.sin(a[QH:])], 1)
    a = np.repeat(rope_angles(S, DC), 2, axis=1)
    c["l7_kcos"] = np.cos(a)[pos]
    c["l7_ksin"] = np.concatenate([-np.sin(a[:, :32]), np.sin(a[:, 32:])], 1)[pos]
    c["l6_upto"] = (d % S)[:, None] <= np.arange(S)[None, :]
    c["l6_after"] = ((d // S)[:, None] == (d // S)[None, :]) & ((d % S)[:, None] > (d % S)[None, :])
    c["l6_mask"] = 0.25 * c["l6_upto"]
    c["l2_before"] = s[:, None] < s[None, :]
    c["l2_same"] = s[:, None] == s[None, :]
    c["l2_first_half"] = (s[:, None] == s[None, :]) & (d[:, None] < S) & (d[None, :] >= S)
    c["l2_iota"] = np.broadcast_to(d[None, :], (P, P))
    c["l2_token"] = d[:, None] + P * np.arange(NT)[None, :]
    c["l2_tile_start"] = np.broadcast_to(P * np.arange(NT)[None, :], (P, NT))
    c["l2_own"] = d[:, None] // C2 == np.arange(4)[None, :]
    c["l11_before"] = d[:, None] < d[None, :]
    c["l11_ones"] = np.ones((P, P))
    c["l11_iota"] = np.broadcast_to(np.arange(E11)[None, :], (P, E11))
    c["l11_overflow"] = TOK + c["l2_token"]
    return {n: np.ascontiguousarray(v, dtype=np.float32) for n, v in c.items()}


def layout(a):
    def kn(w):
        return w.reshape(-1, P, w.shape[1]).transpose(1, 0, 2)

    def cols(v):
        return v.reshape(-1, P).T

    def evens_first(w):
        return w.reshape(w.shape[0], H, 8, 2).transpose(0, 1, 3, 2).reshape(w.shape[0], D)

    def partner(w):
        return w.reshape(w.shape[0], H, 2, 8)[:, :, ::-1].reshape(w.shape[0], D)

    def all_rows(v):
        return np.broadcast_to(v.reshape(1, -1), (P, v.size))

    t = a["ctx_512"].reshape(NT, 2, S, DC).transpose(3, 0, 1, 2)
    ctxT = np.concatenate([np.stack([t, t], 3).reshape(DC, NT, 2 * P), t.reshape(DC, NT, P)], 2).reshape(DC, NT * 3 * P)
    o = {"x": a["x"].reshape(TOK, D), "ctx": a["ctx_512"].reshape(TOK, DC), "ctxT": ctxT}
    o["ctx2"] = np.broadcast_to(a["ctx_512"].reshape(NT, 1, 2, S, DC), (NT, 2, 2, S, DC)).transpose(0, 1, 3, 2, 4).reshape(TOK, 2 * DC)
    o["l0_wq"], o["l0_wk"], o["l0_wv"] = (kn(a["L0_attn_" + n]) for n in ("wq", "wk", "wv"))
    o["l0_wg"] = kn(a["L0_attn_wg"])
    o["l0_wo"] = kn(a["L0_attn_wo"])
    o["l0_bq"], o["l0_bk"] = cols(a["L0_attn_bq"]), cols(a["L0_attn_bk"])
    o["l0_bg"], o["l0_gnw"], o["l0_gnb"] = (cols(a["L0_attn_" + n]) for n in ("bg", "gn_w", "gn_b"))
    o["l0_bv"], o["l0_bo"] = (a["L0_attn_" + n].reshape(1, D) for n in ("bv", "bo"))
    o["l0_gam"] = all_rows(a["L0_attn_gamma"])
    o["l1_qw"], o["l1_kw"] = all_rows(a["L0_xattn_q_norm_w"]), all_rows(a["L0_xattn_k_norm_w"])
    o["l1_wo"] = kn(a["L0_xattn_w_out"].T)
    o["l3_wq"], o["l3_wk"], o["l3_wv"] = (kn(a["L1_attn_" + n].T) for n in ("Wq", "Wk", "Wv"))
    o["l3_wo"] = kn(a["L1_attn_Wo"].T)
    o["l3_gate"] = all_rows(a["L1_attn_gate"])
    o["l4_wq"] = kn(a["L1_xattn_Wq"].T)
    o["l4_wkv"] = a["L1_xattn_Wkv_expand"].T
    o["l4_wo"] = kn(a["L1_xattn_Wout"].T)
    o["l5_w"] = kn(a["L1_ffn_weight"])
    o["l5_b"] = a["L1_ffn_bias"].reshape(1, D)
    wq, wk = evens_first(a["L3_attn_wq"].T), evens_first(a["L3_attn_wk"].T)
    bq, bk = (evens_first(a["L3_attn_" + n].reshape(1, D)) for n in ("bq", "bk"))
    o["l9_wq"], o["l9_wqp"], o["l9_wk"], o["l9_wkp"] = kn(wq), kn(partner(wq)), kn(wk), kn(partner(wk))
    o["l9_bq"] = np.concatenate([cols(bq), cols(partner(bq))], 1)
    o["l9_bk"] = np.concatenate([cols(bk), cols(partner(bk))], 1)
    o["l9_wv"], o["l9_bv"] = kn(a["L3_attn_wv"].T), a["L3_attn_bv"].reshape(1, D)
    o["l8_gu"] = kn(a["L2_ffn_w_gate_up"].T)
    o["l8_down"] = kn(a["L2_ffn_w_down"].T)
    o["l7_wq"] = a["L2_xattn_Wq"].reshape(H, P, D).transpose(1, 0, 2)
    o["l7_krT"], o["l7_kv"] = a["L2_xattn_W_kr"].transpose(2, 0, 1), a["L2_xattn_w_kc_kv"].transpose(1, 0, 2)
    o["raw_kcq"], o["raw_qrT"] = a["L2_xattn_w_kc_q"].transpose(1, 0, 2), a["L2_xattn_W_qr"].transpose(2, 0, 1)
    o["raw_woT"] = a["L2_xattn_Wo"].T.reshape(H, P, D).transpose(1, 0, 2)
    w = a["L2_attn_in_proj_w"]

    def by_step(v):
        return v.reshape(2, P, CT, P).transpose(2, 1, 0, 3).reshape(CT, P, 2 * P)

    conv = np.concatenate([a["L2_attn_conv_w"], a["L2_attn_conv_b"].reshape(-1, 1)], 1)
    o["mamba_in"] = np.concatenate([by_step(w[:, DI:2 * DI]), by_step(w[:, 0:DI]), conv[0:DI].reshape(CT, P, 5)], 2)
    per_channel = np.repeat(a["L2_attn_D_param"], 64).reshape(CT, P, 1)
    o["mamba_out"] = np.concatenate([a["L2_attn_out_proj_w"].reshape(CT, P, D), per_channel,
                                     a["L2_attn_norm_w"].reshape(CT, P, 1)], 2)
    o["l6_wbc"], o["l6_wdt"] = kn(w[:, 2 * DI:2 * DI + 2 * P]), kn(w[:, 2 * DI + 2 * P:])
    o["l6_cbc"] = conv[DI:].reshape(2, P, 5).transpose(1, 0, 2)
    o["l6_dtb"], o["l6_alog"] = all_rows(a["L2_attn_dt_bias"]), all_rows(a["L2_attn_A_log"])
    o["l2_rw"] = kn(a["L0_ffn_router_w"].T)
    wv = np.stack([a["L0_ffn_w1"], a["L0_ffn_v1"]], 1).reshape(NS, 4, 2, F2, 2, P)
    o["moe_w1v1"] = wv.transpose(0, 5, 1, 2, 4, 3).reshape(NS, P, 1536)
    o["moe_w2"] = a["L0_ffn_w2"].reshape(NS, 4, F2, D).transpose(0, 2, 1, 3).reshape(NS, F2, 1024)
    o["l11_wg"], o["l11_sw1"], o["l11_sw3"] = kn(a["L3_ffn_Wg"]), kn(a["L3_ffn_sw1"]), kn(a["L3_ffn_sw3"])
    o["l11_sw2a"], o["l11_sw2b"] = kn(a["L3_ffn_sw2"][0:256]), a["L3_ffn_sw2"][256:]
    for n in ("w1", "w3"):
        o["moe8_" + n] = a["L3_ffn_" + n.upper()].reshape(E11, 2, P, F11).transpose(0, 2, 1, 3).reshape(E11, P, 704)
    o["moe8_w2a"] = a["L3_ffn_W2"][:, 0:256].reshape(E11, 2, P, D).transpose(0, 2, 1, 3).reshape(E11, P, 512)
    o["moe8_w2b"] = a["L3_ffn_W2"][:, 256:]
    t = a["ctx_512"].reshape(TOK, 8, 1, 8)
    o["ctxT32"] = np.broadcast_to(t, (TOK, 8, 4, 8)).reshape(TOK, 2, P).transpose(2, 1, 0)
    o["l9_wo"], o["l9_bo"] = kn(a["L3_attn_wo"].T), a["L3_attn_bo"].reshape(1, D)
    return {n: np.ascontiguousarray(v) for n, v in o.items()}


def kernel(**inputs):
    import concourse.bacc as bacc
    from concourse.bass_utils import run_bass_kernel_spmd

    arrays = {**constants(), **layout({n: np.asarray(v) for n, v in inputs.items()})}
    keep = ["l%d_" % n for n in LAYERS]
    arrays = {n: v for n, v in arrays.items() if layer_of(n) is None or any(n.startswith(k) for k in keep)}
    nc = bacc.Bacc("TRN2", target_bir_lowering=False, num_devices=1)
    dram = {n: nc.dram_tensor("in_" + n, v.shape, F32, kind="ExternalInput").ap() for n, v in arrays.items()}
    out = nc.dram_tensor("out_x", (TOK, D), F32, kind="ExternalOutput").ap()
    scratch = {n: nc.dram_tensor(n, shape, F32, kind="Internal").ap() for n, shape in SCRATCH.items()}
    build(nc, dram, out, scratch)
    r = run_bass_kernel_spmd(nc, [{"in_" + n: v for n, v in arrays.items()}], core_ids=[0])
    return np.asarray(r.results[0]["out_x"]).reshape(B, S, D)
```
